# Optimizing a Trainium2 kernel written in Bass

```python
import numpy as np
import jax
import jax.numpy as jnp

def _softmax(x, axis=-1):
    return jax.nn.softmax(x, axis=axis)

def _gelu(x):
    return jax.nn.gelu(x, approximate=True)

def _silu(x):
    return jax.nn.silu(x)

def _sigmoid(x):
    return jax.nn.sigmoid(x)

def _layernorm(x, axis=-1, eps=1e-05):
    m = jnp.mean(x, axis=axis, keepdims=True)
    v = jnp.var(x, axis=axis, keepdims=True)
    return (x - m) / jnp.sqrt(v + eps)

def _scatter_add(tgt, idx, src, axis=0):
    return tgt.at[idx].add(src)

def _segment_sum(src, seg, n):
    return jax.ops.segment_sum(src, seg, n)
kernel_name = 'mk_adaln_attn_ffn_d1_seqx_r2_ab67f2'

def setup_inputs(seed: int=0):
    np.random.seed(seed)
    _w = jnp.asarray

    def _rec_inputs():
        import jax
        import jax.numpy as jnp
        _rk = jax.random.key(seed)
        x = 7.22e-05 + 1 * jax.random.normal(jax.random.fold_in(_rk, 1), (32, 128, 512), jnp.float32)
        _lenS = 128 - jax.random.randint(jax.random.fold_in(_rk, 7), (32,), 0, max(1, 128 // 4) + 1, jnp.int32)
        _lenS2 = 128 - jax.random.randint(jax.random.fold_in(_rk, 8), (32,), 0, max(1, 128 // 4) + 1, jnp.int32)
        condB_tauraws = -5.74692 + 0.777674 * jax.random.normal(jax.random.fold_in(_rk, 11), (32,), jnp.float32)
        cond_256 = -0.000235209 + 0.019331 * jax.random.normal(jax.random.fold_in(_rk, 12), (32, 128), jnp.float32)
        condB_bn2 = jnp.zeros((32,), jnp.float32)
        cond_1024 = -4.10585e-05 + 0.0199478 * jax.random.normal(jax.random.fold_in(_rk, 14), (32, 512), jnp.float32)
        itok_B_0_8 = jax.random.randint(jax.random.fold_in(_rk, 15), (32,), 0, 9, jnp.int32)
        return (x, condB_tauraws, cond_256, condB_bn2, cond_1024, itok_B_0_8)
    x, condB_tauraws, cond_256, condB_bn2, cond_1024, itok_B_0_8 = _rec_inputs()

    def _L0_cond_setup():
        import jax, jax.numpy as jnp
        import numpy as np
        import math
        B, T, E, D = (4, 1024, 512, 4)

        def _tau_init(t):
            a = 0.1 ** (1.0 / max(t - 1, 1))
            tt = -math.log(max(a, 1e-10))
            return math.log(math.exp(tt) - 1 + 1e-10)

        def causal_ema(b, tau_raw):
            alpha = jnp.exp(-jax.nn.softplus(tau_raw)).astype(b.dtype)

            def step(h, bt):
                h = alpha * h + bt
                return (h, h)
            h0 = jnp.zeros((b.shape[0], b.shape[2]), b.dtype)
            _, hs = jax.lax.scan(step, h0, jnp.swapaxes(b, 0, 1))
            return jnp.swapaxes(hs, 0, 1)
        key = jax.random.key(seed)
        ks = jax.random.split(key, 10)
        s = 0.02
        return {'x': jax.random.normal(ks[0], (B, T, E), jnp.float32), 'tau_ctx': jnp.float32(_tau_init(max(T // 2, 4))), 'tau_raws': jnp.array([_tau_init(max(T // 2 ** i, 2)) for i in range(D)], jnp.float32), 'Wg': jax.random.normal(ks[1], (E, 2 * E), jnp.float32) * s, 'bg': jnp.full((E,), -0.5, jnp.float32), 'Wn1': jax.random.normal(ks[2], (E // 4, E), jnp.float32) * s, 'bn1': jnp.zeros((E // 4,), jnp.float32), 'Wn2': jax.random.normal(ks[3], (D, E // 4), jnp.float32) * s, 'bn2': jnp.zeros((D,), jnp.float32), 'blend': jax.random.normal(ks[4], (D, E), jnp.float32) * s, 'Wsoma': jax.random.normal(ks[5], (E, E), jnp.float32) * s, 'bsoma': jnp.zeros((E,), jnp.float32), 'Wtemp': jax.random.normal(ks[6], (E, E), jnp.float32) * s, 'btemp': jnp.zeros((E,), jnp.float32), 'Wout': jax.random.normal(ks[7], (E, E), jnp.float32) * s, 'gamma': jnp.ones((E,), jnp.float32), 'beta': jnp.zeros((E,), jnp.float32)}
    _L0_cond_all = _L0_cond_setup()
    _L0_cond_in = {k: v for k, v in _L0_cond_all.items() if k in ('tau_ctx', 'Wg', 'bg', 'Wn1', 'bn1', 'Wsoma', 'bsoma', 'Wtemp', 'btemp', 'Wout', 'gamma', 'beta')}
    del _L0_cond_all

    def _L0_attn_setup():
        import jax, jax.numpy as jnp
        import numpy as np
        import math
        B, N, DIM = (4, 2048, 512)
        HEADS, DHEAD, NRF = (16, 64, 64)
        STAB = 1e-06

        def _phi(t, RF):
            return jax.nn.relu(jnp.einsum('bhnd,hdr->bhnr', t, RF))
        key = jax.random.key(seed)
        k1, k2, k3, k4 = jax.random.split(key, 4)
        x = jax.random.normal(k1, (B, N, DIM), dtype=jnp.float32)
        W_qkv = jax.random.normal(k2, (DIM, 3 * HEADS * DHEAD), dtype=jnp.float32) * (1.0 / math.sqrt(DIM))
        RF = jax.random.normal(k3, (HEADS, DHEAD, NRF), dtype=jnp.float32) / math.sqrt(NRF)
        W_out = jax.random.normal(k4, (HEADS * DHEAD, DIM), dtype=jnp.float32) * (1.0 / math.sqrt(HEADS * DHEAD))
        b_out = jnp.zeros((DIM,), dtype=jnp.float32)
        return {'x': x, 'W_qkv': W_qkv, 'RF': RF, 'W_out': W_out, 'b_out': b_out}
    _L0_attn_all = _L0_attn_setup()
    _L0_attn_in = {k: v for k, v in _L0_attn_all.items() if k in ('W_qkv', 'RF', 'W_out', 'b_out')}
    del _L0_attn_all

    def _L0_cond2_setup():
        import jax, jax.numpy as jnp
        import numpy as np
        LN_EPS = 1e-05
        key = jax.random.key(seed)
        ks = jax.random.split(key, 8)
        B, S, H, A, L = (32, 1024, 512, 128, 10)
        return {'hidden_states': jax.random.normal(ks[0], (B, S, H), dtype=jnp.float32), 'language_ids': jax.random.randint(ks[1], (B,), 0, L, dtype=jnp.int64), 'W1': jax.random.normal(ks[2], (L, H, A), dtype=jnp.float32) * (1.0 / np.sqrt(H)), 'b1': jnp.zeros((L, A), dtype=jnp.float32), 'W2': jax.random.normal(ks[3], (L, A, H), dtype=jnp.float32) * (1.0 / np.sqrt(A)), 'b2': jnp.zeros((L, H), dtype=jnp.float32), 'gamma': jnp.ones((L, H), dtype=jnp.float32), 'beta': jnp.zeros((L, H), dtype=jnp.float32)}
    _L0_cond2_all = _L0_cond2_setup()
    _L0_cond2_in = {k: v for k, v in _L0_cond2_all.items() if k in ('W1', 'b1', 'W2', 'b2', 'gamma', 'beta')}
    del _L0_cond2_all

    def _L0_ffn_setup():
        import jax, jax.numpy as jnp
        import numpy as np
        NUM_EXPERTS = 8
        TOP_K = 2
        CAPACITY_FACTOR = 1.0

        def _dispatch_compute(xf, top_expert, w1, w2, capacity):
            tokens, hs = xf.shape
            tpe = jnp.bincount(top_expert, length=NUM_EXPERTS)
            indices = jnp.argsort(top_expert)
            offsets = jnp.concatenate([jnp.zeros((1,), tpe.dtype), jnp.cumsum(tpe)[:-1]])
            slot = jnp.arange(capacity)
            pos = offsets[:, None] + slot[None, :]
            valid = slot[None, :] < tpe[:, None]
            tok_idx = indices[jnp.minimum(pos, tokens - 1)]
            xe = jnp.where(valid[..., None], xf[tok_idx], 0.0)
            h = jax.nn.gelu(jnp.einsum('ech,ehf->ecf', xe, w1), approximate=True)
            ye = jnp.einsum('ecf,efh->ech', h, w2)
            tok_safe = jnp.where(valid, tok_idx, tokens)
            out = jnp.zeros((tokens + 1, hs), xf.dtype).at[tok_safe.reshape(-1)].add(ye.reshape(-1, hs))
            return out[:tokens]
        key = jax.random.key(seed)
        k1, k2, k3, k4 = jax.random.split(key, 4)
        hs, ffn = (512, 2048)
        x = jax.random.normal(k1, (1024, 2, hs), dtype=jnp.float32)
        router_w = jax.random.normal(k2, (hs, NUM_EXPERTS), dtype=jnp.float32) * hs ** (-0.5)
        w1 = jax.random.normal(k3, (NUM_EXPERTS, hs, ffn), dtype=jnp.float32) * 0.02
        w2 = jax.random.normal(k4, (NUM_EXPERTS, ffn, hs), dtype=jnp.float32) * 0.02
        bias = jnp.zeros((1, 1, hs), dtype=jnp.float32)
        return {'x': x, 'router_w': router_w, 'w1': w1, 'w2': w2, 'bias': bias}
    _L0_ffn_all = _L0_ffn_setup()
    _L0_ffn_in = {k: v for k, v in _L0_ffn_all.items() if k in ('router_w', 'w1', 'w2', 'bias')}
    del _L0_ffn_all
    return {'x': x, 'condB_tauraws': condB_tauraws, 'cond_256': cond_256, 'condB_bn2': condB_bn2, 'cond_1024': cond_1024, 'itok_B_0_8': itok_B_0_8, 'L0_cond_tau_ctx': _L0_cond_in['tau_ctx'], 'L0_cond_Wg': _L0_cond_in['Wg'], 'L0_cond_bg': _L0_cond_in['bg'], 'L0_cond_Wn1': _L0_cond_in['Wn1'], 'L0_cond_bn1': _L0_cond_in['bn1'], 'L0_cond_Wsoma': _L0_cond_in['Wsoma'], 'L0_cond_bsoma': _L0_cond_in['bsoma'], 'L0_cond_Wtemp': _L0_cond_in['Wtemp'], 'L0_cond_btemp': _L0_cond_in['btemp'], 'L0_cond_Wout': _L0_cond_in['Wout'], 'L0_cond_gamma': _L0_cond_in['gamma'], 'L0_cond_beta': _L0_cond_in['beta'], 'L0_attn_W_qkv': _L0_attn_in['W_qkv'], 'L0_attn_RF': _L0_attn_in['RF'], 'L0_attn_W_out': _L0_attn_in['W_out'], 'L0_attn_b_out': _L0_attn_in['b_out'], 'L0_cond2_W1': _L0_cond2_in['W1'], 'L0_cond2_b1': _L0_cond2_in['b1'], 'L0_cond2_W2': _L0_cond2_in['W2'], 'L0_cond2_b2': _L0_cond2_in['b2'], 'L0_cond2_gamma': _L0_cond2_in['gamma'], 'L0_cond2_beta': _L0_cond2_in['beta'], 'L0_ffn_router_w': _L0_ffn_in['router_w'], 'L0_ffn_w1': _L0_ffn_in['w1'], 'L0_ffn_w2': _L0_ffn_in['w2'], 'L0_ffn_bias': _L0_ffn_in['bias']}

def reference(x, condB_tauraws, cond_256, condB_bn2, cond_1024, itok_B_0_8, L0_cond_tau_ctx, L0_cond_Wg, L0_cond_bg, L0_cond_Wn1, L0_cond_bn1, L0_cond_Wsoma, L0_cond_bsoma, L0_cond_Wtemp, L0_cond_btemp, L0_cond_Wout, L0_cond_gamma, L0_cond_beta, L0_attn_W_qkv, L0_attn_RF, L0_attn_W_out, L0_attn_b_out, L0_cond2_W1, L0_cond2_b1, L0_cond2_W2, L0_cond2_b2, L0_cond2_gamma, L0_cond2_beta, L0_ffn_router_w, L0_ffn_w1, L0_ffn_w2, L0_ffn_bias):
    import jax
    import jax.numpy as jnp

    def _L0_cond_ref(x, tau_ctx, tau_raws, Wg, bg, Wn1, bn1, Wn2, bn2, blend, Wsoma, bsoma, Wtemp, btemp, Wout, gamma, beta):
        import jax, jax.numpy as jnp
        import numpy as np
        import math
        B, T, E, D = (4, 1024, 512, 4)

        def _tau_init(t):
            a = 0.1 ** (1.0 / max(t - 1, 1))
            tt = -math.log(max(a, 1e-10))
            return math.log(math.exp(tt) - 1 + 1e-10)

        def causal_ema(b, tau_raw):
            alpha = jnp.exp(-jax.nn.softplus(tau_raw)).astype(b.dtype)

            def step(h, bt):
                h = alpha * h + bt
                return (h, h)
            h0 = jnp.zeros((b.shape[0], b.shape[2]), b.dtype)
            _, hs = jax.lax.scan(step, h0, jnp.swapaxes(b, 0, 1))
            return jnp.swapaxes(hs, 0, 1)
        ctx = causal_ema(x, tau_ctx)
        gate_in = jnp.concatenate([x, ctx], axis=-1)
        wg = jax.nn.sigmoid(jnp.einsum('btc,ec->bte', gate_in, Wg) + bg)
        gated = x * wg
        h1 = jax.nn.gelu(jnp.einsum('btc,hc->bth', x, Wn1) + bn1, approximate=False)
        mod = 0.5 + jax.nn.sigmoid(jnp.einsum('bth,dh->btd', h1, Wn2) + bn2)
        traces = jax.vmap(lambda tau, m: causal_ema(gated * m[..., None], tau))(tau_raws, jnp.moveaxis(mod, -1, 0))
        blend_w = jax.nn.softmax(blend, axis=0)
        temporal = jnp.einsum('dbtc,dc->btc', traces, blend_w)
        gate = jax.nn.sigmoid(jnp.einsum('btc,ec->bte', temporal, Wtemp) + btemp)
        soma = jax.nn.gelu(jnp.einsum('btc,ec->bte', x, Wsoma) + bsoma, approximate=False)
        out = jnp.einsum('btc,ec->bte', soma * gate, Wout)
        mu = out.mean(-1, keepdims=True)
        var = out.var(-1, keepdims=True)
        return (out - mu) / jnp.sqrt(var + 1e-05) * gamma + beta

    def _L0_attn_ref(x, W_qkv, RF, W_out, b_out):
        import jax, jax.numpy as jnp
        import numpy as np
        import math
        B, N, DIM = (4, 2048, 512)
        HEADS, DHEAD, NRF = (16, 64, 64)
        STAB = 1e-06

        def _phi(t, RF):
            return jax.nn.relu(jnp.einsum('bhnd,hdr->bhnr', t, RF))
        b, n, _ = x.shape
        qkv = x @ W_qkv
        q, k, v = jnp.split(qkv, 3, axis=-1)

        def to_heads(t):
            return t.reshape(b, n, HEADS, DHEAD).transpose(0, 2, 1, 3)
        q, k, v = (to_heads(q), to_heads(k), to_heads(v))
        phi_q = _phi(q, RF)
        phi_k = _phi(k, RF)
        kv = jnp.einsum('bhnr,bhnd->bhrd', phi_k, v)
        out = jnp.einsum('bhnr,bhrd->bhnd', phi_q, kv)
        k_sum = phi_k.sum(axis=2)
        normalizer = jnp.einsum('bhnr,bhr->bhn', phi_q, k_sum)[..., None] + STAB
        out = out / normalizer
        out = out.transpose(0, 2, 1, 3).reshape(b, n, HEADS * DHEAD)
        out = out @ W_out + b_out
        return out

    def _L0_cond2_ref(hidden_states, language_ids, W1, b1, W2, b2, gamma, beta):
        import jax, jax.numpy as jnp
        import numpy as np
        LN_EPS = 1e-05
        w1 = W1[language_ids]
        w2 = W2[language_ids]
        h = jnp.einsum('bsh,bha->bsa', hidden_states, w1) + b1[language_ids][:, None, :]
        h = jax.nn.relu(h)
        adapted = jnp.einsum('bsa,bah->bsh', h, w2) + b2[language_ids][:, None, :]
        x = hidden_states + adapted
        mean = jnp.mean(x, axis=-1, keepdims=True)
        var = jnp.mean(jnp.square(x - mean), axis=-1, keepdims=True)
        normed = (x - mean) * jax.lax.rsqrt(var + LN_EPS)
        return normed * gamma[language_ids][:, None, :] + beta[language_ids][:, None, :]

    def _L0_ffn_ref(x, router_w, w1, w2, bias):
        import jax, jax.numpy as jnp
        import numpy as np
        NUM_EXPERTS = 8
        TOP_K = 2
        CAPACITY_FACTOR = 1.0

        def _dispatch_compute(xf, top_expert, w1, w2, capacity):
            tokens, hs = xf.shape
            tpe = jnp.bincount(top_expert, length=NUM_EXPERTS)
            indices = jnp.argsort(top_expert)
            offsets = jnp.concatenate([jnp.zeros((1,), tpe.dtype), jnp.cumsum(tpe)[:-1]])
            slot = jnp.arange(capacity)
            pos = offsets[:, None] + slot[None, :]
            valid = slot[None, :] < tpe[:, None]
            tok_idx = indices[jnp.minimum(pos, tokens - 1)]
            xe = jnp.where(valid[..., None], xf[tok_idx], 0.0)
            h = jax.nn.gelu(jnp.einsum('ech,ehf->ecf', xe, w1), approximate=True)
            ye = jnp.einsum('ecf,efh->ech', h, w2)
            tok_safe = jnp.where(valid, tok_idx, tokens)
            out = jnp.zeros((tokens + 1, hs), xf.dtype).at[tok_safe.reshape(-1)].add(ye.reshape(-1, hs))
            return out[:tokens]
        sl, bs, hs = x.shape
        tokens = sl * bs
        capacity = int(CAPACITY_FACTOR * tokens / NUM_EXPERTS)
        xf = x.reshape(tokens, hs)
        scores = jax.nn.softmax(xf @ router_w, axis=-1)
        expert_weights, top_experts = jax.lax.top_k(scores, TOP_K)
        out = jnp.zeros_like(xf)
        for k in range(TOP_K):
            y = _dispatch_compute(xf, top_experts[:, k].astype(jnp.int32), w1, w2, capacity)
            out = out + y * expert_weights[:, k][:, None]
        return out.reshape(sl, bs, hs) + bias
    x = x + _L0_attn_ref(_L0_cond_ref(x, L0_cond_tau_ctx, condB_tauraws, L0_cond_Wg, L0_cond_bg, L0_cond_Wn1, L0_cond_bn1, cond_256, condB_bn2, cond_1024, L0_cond_Wsoma, L0_cond_bsoma, L0_cond_Wtemp, L0_cond_btemp, L0_cond_Wout, L0_cond_gamma, L0_cond_beta), L0_attn_W_qkv, L0_attn_RF, L0_attn_W_out, L0_attn_b_out)
    x = x + _L0_ffn_ref(_L0_cond2_ref(x, itok_B_0_8, L0_cond2_W1, L0_cond2_b1, L0_cond2_W2, L0_cond2_b2, L0_cond2_gamma, L0_cond2_beta), L0_ffn_router_w, L0_ffn_w1, L0_ffn_w2, L0_ffn_bias)
    return x

_drawn_inputs = setup_inputs


def setup_inputs(seed=0):
    import zlib

    import numpy as np

    out = dict(_drawn_inputs(seed))
    spreads = {'condB_bn2': (0.0, 2.0),
     'L0_cond_bg': (-0.5, 0.6),
     'L0_cond_bn1': (0.0, 2.0),
     'L0_cond_bsoma': (0.0, 0.1),
     'L0_cond_btemp': (0.0, 0.534),
     'L0_cond_gamma': (1.0, 0.2),
     'L0_cond_beta': (0.0, 0.1),
     'L0_attn_b_out': (0.0, 0.1),
     'L0_cond2_b1': (0.0, 0.451),
     'L0_cond2_b2': (0.0, 0.356),
     'L0_cond2_gamma': (1.0, 0.2),
     'L0_cond2_beta': (0.0, 0.274),
     'L0_ffn_bias': (0.0, 0.1)}
    factors = {'condB_tauraws': 8.0, 'cond_256': 40.777, 'cond_1024': 64.0, 'L0_cond_Wn1': 42.169}
    for name, (base, spread) in spreads.items():
        noise = np.random.default_rng([zlib.crc32(name.encode()), seed]).standard_normal(out[name].shape)
        drawn = base * np.exp(spread * noise) if base else spread * noise
        out[name] = jnp.asarray(drawn.astype(out[name].dtype))
    for name, factor in factors.items():
        out[name] = (out[name] * factor).astype(out[name].dtype)
    return out
```

```python
from contextlib import ExitStack

import numpy as np
import concourse.bass as bass
from concourse import mybir

F32 = mybir.dt.float32
F16 = mybir.dt.float16
I32 = mybir.dt.int32
U32 = mybir.dt.uint32
ALU = mybir.AluOpType
ACT = mybir.ActivationFunctionType
AX_X = mybir.AxisListType.X

P = 128
B = 32
E = 512
CH = E // P
G = 4
GT = G * P
TRIPS = B // G
D = 32
L = 8
NL = P // L

PASSES = ((0, 0), (0, 1), (1, 0))
WS = 64.0
QS = 16.0


class Signal:

    def __init__(self, sem, per=1, step=1):
        self.sem, self.per, self.step = sem, per, step

    def after(self, trip, n=0):
        return trip * (self.per * self.step) + n * self.step


class Semaphores:

    def __init__(self, nc):
        self.nc, self.taken = nc, []

    def new(self, name):
        self.taken.append(self.nc.alloc_semaphore(name))
        return self.taken[-1]

    def __enter__(self):
        return self

    def __exit__(self, *error):
        self.nc.clear_and_free_semaphores(self.taken)
        self.nc.all_engine_barrier()


def wait(eng, signal, trip, n=0):
    value = signal.after(trip, n)
    if isinstance(value, int) and value == 0:
        return
    eng.wait_ge(signal.sem, value)


def repeated(ap, axis, n):
    ap = ap.unsqueeze(axis)
    shape = list(ap.shape)
    shape[axis] = n
    return ap.broadcast_to(shape)


def three_passes(pe, out, pairs):
    n = len(pairs) * len(PASSES)
    i = 0
    for lhs, rhs in pairs:
        for a, b in PASSES:
            last = pe.matmul(out, lhs(a), rhs(b), start=(i == 0), stop=(i == n - 1))
            i += 1
    return last


def constant_tables():
    t = np.arange(P)
    s = t[:, None]
    n_ctx = t[None, :] - s
    n_blk = np.repeat(L * np.arange(NL) - 1, D)[None, :] - s
    p32 = (t // D)[:, None]
    n_out = np.arange(D)[None, :] - L * p32 + 1
    parts = {
        "ident": np.eye(P),
        "n_ctx": np.maximum(n_ctx, 0), "m_ctx": n_ctx >= 0,
        "n_blk": np.maximum(n_blk, 0), "m_blk": n_blk >= 0,
        "n_out": np.clip(n_out, 0, L), "m_out": (n_out >= 1) & (n_out <= L),
        "lag_mask": (s % L >= np.arange(L)[None, :]) / 16.0,
        "n_lag": np.tile(np.arange(L), (P, 1)),
        "expert": np.tile(np.arange(8), (P, 2)),
        "choice": np.tile([0, 8], (P, 1)),
        "token": s,
        "dump": B * P + s,
        "before": s < t[None, :],
    }
    at, cols = {}, 0
    for k, v in parts.items():
        at[k] = (cols, cols + v.shape[1])
        cols += v.shape[1]
    table = np.concatenate([np.asarray(v, np.float32) for v in parts.values()], 1)
    return table, at


def cond_phase(nc, table, x, x_t, tau_ctx, tau, Wg, bg, Wn1, bn1, Wn2, bn2, blend_t, Wsoma, bsoma,
               Wtemp, btemp, Wout, gamma, beta, cond_t):
    _, AT = constant_tables()
    with ExitStack() as ctx, Semaphores(nc) as semaphores:
        def sb(name, shape, dt=F32):
            return ctx.enter_context(nc.sbuf_tensor("c_" + name, shape, dt))

        def sem(name, per=1, step=1):
            return Signal(semaphores.new("c_" + name), per, step)

        bank = [ctx.enter_context(nc.psum_tensor(f"c_bank{i}", [P, 512], F32)) for i in range(8)]

        wg = sb("wg", [P, 2 * CH, 2, E], F16)
        wsoma = sb("wsoma", [P, CH, 2, E], F16)
        wtemp = sb("wtemp", [P, CH, 2, E], F16)
        wout = sb("wout", [P, CH, 2, E], F16)
        wn1 = sb("wn1", [P, CH, 2, P], F16)
        wn2 = sb("wn2", [P, 3, D])
        cst = sb("cst", [P, AT["n_lag"][1]])
        const = lambda k: cst[:, AT[k][0]:AT[k][1]]
        ident = const("ident")
        neg_sp = sb("neg_sp", [P, D + 2])
        sp_tmp = sb("sp_tmp", [P, D + 2])
        decay_ctx = sb("decay_ctx", [P, P])
        decay_blk = sb("decay_blk", [P, NL * D])
        decay_out = sb("decay_out", [P, D])
        decay_lag = sb("decay_lag", [P, L])
        blend_rows = sb("blend_rows", [P, E])
        lag_w = sb("lag_w", [3 * D, L, E], F16)
        bias_cols = sb("bias_cols", [P, 2 * CH + 2])
        bn2_rows = sb("bn2_rows", [P, D])
        bg_halves = sb("bg_halves", [1, 2, E], F16)
        ones_row = sb("ones_row", [1, P], F16)
        gamma_rows = sb("gamma_rows", [P, E])
        beta_rows = sb("beta_rows", [P, E])

        xt_in = sb("xt_in", [P, CH, GT])
        x_in = sb("x_in", [P, G, E])
        x_h = sb("x_h", [P, CH, 2, GT], F16)
        ct_h = sb("ct_h", [P, CH, 2, GT], F16)
        h1 = sb("h1", [P, GT])
        modt = sb("modt", [3 * D, GT])
        mod_st = sb("mod_st", [3 * D, G, L + P], F16)
        mod = sb("mod", [P, G * D])
        gate_sig = sb("gate_sig", [P, 2, E])
        gated = sb("gated", [P, G, E])
        shifted = sb("shifted", [P, 2, L - 1, E])
        blk_mod = sb("blk_mod", [P, 2, NL * D])
        state_w = sb("state_w", [P, 4, E])
        lagged = sb("lagged", [P, L, E])
        temporal = sb("temporal", [P, G, E])
        soma = sb("soma", [P, CH, GT])
        gate2 = sb("gate2", [P, 2, GT])
        prod_f = sb("prod_f", [P, 2, GT])
        prod_h = sb("prod_h", [P, CH, 2, GT], F16)
        stats = sb("stats", [P, G, 6])
        mv = sb("mv", [P, G, 2])
        var_e = sb("var_e", [P, G])
        half_pow = sb("half_pow", [P, 1])
        rstd = sb("rstd", [P, G])
        z = temporal
        z_h = prod_h[:].rearrange("p a h t -> p (a h t)").rearrange("p (b c h t) -> p b c h t", b=G, c=CH, h=2)
        bg_row = blk_mod[0:1, 1, :]

        cst_in = sem("cst_in")
        vec_in = sem("vec_in")
        w_in = [sem(f"w_in{i}") for i in range(6)]
        w_hi, w_lo = sem("w_hi"), sem("w_lo")
        sp_step = sem("sp_step")
        sp_exp = sem("sp_exp")
        dve_step = sem("dve_step")
        act_step = sem("act_step")
        pe_step = sem("pe_step")
        lag_rows, lag_hi = sem("lag_rows"), sem("lag_hi")
        z0 = sem("z0")
        pieces = [(Wn1, wn1, 0, P), (Wg, wg, 0, E), (Wg, wg, CH, E), (Wsoma, wsoma, 0, E),
                  (Wtemp, wtemp, 0, E), (Wout, wout, 0, E)]
        flat = prod_h[:].bitcast(F32).rearrange("p a h t -> p (a h t)").rearrange("p (c n) -> p c n", c=CH)
        stage = [gate2[:, 0, :].rearrange("p (c n) -> p c n", c=CH), flat, gated[:], temporal[:], soma[:], state_w[:]]
        const_loads = (
            (cst[:], table[:, 0:AT["n_lag"][1]]),
            (neg_sp[:, 0:D], tau.partition_broadcast(P)),
            (neg_sp[:, D:D + 1], tau_ctx.partition_broadcast(P)),
            *((neg_sp[D * q:D * q + D, D + 1:D + 2], tau.rearrange("(d a) -> d a", a=1)) for q in range(4)),
            (gate_sig[:, 0, 0:CH * D], blend_t),
            (bias_cols[:, 2 * CH:2 * CH + 1], bn1.rearrange("(d a) -> d a", a=1)),
            (bg_row, bg.rearrange("(a d) -> a d", a=1)),
        )
        vector_loads = (
            (bias_cols[:, 0:CH], bsoma), (bias_cols[:, CH:2 * CH], btemp),
            *((bias_cols[D * q:D * q + D, 2 * CH + 1:2 * CH + 2], bn2.rearrange("(d a) -> d a", a=1)) for q in range(4)),
            (bn2_rows[:], bn2.partition_broadcast(P)),
            (gamma_rows[:], gamma.partition_broadcast(P)),
            (beta_rows[:], beta.partition_broadcast(P)),
            *((wn2[:, q, :], Wn2) for q in range(3)),
        )

        def load_piece(sp, i):
            src, _, c0, n = pieces[i]
            sp.dma_start(stage[i][:, :, 0:n], src[:, c0:c0 + CH, :]).then_inc(w_in[i].sem, 16)

        def piece_hi(act, i):
            _, dst, c0, n = pieces[i]
            act.wait_ge(w_in[i].sem, 16)
            act.activation(dst[:, c0:c0 + CH, 0, :], stage[i][:, :, 0:n], ACT.Copy, scale=WS).then_inc(w_hi.sem, 1)

        def piece_lo(dve, i):
            _, dst, c0, n = pieces[i]
            dve.wait_ge(w_hi.sem, i + 1)
            for c in range(CH):
                last = dve.scalar_tensor_tensor(dst[:, c0 + c, 1, :], stage[i][:, c, 0:n], WS, dst[:, c0 + c, 0, :],
                                                ALU.mult, ALU.subtract)
            last.then_inc(w_lo.sem, 1)

        def constants_pool(pool):
            for dst, src in vector_loads:
                pool.dma_start(dst, src).then_inc(vec_in.sem, 16)
            pool.memset(mod_st[:], 0.0).then_inc(z0.sem, 1)
            pool.memset(shifted[:], 0.0).then_inc(z0.sem, 1)
            pool.memset(half_pow[:], -0.5).then_inc(z0.sem, 1)
            pool.memset(ones_row[:], 1.0).then_inc(z0.sem, 1)
            pool.wait_ge(z0.sem, 4)

        def constants_scalar(act):
            act.wait_ge(cst_in.sem, 16 * len(const_loads))
            act.activation(sp_tmp[:], neg_sp[:], ACT.Abs).then_inc(sp_step.sem, 1)
            act.wait_ge(sp_step.sem, 1)
            act.activation(sp_tmp[:], sp_tmp[:], ACT.Exp, scale=-1.0).then_inc(act_step.sem, 1)
            act.wait_ge(act_step.sem, 1)
            act.activation(sp_tmp[:], sp_tmp[:], ACT.Ln, bias=1.0).then_inc(act_step.sem, 1)
            act.wait_ge(sp_step.sem, 4)
            act.activation(decay_ctx[:], const("n_ctx"), ACT.Exp, scale=neg_sp[:, D:D + 1]).then_inc(sp_exp.sem, 1)
            act.activation(decay_out[:], const("n_out"), ACT.Exp, scale=neg_sp[:, D + 1:D + 2]).then_inc(sp_exp.sem, 1)
            act.activation(decay_lag[:], const("n_lag"), ACT.Exp, scale=neg_sp[:, D + 1:D + 2]).then_inc(sp_exp.sem, 1)
            act.activation(decay_blk[:], decay_blk[:], ACT.Exp).then_inc(sp_exp.sem, 1)
            act.wait_ge(dve_step.sem, 2)
            act.activation(gate_sig[:, 0, 0:CH * D], gate_sig[:, 0, 0:CH * D], ACT.Exp).then_inc(act_step.sem, 1)

        def constants_vector(dve):
            dve.wait_ge(cst_in.sem, 16 * len(const_loads))
            dve.wait_ge(sp_step.sem, 1)
            dve.tensor_scalar(neg_sp[:], neg_sp[:], 0.0, -1.0, ALU.max, ALU.mult).then_inc(sp_step.sem, 1)
            dve.wait_ge(act_step.sem, 2)
            dve.wait_ge(sp_step.sem, 2)
            dve.tensor_tensor(neg_sp[:], neg_sp[:], sp_tmp[:], ALU.subtract).then_inc(sp_step.sem, 1)
            dve.wait_ge(sp_step.sem, 3)
            dve.tensor_tensor(decay_blk[:].rearrange("p (k d) -> p k d", d=D),
                              const("n_blk").rearrange("p (k d) -> p k d", d=D),
                              repeated(neg_sp[:, 0:D], 1, NL),
                              ALU.mult).then_inc(sp_step.sem, 1)
            bl = gate_sig[:, 0, 0:CH * D].rearrange("p (c d) -> p c d", d=D)
            red = stats[:, 0, 0:CH]
            red_b = repeated(red, 2, D)
            dve.tensor_reduce(red, bl, AX_X, ALU.max).then_inc(dve_step.sem, 1)
            dve.wait_ge(dve_step.sem, 1)
            dve.tensor_tensor(bl, bl, red_b, ALU.subtract).then_inc(dve_step.sem, 1)
            dve.wait_ge(act_step.sem, 3)
            dve.tensor_reduce(red, bl, AX_X, ALU.add).then_inc(dve_step.sem, 1)
            dve.wait_ge(dve_step.sem, 3)
            dve.reciprocal(red, red).then_inc(dve_step.sem, 1)
            dve.wait_ge(dve_step.sem, 4)
            bl4 = blk_mod[:, 0, :].rearrange("p (c r d) -> p c r d", c=CH, r=4)
            for r in range(4):
                dve.tensor_tensor(bl4[:, :, r, :], bl, red_b, ALU.mult).then_inc(dve_step.sem, 1)
            dve.wait_ge(sp_exp.sem, 4)
            dve.tensor_tensor(decay_ctx[:], decay_ctx[:], const("m_ctx"), ALU.mult).then_inc(dve_step.sem, 1)
            dve.tensor_tensor(decay_blk[:], decay_blk[:], const("m_blk"), ALU.mult).then_inc(dve_step.sem, 1)
            dve.tensor_tensor(decay_out[:], decay_out[:], const("m_out"), ALU.mult).then_inc(dve_step.sem, 1)
            dve.tensor_scalar(decay_lag[:], decay_lag[:], 16.0, None, ALU.mult).then_inc(dve_step.sem, 1)
            dve.wait_ge(pe_step.sem, 1)
            dve.tensor_copy(blend_rows[:], bank[0][:]).then_inc(dve_step.sem, 1)

        def bias_vector(dve):
            dve.tensor_scalar(bg_row, bg_row, WS, None, ALU.mult).then_inc(dve_step.sem, 1)
            dve.wait_ge(dve_step.sem, 14)
            dve.tensor_copy(bg_halves[:, 0, :], bg_row).then_inc(dve_step.sem, 1)
            dve.wait_ge(dve_step.sem, 15)
            dve.tensor_tensor(bg_halves[:, 1, :], bg_row, bg_halves[:, 0, :], ALU.subtract).then_inc(dve_step.sem, 1)

        lw = lagged[0:3 * D]

        def later_scalar(act):
            act.wait_ge(vec_in.sem, 16 * len(vector_loads))
            act.wait_ge(dve_step.sem, 13)
            for j in range(L):
                act.activation(lw[:, j, :], blend_rows[0:3 * D, :], ACT.Copy,
                               scale=decay_lag[0:3 * D, j:j + 1]).then_inc(lag_rows.sem, 1)
            act.wait_ge(lag_rows.sem, L)
            act.activation(lag_w[:], lw, ACT.Copy).then_inc(lag_hi.sem, 1)
            for i in range(3, 6):
                piece_hi(act, i)

        def later_vector(dve):
            dve.wait_ge(lag_hi.sem, 1)
            dve.tensor_tensor(lag_w[D:2 * D], lw[D:2 * D], lag_w[D:2 * D], ALU.subtract).then_inc(dve_step.sem, 1)
            for i in range(3, 6):
                piece_lo(dve, i)

        def constants_tensor(pe):
            pe.wait_ge(dve_step.sem, 8)
            for c in range(CH):
                last = pe.transpose(bank[0][:, c * P:c * P + P], blk_mod[:, 0, c * P:c * P + P], ident)
            last.then_inc(pe_step.sem, 1)

        xt_load, x_load = sem("xt_load", 1, 16), sem("x_load", 1, 16)
        shift_in = [sem(f"shift_in{i}", 2 * (L - 1), 16) for i in range(2)]
        z_out = sem("z_out", 1, 16)
        ctx_mm, h1_mm, modt_mm, mod_mm = sem("ctx_mm", G), sem("h1_mm"), sem("modt_mm"), sem("mod_mm")
        gate_mm, state_mm, lag_mm, y_mm = sem("gate_mm", G), sem("state_mm", 4 * G), sem("lag_mm", L * G), sem("y_mm", G)
        soma_mm, temp_tr, gate2_mm = sem("soma_mm", CH), sem("temp_tr", G), sem("gate2_mm", CH)
        out_mm, z_tr = sem("out_mm"), sem("z_tr", G)
        x_hi, ctx_hi, h1_done, modt_sig, mod_sig = sem("x_hi"), sem("ctx_hi", G), sem("h1_done"), sem("modt_sig"), sem("mod_sig")
        gate_done, soma_done, temp_hi, gate2_done, z_hi = sem("gate_done", G), sem("soma_done", CH), sem("temp_hi", G), sem("gate2_done", CH), sem("z_hi", G)
        x_lo, ctx_lo, modt_half, modt_hi, modt_lo = sem("x_lo"), sem("ctx_lo", G), sem("modt_half"), sem("modt_hi"), sem("modt_lo")
        mod_pre, gated_done, blk_done = sem("mod_pre"), sem("gated_done", G), sem("blk_done", G)
        state_done, lag_done, temp_done, temp_lo = sem("state_done", 4 * G), sem("lag_done", L * G), sem("temp_done", G), sem("temp_lo", G)
        prod_done, prod_hi, prod_lo = sem("prod_done", CH), sem("prod_hi", CH), sem("prod_lo", CH)
        st_done, mv_done, var_done = sem("st_done", G), sem("mv_done", G), sem("var_done", G)
        centred, z_done, z_lo = sem("centred", G), sem("z_done", G), sem("z_lo", G)
        sum_done, rstd_done = sem("sum_done", (L - 1) * G), sem("rstd_done", G)

        CTX_BANK = (5, 2, 3, 4)
        GATE_BANK = (7, 0, 1, 2)
        Z_BANK = (3, 4, 5, 6)
        SOMA_BANK = (0, 0, 0, 5)
        OUT_BANK = (6, 7, 0, 1)

        def cols(b):
            return slice(b * P, b * P + P)

        FIRST, LAST = 0, TRIPS - 1

        def sync_trip(sp, g):
            if g is FIRST:
                for dst, src in const_loads:
                    sp.dma_start(dst, src).then_inc(cst_in.sem, 16)
                load_piece(sp, 0)
                sp.dma_start(xt_in[:], x_t[0]).then_inc(xt_load.sem, 16)
                sp.dma_start(x_in[:], x[0]).then_inc(x_load.sem, 16)
                for i in range(1, 6):
                    load_piece(sp, i)
            if g is not LAST:
                wait(sp, x_lo, g, 1)
                sp.dma_start(xt_in[:], x_t[g + 1]).then_inc(xt_load.sem, 16)
            for b in range(G):
                wait(sp, gated_done, g, b + 1)
                for j in range(1, L):
                    sp.dma_start(shifted[j:P, b % 2, j - 1, :], gated[0:P - j, b, :]).then_inc(shift_in[b % 2].sem, 16)
            if g is not LAST:
                sp.dma_start(x_in[:], x[g + 1]).then_inc(x_load.sem, 16)

        def store_z(sp, g):
            wait(sp, z_lo, g, G)
            sp.dma_start(cond_t[g], z_h).then_inc(z_out.sem, 16)

        def z_transposes(pe, g):
            for b in range(G):
                wait(pe, z_done, g, b + 1)
                for c in range(CH):
                    last = pe.transpose(bank[Z_BANK[b]][:, cols(c)], z[:, b, cols(c)], ident)
                last.then_inc(z_tr.sem, 1)

        def tensor_trip(pe, g, prev):
            def lag_pair(b, i):
                for j in (2 * i, 2 * i + 1):
                    n = L * b + j
                    if n < 2 and prev is not None:
                        wait(pe, z_lo, prev, n + 2)
                    if n >= 2:
                        wait(pe, lag_done, g, n - 1)
                    pe.matmul(bank[4 + j % 2][:], mod_st[:, b, L - j:L - j + P], lag_w[:, j, :],
                              start=True, stop=True).then_inc(lag_mm.sem, 1)

            def outputs(b, i):
                n = 4 * b + i
                wait(pe, state_done, g, n + 1)
                mm = pe.matmul(bank[6 + b % 2][D * i:D * i + D, :], decay_out[:], state_w[:, i, :],
                               start=True, stop=True)
                if i == 3:
                    mm.then_inc(y_mm.sem, 1)

            if g is FIRST:
                constants_tensor(pe)
                pe.wait_ge(w_lo.sem, 1)
            wait(pe, x_lo, g, 1)
            wait(pe, x_hi, g, 1)
            wait(pe, lag_done, g)
            three_passes(pe, bank[4][:], [(lambda h, c=c: wn1[:, c, h, :], lambda h, c=c: x_h[:, c, h, :])
                                          for c in range(CH)]).then_inc(h1_mm.sem, 1)
            wait(pe, x_load, g, 1)
            for b in range(G):
                if b == 0:
                    wait(pe, soma_done, g)
                elif b < 3:
                    if prev is not None:
                        wait(pe, gate2_done, prev, b + 2)
                else:
                    wait(pe, h1_done, g, 1)
                for c in range(CH):
                    last = pe.matmul(bank[CTX_BANK[b]][:, cols(c)], x_in[:, b, cols(c)], decay_ctx[:], start=True, stop=True)
                last.then_inc(ctx_mm.sem, 1)

            def gate(b):
                k = GATE_BANK[b]
                if b == 0:
                    wait(pe, centred, g)
                elif b == 3:
                    wait(pe, ctx_lo, g, 2)
                if g is FIRST and b == 0:
                    pe.wait_ge(w_lo.sem, 3)
                    pe.wait_ge(dve_step.sem, 16)
                    pe.wait_ge(z0.sem, 4)
                for h in range(2):
                    pe.matmul(bank[k][:], ones_row[:], bg_halves[:, h, :], start=(h == 0), stop=False)
                n = 0
                for c in range(2 * CH):
                    act_in = x_h if c < CH else ct_h
                    if c == CH:
                        wait(pe, ctx_lo, g, b + 1)
                    for a, w in PASSES:
                        n += 1
                        last = pe.matmul(bank[k][:], act_in[:, c % CH, a, cols(b)], wg[:, c, w, :],
                                         start=False, stop=(n == 2 * CH * 3))
                last.then_inc(gate_mm.sem, 1)

            gate(0)
            wait(pe, h1_done, g, 1)
            if g is FIRST:
                pe.wait_ge(vec_in.sem, 16 * len(vector_loads))
            wait(pe, ctx_lo, g, 1)
            pe.matmul(bank[5][0:3 * D, :], wn2[:].rearrange("p a d -> p (a d)"), h1[:],
                      start=True, stop=True).then_inc(modt_mm.sem, 1)
            for b in range(G):
                last = pe.matmul(bank[6][:, D * b:D * b + D], h1[:, cols(b)], wn2[:, 0, :], start=True, stop=True)
            last.then_inc(mod_mm.sem, 1)
            gate(1)
            gate(2)
            if prev is not None:
                wait(pe, ctx_lo, g, 4)
                wait(pe, modt_sig, g, 1)
                wait(pe, mod_pre, g, 1)
                z_transposes(pe, prev)
            gate(3)

            def soma_chunk(e):
                if e == 0:
                    wait(pe, gate_done, g, 2)
                elif e < 3:
                    wait(pe, soma_done, g, e)
                else:
                    wait(pe, lag_done, g, L * G)
                three_passes(pe, bank[SOMA_BANK[e]][:], [(lambda h, c=c: wsoma[:, c, h, cols(e)],
                                                          lambda h, c=c: x_h[:, c, h, :])
                                                         for c in range(CH)]).then_inc(soma_mm.sem, 1)

            wait(pe, modt_lo, g, 1)
            if g is FIRST:
                pe.wait_ge(w_lo.sem, len(pieces))
                pe.wait_ge(dve_step.sem, 17)
            for b in range(G):
                for i in range(4):
                    n = 4 * b + i
                    if i == 0:
                        wait(pe, blk_done, g, b + 1)
                        wait(pe, gated_done, g, b + 1)
                    if n == 0:
                        wait(pe, gate_done, g, G)
                        wait(pe, modt_sig, g, 1)
                    if n == 1:
                        wait(pe, z_lo, prev, 1) if prev is not None else wait(pe, ctx_lo, g, G)
                    if n >= 2:
                        wait(pe, state_done, g, n - 1)
                    pe.matmul(bank[2 + i % 2][:], blk_mod[:, b % 2, P * i:P * i + P], gated[:, b, :],
                              start=True, stop=True).then_inc(state_mm.sem, 1)
                    lag_pair(b, i)
                    if i == 1:
                        if b == 0:
                            wait(pe, z_lo, prev, G) if prev is not None else wait(pe, mod_pre, g, 1)
                        elif b == 1:
                            wait(pe, gate_done, g, 1)
                        else:
                            wait(pe, temp_done, g, b - 1)
                    if i >= 1:
                        outputs(b, i - 1)
                outputs(b, 3)
                if b == 0:
                    soma_chunk(0)
                else:
                    temporal_transpose(pe, g, b - 1)
            soma_chunk(1)
            soma_chunk(2)
            temporal_transpose(pe, g, G - 1)
            soma_chunk(3)

            def gate2_chunk(e):
                wait(pe, gate2_done, g, e - 1) if e >= 2 else wait(pe, state_done, g, 4 * G)
                three_passes(pe, bank[2 + e % 2][:], [(lambda h, c=c: wtemp[:, c, h, cols(e)], lambda h, c=c: ct_h[:, c, h, :])
                                                      for c in range(CH)]).then_inc(gate2_mm.sem, 1)

            def out_chunk(e):
                wait(pe, prod_lo, g, e + 1)
                for b in range(G):
                    k = OUT_BANK[b]
                    if e == 0:
                        if b < 2:
                            wait(pe, temp_done, g, G)
                        elif b == 2:
                            wait(pe, soma_done, g, CH)
                        else:
                            wait(pe, temp_lo, g, G)
                    for i, (a, w) in enumerate(PASSES):
                        last = pe.matmul(bank[k][:], prod_h[:, e, a, cols(b)], wout[:, e, w, :],
                                         start=(e == 0 and i == 0), stop=(e == CH - 1 and i == 2))
                if e == CH - 1:
                    last.then_inc(out_mm.sem, 1)

            wait(pe, temp_hi, g, G)
            wait(pe, temp_lo, g, G)
            gate2_chunk(0)
            gate2_chunk(1)
            out_chunk(0)
            gate2_chunk(2)
            out_chunk(1)
            gate2_chunk(3)
            out_chunk(2)
            out_chunk(3)

        def temporal_transpose(pe, g, b):
            wait(pe, temp_done, g, b + 1)
            if b == 0:
                wait(pe, gate_done, g, 3)
            else:
                wait(pe, temp_lo, g, b)
            for c in range(CH):
                last = pe.transpose(bank[1][:, cols(c)], temporal[:, b, cols(c)], ident)
            last.then_inc(temp_tr.sem, 1)

        def scalar_z(act, g):
            for b in range(G):
                wait(act, z_tr, g, b + 1)
                act.activation(z_h[:, b, :, 0, :], bank[Z_BANK[b]][:].rearrange("p (c t) -> p c t", c=CH),
                               ACT.Copy).then_inc(z_hi.sem, 1)

        def scalar_x(act, g):
            wait(act, xt_load, g, 1)
            wait(act, soma_mm, g)
            act.activation(x_h[:, :, 0, :], xt_in[:], ACT.Copy).then_inc(x_hi.sem, 1)

        def scalar_trip(act, g, prev):
            if g is FIRST:
                constants_scalar(act)
                piece_hi(act, 0)
                scalar_x(act, 0)
                piece_hi(act, 1)
                piece_hi(act, 2)
            wait(act, h1_mm, g, 1)
            wait(act, mod_mm, g)
            act.activation(h1[:], bank[4][:], ACT.Gelu, bias=bias_cols[:, 2 * CH:2 * CH + 1],
                           scale=1.0 / WS).then_inc(h1_done.sem, 1)
            wait(act, gate2_mm, g)
            for b in range(G):
                wait(act, ctx_mm, g, b + 1)
                act.activation(ct_h[:, :, 0, cols(b)], bank[CTX_BANK[b]][:].rearrange("p (c t) -> p c t", c=CH),
                               ACT.Copy).then_inc(ctx_hi.sem, 1)
            if g is FIRST:
                later_scalar(act)
            wait(act, gated_done, g)
            for b in range(G):
                wait(act, gate_mm, g, b + 1)
                if b >= 2:
                    wait(act, gated_done, g, b - 1)
                act.activation(gate_sig[:, b % 2, :], bank[GATE_BANK[b]][:], ACT.Sigmoid,
                               scale=1.0 / WS).then_inc(gate_done.sem, 1)
                if b == 2 and prev is not None:
                    scalar_z(act, prev)
                if b == 0:
                    wait(act, modt_mm, g, 1)
                    wait(act, modt_lo, g)
                    act.activation(modt[:], bank[5][0:3 * D, :], ACT.Sigmoid,
                                   bias=bias_cols[0:3 * D, 2 * CH + 1:2 * CH + 2]).then_inc(modt_sig.sem, 1)
                    wait(act, mod_pre, g, 1)
                    act.activation(mod[:], mod[:], ACT.Sigmoid).then_inc(mod_sig.sem, 1)
            def scalar_soma(e):
                wait(act, soma_mm, g, e + 1)
                if e == 0:
                    wait(act, prod_done, g)
                act.activation(soma[:, e, :], bank[SOMA_BANK[e]][:], ACT.Gelu, bias=bias_cols[:, e:e + 1],
                               scale=1.0 / WS).then_inc(soma_done.sem, 1)

            scalar_soma(0)
            for b in range(G - 1):
                scalar_temporal(act, g, b)
            scalar_soma(1)
            scalar_soma(2)
            scalar_temporal(act, g, G - 1)
            scalar_soma(3)
            if g is not LAST:
                scalar_x(act, g + 1)
            for e in range(CH):
                wait(act, gate2_mm, g, e + 1)
                if e >= 2:
                    wait(act, prod_done, g, e - 1)
                act.activation(gate2[:, e % 2, :], bank[2 + e % 2][:], ACT.Sigmoid,
                               bias=bias_cols[:, CH + e:CH + e + 1], scale=1.0 / WS).then_inc(gate2_done.sem, 1)

        def scalar_temporal(act, g, b):
            wait(act, temp_tr, g, b + 1)
            act.activation(ct_h[:, :, 0, cols(b)], bank[1][:].rearrange("p (c t) -> p c t", c=CH),
                           ACT.Copy).then_inc(temp_hi.sem, 1)

        def vector_z(dve, g):
            for b in range(G):
                wait(dve, z_hi, g, b + 1)
                dve.tensor_tensor(z_h[:, b, :, 1, :], bank[Z_BANK[b]][:].rearrange("p (c t) -> p c t", c=CH),
                                  z_h[:, b, :, 0, :], ALU.subtract).then_inc(z_lo.sem, 1)

        def vector_x(dve, g):
            wait(dve, x_hi, g, 1)
            dve.tensor_tensor(x_h[:, :, 1, :], xt_in[:], x_h[:, :, 0, :], ALU.subtract).then_inc(x_lo.sem, 1)

        def vector_norm(dve, g):
            wait(dve, rstd_done, g, 1)
            for b in range(G):
                wait(dve, centred, g, b + 1)
                dve.scalar_tensor_tensor(z[:, b, :], z[:, b, :], rstd[:, b:b + 1], beta_rows[:],
                                         ALU.mult, ALU.add).then_inc(z_done.sem, 1)

        def vector_trip(dve, g, prev):
            if g is FIRST:
                constants_vector(dve)
                piece_lo(dve, 0)
                vector_x(dve, 0)
                piece_lo(dve, 1)
                piece_lo(dve, 2)
                bias_vector(dve)
            for b in range(G):
                wait(dve, ctx_hi, g, b + 1)
                dve.tensor_tensor(ct_h[:, :, 1, cols(b)], bank[CTX_BANK[b]][:].rearrange("p (c t) -> p c t", c=CH),
                                  ct_h[:, :, 0, cols(b)], ALU.subtract).then_inc(ctx_lo.sem, 1)
            if prev is not None:
                vector_norm(dve, prev)
            else:
                dve.wait_ge(vec_in.sem, 16 * len(vector_loads))
                dve.wait_ge(z0.sem, 4)
                later_vector(dve)
            wait(dve, mod_mm, g, 1)
            wait(dve, blk_done, g)
            dve.tensor_tensor(mod[:].rearrange("p (b d) -> p b d", d=D),
                              bank[6][:, 0:G * D].rearrange("p (b d) -> p b d", d=D),
                              repeated(bn2_rows[:], 1, G), ALU.add).then_inc(mod_pre.sem, 1)
            wait(dve, modt_sig, g, 1)
            dve.tensor_scalar(modt[:], modt[:], 0.5, None, ALU.add).then_inc(modt_half.sem, 1)
            wait(dve, modt_half, g, 1)
            wait(dve, lag_mm, g)
            m4 = modt[:].rearrange("p (b t) -> p b t", b=G)
            dve.tensor_copy(mod_st[:, :, L:L + P], m4).then_inc(modt_hi.sem, 1)
            wait(dve, modt_hi, g, 1)
            dve.tensor_tensor(mod_st[2 * D:3 * D, :, L:L + P], m4[2 * D:3 * D], mod_st[2 * D:3 * D, :, L:L + P],
                              ALU.subtract).then_inc(modt_lo.sem, 1)
            wait(dve, x_load, g, 1)

            def gate_and_block(b):
                if b == 0:
                    wait(dve, state_mm, g)
                    wait(dve, shift_in[0], g)
                    wait(dve, shift_in[1], g)
                    wait(dve, lag_done, g)
                wait(dve, gate_done, g, b + 1)
                dve.tensor_tensor(gated[:, b, :], x_in[:, b, :], gate_sig[:, b % 2, :], ALU.mult).then_inc(gated_done.sem, 1)
                wait(dve, mod_sig, g, 1)
                if b >= 2:
                    wait(dve, state_mm, g, 4 * (b - 1))
                dve.scalar_tensor_tensor(blk_mod[:, b % 2, :].rearrange("p (k d) -> p k d", d=D),
                                         repeated(mod[:, D * b:D * b + D], 1, NL), 0.5,
                                         decay_blk[:].rearrange("p (k d) -> p k d", d=D),
                                         ALU.add, ALU.mult).then_inc(blk_done.sem, 1)

            gate_and_block(0)
            gate_and_block(1)
            if prev is not None:
                vector_z(dve, prev)
            def temporal_sum(b):
                wait(dve, sum_done, g, (L - 1) * (b + 1))
                wait(dve, y_mm, g, b + 1)
                dve.tensor_tensor(temporal[:, b, :], bank[6 + b % 2][:], temporal[:, b, :], ALU.add).then_inc(temp_done.sem, 1)

            for b in range(G):
                if b >= 1 and b + 1 < G:
                    gate_and_block(b + 1)
                if b >= 2:
                    vector_temporal(dve, g, b - 2)
                for i in range(4):
                    n = 4 * b + i
                    wait(dve, state_mm, g, n + 1)
                    if n >= 4:
                        wait(dve, y_mm, g, b)
                    elif n == 0:
                        wait(dve, y_mm, g)
                    dve.tensor_tensor(state_w[:, i, :], bank[2 + i % 2][:], blend_rows[:], ALU.mult).then_inc(state_done.sem, 1)
                    for j in (2 * i, 2 * i + 1):
                        n = L * b + j
                        wait(dve, lag_mm, g, n + 1)
                        if j == 0:
                            wait(dve, gated_done, g, b + 1)
                        if j == 1:
                            wait(dve, shift_in[b % 2], g, (L - 1) * (b // 2 + 1))
                        if b == 0:
                            if j == 0:
                                wait(dve, sum_done, g)
                        else:
                            wait(dve, sum_done, g, (L - 1) * (b - 1) + max(j, 1))
                        src = gated[:, b, :] if j == 0 else shifted[:, b % 2, j - 1, :]
                        dve.scalar_tensor_tensor(lagged[:, j, :], bank[4 + j % 2][:], const("lag_mask")[:, j:j + 1],
                                                 src, ALU.mult, ALU.mult).then_inc(lag_done.sem, 1)
                    if i == 1 and b >= 1:
                        temporal_sum(b - 1)
            vector_temporal(dve, g, G - 2)
            temporal_sum(G - 1)
            vector_temporal(dve, g, G - 1)
            if g is not LAST:
                vector_x(dve, g + 1)
            for e in range(CH):
                wait(dve, gate2_done, g, e + 1)
                wait(dve, soma_done, g, e + 1)
                dve.tensor_tensor(prod_f[:, e % 2, :], soma[:, e, :], gate2[:, e % 2, :], ALU.mult).then_inc(prod_done.sem, 1)
                wait(dve, prod_done, g, e + 1)
                if e == 0:
                    wait(dve, z_out, g)
                dve.tensor_copy(prod_h[:, e, 0, :], prod_f[:, e % 2, :]).then_inc(prod_hi.sem, 1)
                wait(dve, prod_hi, g, e + 1)
                dve.tensor_tensor(prod_h[:, e, 1, :], prod_f[:, e % 2, :], prod_h[:, e, 0, :],
                                  ALU.subtract).then_inc(prod_lo.sem, 1)
            wait(dve, out_mm, g, 1)
            for b in range(G):
                k = OUT_BANK[b]
                dve.bn_stats(stats[:, b, :], bank[k][:]).then_inc(st_done.sem, 1)
            wait(dve, st_done, g, G)
            dve.memset(var_e[:], 0.0)
            for b in range(G):
                dve.bn_aggr(mv[:, b, :], stats[:, b, :]).then_inc(mv_done.sem, 1)
            wait(dve, mv_done, g, G)
            dve.tensor_scalar(var_e[:], mv[:, :, 1], 1e-5 * WS * WS, None, ALU.add).then_inc(var_done.sem, 1)
            for b in range(G):
                k = OUT_BANK[b]
                dve.scalar_tensor_tensor(z[:, b, :], bank[k][:], mv[:, b, 0:1], gamma_rows[:],
                                         ALU.subtract, ALU.mult).then_inc(centred.sem, 1)

        def vector_temporal(dve, g, b):
            wait(dve, temp_hi, g, b + 1)
            dve.tensor_tensor(ct_h[:, :, 1, cols(b)], bank[1][:].rearrange("p (c t) -> p c t", c=CH),
                              ct_h[:, :, 0, cols(b)], ALU.subtract).then_inc(temp_lo.sem, 1)

        def pool_trip(pool, g):
            wait(pool, z_tr, g)
            for b in range(G):
                for j in range(1, L):
                    wait(pool, lag_done, g, L * b + j + 1)
                    if j > 1:
                        wait(pool, sum_done, g, (L - 1) * b + j - 1)
                    pool.tensor_tensor(temporal[:, b, :], lagged[:, 0, :] if j == 1 else temporal[:, b, :],
                                       lagged[:, j, :], ALU.add).then_inc(sum_done.sem, 1)
            wait(pool, var_done, g, 1)
            pool.tensor_tensor(rstd[:], var_e[:], half_pow[:].broadcast_to([P, G]), ALU.pow).then_inc(rstd_done.sem, 1)

        rstd_done.per = 1
        var_done.per = 1

        with nc.Block() as block:
            @block.sync
            def _(sp):
                sync_trip(sp, FIRST)
                with sp.Fori(1, LAST) as g:
                    sync_trip(sp, g)
                    store_z(sp, g - 1)
                sync_trip(sp, LAST)
                store_z(sp, LAST - 1)
                store_z(sp, TRIPS - 1)
                wait(sp, z_out, TRIPS)

            @block.tensor
            def _(pe):
                tensor_trip(pe, FIRST, None)
                with pe.Fori(1, LAST) as g:
                    tensor_trip(pe, g, g - 1)
                tensor_trip(pe, LAST, LAST - 1)
                z_transposes(pe, TRIPS - 1)

            @block.scalar
            def _(act):
                scalar_trip(act, FIRST, None)
                with act.Fori(1, LAST) as g:
                    scalar_trip(act, g, g - 1)
                scalar_trip(act, LAST, LAST - 1)
                scalar_z(act, TRIPS - 1)

            @block.vector
            def _(dve):
                vector_trip(dve, FIRST, None)
                with dve.Fori(1, LAST) as g:
                    vector_trip(dve, g, g - 1)
                vector_trip(dve, LAST, LAST - 1)
                vector_norm(dve, LAST)
                vector_z(dve, LAST)

            @block.gpsimd
            def _(pool):
                constants_pool(pool)
                pool_trip(pool, 0)
                with pool.Fori(1, TRIPS) as g:
                    pool_trip(pool, g)


def attention_phase(nc, table, cond_t, x, WqT, WkT, RF, Wv, Wo, b_out, ffn_bias, lang, A1, A2, rows3,
                    router, acc, tokens, slots):
    _, AT = constant_tables()
    HP = 8
    HD = P * HP
    with ExitStack() as ctx, Semaphores(nc) as semaphores:
        def sb(name, shape, dt=F32):
            return ctx.enter_context(nc.sbuf_tensor("a_" + name, shape, dt))

        def sem(name, per=1, step=1):
            return Signal(semaphores.new("a_" + name), per, step)

        bank = [ctx.enter_context(nc.psum_tensor(f"a_bank{i}", [P, 512], F32)) for i in range(8)]

        wq = sb("wq", [P, CH, 2, HD], F16)
        wk = sb("wk", [P, CH, 2, HD], F16)
        wv = sb("wv", [P, CH, 2, HD], F16)
        wo = sb("wo", [P, HP, 2, E], F16)
        wr = sb("wr", [P, CH, 8])
        cst = sb("cst", [P, P + 20])
        ident = cst[:, 0:P]
        expert, choice = cst[:, P:P + 16], cst[:, P + 16:P + 18]
        cur_token, dump = cst[:, P + 18:P + 19], cst[:, P + 19:P + 20]
        before = sb("before", [P, P], F16)
        ones = sb("ones", [P, P], F16)
        b_out_rows = sb("b_out_rows", [P, E])
        bias_rows = sb("bias_rows", [P, E])
        half_pow = sb("half_pow", [P, 1])
        lang_i = sb("lang_i", [P, B], I32)
        lang_rows = sb("lang_rows", [P, B], I32)
        ct = sb("ct", [P, G, CH, 2, P], F16)
        phq = sb("phq", [P, HP, 2, GT], F16)
        phk = sb("phk", [P, 2, 2, HD], F16)
        v_h = sb("v_h", [P, 2, 2, 16, 65], F16)
        kv = sb("kv", [P, 2, 2, 16, 66], F16)
        nrm = sb("nrm", [P, 2, 16])
        o = sb("o", [P, 2, HD])
        ot = sb("ot", [P, 2, HP, 2, P], F16)
        xr = sb("xr", [P, G, E])
        r = sb("r", [P, 2, E])
        xo = sb("xo", [P, 2, E])
        x1t = sb("x1t", [P, CH, 2, P], F16)
        aw_raw = sb("aw_raw", [P, E + E + 1])
        aw1 = sb("aw1", [P, CH, 2, P], F16)
        aw2 = sb("aw2", [P, 2, E], F16)
        b1 = sb("b1", [P, 2])
        arow = sb("arow", [P, 2, 3 * E])
        hf = sb("hf", [P, P])
        ht = sb("ht", [P, 2, P], F16)
        y = sb("y", [P, 2, E])
        yt = sb("yt", [P, E])
        stats, mv, var_e, rstd = sb("stats", [P, 6]), sb("mv", [P, 2]), sb("var_e", [P, 1]), sb("rstd", [P, 1])
        small = sb("small", [P, 96])
        scratch = small[:, 88:89]
        neg_max, total, inv = small[:, 0:1], small[:, 1:2], small[:, 2:3]
        ex, top = small[:, 8:16], small[:, 16:24]
        index_f, hit, pos, place_f = small[:, 24:26], small[:, 32:48], small[:, 48:50], small[:, 50:52]
        hit_n = small[:, 56:72]
        index_u = sb("index_u", [P, 8], U32)
        hit_h = sb("hit_h", [P, 16], F16)
        seen = sb("seen", [P, 16], F16)
        place_u = sb("place_u", [P, 2, 2], U32)
        entry = sb("entry", [P, 2, 2, 2], I32)
        pool_dummy = sb("pool_dummy", [P, 2])
        row_now, zero_i = sb("row_now", [P, 2], I32), sb("zero_i", [P, 1], I32)

        in_a, in_b, z0 = sem("in_a"), sem("in_b"), sem("z0")
        wt_in = [sem(f"wt_in{i}") for i in range(2)]
        fold_mm, fold_hi, fold_lo, pre, tab_out = sem("fold_mm"), sem("fold_hi"), sem("fold_lo"), sem("pre"), sem("tab_out")
        rf_bd = xr[:].rearrange("p g e -> p (g e)")[:, 0:HD].rearrange("p (h c) -> p h c", h=HP)
        stage = [arow[:].rearrange("p a e -> p (a e)")[:, 0:4 * E].rearrange("p (c n) -> p c n", c=4),
                 phq[:].bitcast(F32).rearrange("p a h t -> p (a h t)")[:, 0:4 * E].rearrange("p (c n) -> p c n", c=4)]
        dump_rows = o[:].rearrange("p a n -> p (a n)")[:, 0:P].bitcast(I32)
        zero_rows = y[:, 0, :]
        folded = [(WqT, wq, 0), (WqT, wq, 4), (WkT, wk, 0), (WkT, wk, 4)]
        plain = [(Wv, wv, 0), (Wv, wv, 1), (Wo, wo, 0), (Wo, wo, 1)]
        loads_a = (
            (ident, table[:, AT["ident"][0]:AT["ident"][1]]),
            (cst[:, P:P + 20], table[:, AT["expert"][0]:AT["dump"][1]]),
            (o[:, 1, 0:P], table[:, AT["before"][0]:AT["before"][1]]),
            (lang_i[:], lang.partition_broadcast(P)),
        )
        loads_b = (
            (wr[:], router), (b_out_rows[:], b_out.partition_broadcast(P)),
            (bias_rows[:], ffn_bias.partition_broadcast(P)),
            (rf_bd[0:64, :, 0:64], RF[:, 0:HP, :]), (rf_bd[64:P, :, 64:P], RF[:, HP:2 * HP, :]),
        )
        with nc.Block() as block:
            @block.sync
            def _(sp):
                for dst, src in loads_a:
                    sp.dma_start(dst, src).then_inc(in_a.sem, 16)
                for i, (src, _, p0) in enumerate(folded + plain):
                    if i >= 2:
                        if i - 2 < 4:
                            wait(sp, fold_mm, 0, 4 * (i - 1))
                        else:
                            wait(sp, fold_lo, 0, 16 + 4 * (i - 5))
                    if src is Wv:
                        piece = src[:, 2 * p0:2 * p0 + 2, :].rearrange("p c (a n) -> p (c a) n", a=2)
                    elif src is Wo:
                        piece = src[:, 4 * p0:4 * p0 + 4, :]
                    else:
                        piece = src[:, p0:p0 + 4, :]
                    sp.dma_start(stage[i % 2], piece).then_inc(wt_in[i % 2].sem, 16)
                wait(sp, pre, 0, 1)
                sp.dma_start(slots.rearrange("(p j) e -> p j e", p=P),
                             dump_rows.rearrange("p (j e) -> p j e", e=2)).then_inc(tab_out.sem, 16)
                wait(sp, z0, 0, 10)
                sp.dma_start(tokens[B * P:(B + 1) * P, :], zero_rows).then_inc(tab_out.sem, 16)
                sp.dma_start(acc[B * P:(B + 1) * P, :], zero_rows).then_inc(tab_out.sem, 16)
                sp.wait_ge(tab_out.sem, 48)

            @block.gpsimd
            def _(pool):
                pool.memset(rf_bd, 0.0).then_inc(z0.sem, 1)
                pool.wait_ge(z0.sem, 1)
                for dst, src in loads_b:
                    pool.dma_start(dst, src).then_inc(in_b.sem, 16)
                pool.memset(zero_rows, 0.0).then_inc(z0.sem, 1)
                pool.memset(o[:, 0, :], 0.0).then_inc(z0.sem, 1)
                pool.memset(kv[:], 0.0).then_inc(z0.sem, 1)
                pool.memset(v_h[:, :, 0], 1.0).then_inc(z0.sem, 1)
                pool.memset(v_h[:, :, 1], 0.0).then_inc(z0.sem, 1)
                pool.memset(ones[:], 1.0).then_inc(z0.sem, 1)
                pool.memset(seen[:], 0.0).then_inc(z0.sem, 1)
                pool.memset(half_pow[:], -0.5).then_inc(z0.sem, 1)
                pool.memset(pool_dummy[:], 0.0).then_inc(z0.sem, 1)
                pool.memset(zero_i[:], 0).then_inc(z0.sem, 1)
                pool.wait_ge(z0.sem, 11)
                pool.wait_ge(in_b.sem, 16 * len(loads_b))

            @block.tensor
            def _(pe):
                pe.wait_ge(in_b.sem, 16 * len(loads_b))
                for i in range(4):
                    pe.wait_ge(wt_in[i % 2].sem, 16 * (i // 2 + 1))
                    for c in range(CH):
                        n = CH * i + c
                        if n >= 8:
                            wait(pe, fold_lo, 0, n - 7)
                        for q in range(4):
                            last = pe.matmul(bank[n % 8][:, q * P:q * P + P], stage[i % 2][:, q, c * P:c * P + P],
                                             rf_bd[:, folded[i][2] + q, :], start=True, stop=True)
                        last.then_inc(fold_mm.sem, 1)

            def dst_of(i, c):
                _, dst, p0 = (folded + plain)[i]
                if i < 4:
                    return lambda h: dst[:, c, h, p0 * P:p0 * P + 512]
                if dst is wv:
                    return lambda h: dst[:, 2 * p0 + c // 2, h, (c % 2) * 512:(c % 2) * 512 + 512]
                return lambda h: dst[:, 4 * p0 + c, h, :]

            def src_of(i, c):
                return bank[(CH * i + c) % 8][:] if i < 4 else stage[i % 2][:, c, :]

            @block.scalar
            def _(act):
                for i in range(8):
                    if i >= 4:
                        act.wait_ge(wt_in[i % 2].sem, 16 * (i // 2 + 1))
                    for c in range(CH):
                        if i < 4:
                            wait(act, fold_mm, 0, CH * i + c + 1)
                        act.activation(dst_of(i, c)(0), src_of(i, c), ACT.Copy, scale=QS).then_inc(fold_hi.sem, 1)

            @block.vector
            def _(dve):
                dve.wait_ge(in_a.sem, 16 * len(loads_a))
                wait(dve, z0, 0, 3)
                dve.tensor_copy(dump_rows.rearrange("p (j e) -> p j e", e=2)[:, :, 0], dump.broadcast_to([P, 64])).then_inc(pre.sem, 1)
                dve.tensor_copy(before[:], o[:, 1, 0:P]).then_inc(pre.sem, 1)
                dve.tensor_copy(aw_raw[:, 0:B], lang_i[:]).then_inc(pre.sem, 1)
                dve.wait_ge(pre.sem, 3)
                dve.scalar_tensor_tensor(aw_raw[:, 0:B], aw_raw[:, 0:B], float(P), cur_token.broadcast_to([P, B]),
                                         ALU.mult, ALU.add).then_inc(pre.sem, 1)
                dve.wait_ge(pre.sem, 4)
                dve.tensor_copy(lang_rows[:], aw_raw[:, 0:B]).then_inc(pre.sem, 1)
                for i in range(8):
                    for c in range(CH):
                        wait(dve, fold_hi, 0, CH * i + c + 1)
                        dve.scalar_tensor_tensor(dst_of(i, c)(1), src_of(i, c), QS, dst_of(i, c)(0),
                                                 ALU.mult, ALU.subtract).then_inc(fold_lo.sem, 1)
                dve.wait_ge(pre.sem, 5)
                dve.wait_ge(fold_lo.sem, 32)

        ct_in, x_in = ([sem(f"{k}{i}", 1, 16) for i in range(G)] for k in ("ct_in", "x_in"))
        acc_out, tok_out = ([sem(f"{k}{i}", G // 2, 16) for i in range(2)] for k in ("acc_out", "tok_out"))
        slot_out = [sem(f"slot_out{i}", G, 16) for i in range(2)]
        aw_in, arow_in = sem("aw_in", 2 * G, 16), [sem(f"arow_in{i}", G // 2, 16) for i in range(2)]
        q_mm, k_mm, v_mm = sem("q_mm", HP), sem("k_mm", 2 * G), sem("v_mm", 2 * G)
        kv_mm, o_mm, o_tr, att_mm = sem("kv_mm", G), sem("o_mm", G), sem("o_tr", G), sem("att_mm", G)
        x1_tr, h_mm, ad_mm, y_tr, route_mm, count_mm = (sem(k, G) for k in ("x1_tr", "h_mm", "ad_mm", "y_tr", "route_mm", "count_mm"))
        q_hi, k_hi, v_hi, kv_hi, o_hi = sem("q_hi", HP), sem("k_hi", 2 * G), sem("v_hi", 2 * G), sem("kv_hi", 6 * G), sem("o_hi", 2 * G)
        x1_hi, h_done, y_copied, exp_done, aw_hi = (sem(k, G) for k in ("x1_hi", "h_done", "y_copied", "exp_done", "aw_hi"))
        q_lo, k_lo, v_lo, kv_lo, o_lo = sem("q_lo", HP), sem("k_lo", 2 * G), sem("v_lo", 2 * G), sem("kv_lo", 6 * G), sem("o_lo", 2 * G)
        nrm_add, nrm_inv, o_done, x1_done, x1_lo, h_hi, h_lo = (sem(k, G) for k in ("nrm_add", "nrm_inv", "o_done", "x1_done", "x1_lo", "h_hi", "h_lo"))
        s_done, st_done, mv_done, var_done, y_c, y_done, aw_lo = (sem(k, G) for k in ("s_done", "st_done", "mv_done", "var_done", "y_c", "y_done", "aw_lo"))
        max_done, inv_done, prob_done, top_done, index_done, indexf_done, hit_done, hith_done = (
            sem(k, G) for k in ("max_done", "inv_done", "prob_done", "top_done", "index_done", "indexf_done", "hit_done", "hith_done"))
        hitn_done, pos_done, placef_done, place_done = (sem(k, G) for k in ("hitn_done", "pos_done", "placef_done", "place_done"))
        xb_done, r_done, xo_done, rstd_done, cur_done = (sem(k, G) for k in ("xb_done", "r_done", "xo_done", "rstd_done", "cur_done"))
        seen_done, row_done = sem("seen_done", G), sem("row_done", G)
        entry_done = sem("entry_done", G)

        def earlier(g, b, k):
            if b >= k:
                return g, b - k
            return None if isinstance(g, int) and g == 0 else (g - 1, b - k + G)

        def four(ap):
            return ap.rearrange("p (c t) -> p c t", c=CH)

        def pairs(q, width):
            n = min(3, HP - 3 * q)
            return n, bank[2 + q][:, 0:n * width]

        def sync_slot(sp, g, b, heavy):
            if heavy:
                prev = earlier(g, b, G)
                if prev:
                    wait(sp, v_mm, prev[0], 2 * b + 2)
                sp.dma_start(ct[:, b], cond_t[g][:, b]).then_inc(ct_in[b].sem, 16)
                if prev:
                    wait(sp, xo_done, prev[0], b + 1)
                sp.dma_start(xr[:, b, :], x[g][:, b, :]).then_inc(x_in[b].sem, 16)

        def stores(act, t):
            wait(act, xo_done, t[0], t[1] + 1)
            act.dma_start(acc_rows(t), xo[:, t[1] % 2, :]).then_inc(acc_out[t[1] % 2].sem, 16)
            wait(act, y_done, t[0], t[1] + 1)
            act.dma_start(token_rows(t), y[:, t[1] % 2, :]).then_inc(tok_out[t[1] % 2].sem, 16)

        acc_v = acc[0:B * P, :].rearrange("(g b p) e -> g b p e", b=G, p=P)
        tok_v = tokens[0:B * P, :].rearrange("(g b p) e -> g b p e", b=G, p=P)

        def acc_rows(t):
            return acc_v[t[0]][t[1]]

        def token_rows(t):
            return tok_v[t[0]][t[1]]

        def k_or_v(pe, g, b, i):
            w, mm, lo = (wk, k_mm, k_lo) if i < 2 else (wv, v_mm, v_lo)
            if i == 0:
                wait(pe, ct_in[b], g, 1)
                before_b = earlier(g, b, 1)
                if before_b:
                    wait(pe, v_lo, before_b[0], 2 * before_b[1] + 1)
            elif i == 1:
                before_b = earlier(g, b, 1)
                if before_b:
                    wait(pe, v_lo, before_b[0], 2 * before_b[1] + 2)
            elif b == 0:
                wait(pe, q_lo, g, HP - 3 + i)
            else:
                wait(pe, k_lo, g, 2 * b + i - 1)
            half = slice((i % 2) * 512, (i % 2) * 512 + 512)
            three_passes(pe, bank[i % 2][:], [(lambda h, c=c: ct[:, b, c, h, :], lambda h, c=c: w[:, c, h, half])
                                              for c in range(CH)]).then_inc(mm.sem, 1)

        def q_block(pe, g, i):
            for b in range(G if i == 0 else 0):
                wait(pe, ct_in[b], g, 1)
            if i < 2:
                wait(pe, k_lo, g, i + 1)
            else:
                wait(pe, q_lo, g, i - 1)
            three_passes(pe, bank[i % 2][:], [(lambda h, c=c: wq[:, c, h, i * P:i * P + P], lambda h, c=c: ct[:, :, c, h, :])
                                              for c in range(CH)]).then_inc(q_mm.sem, 1)

        def kv_products(pe, t):
            g, b = t
            wait(pe, k_lo, g, 2 * b + 2)
            wait(pe, v_lo, g, 2 * b + 2)
            before_b = earlier(g, b, 1)
            if before_b:
                wait(pe, x1_done, before_b[0], before_b[1] + 1)
                before_c = earlier(g, b, 2)
                if before_c:
                    wait(pe, s_done, before_c[0], before_c[1] + 1)
            for h in range(HP):
                out = bank[2 + h // 3][:, (h % 3) * 130:(h % 3) * 130 + 130]
                for i, (a, w) in enumerate(PASSES):
                    last = pe.matmul(out, phk[:, b % 2, a, h * P:h * P + P], v_h[:, b % 2, w, 2 * h:2 * h + 2, :],
                                     start=(i == 0), stop=(i == 2))
            last.then_inc(kv_mm.sem, 1)

        def attend(pe, t):
            g, b = t
            wait(pe, kv_lo, g, 6 * b + 6)
            wait(pe, q_lo, g, HP)
            for h in range(HP):
                out = bank[2 + h // 3][:, (h % 3) * 132:(h % 3) * 132 + 132]
                for i, (a, w) in enumerate(PASSES):
                    last = pe.matmul(out, phq[:, h, a, b * P:b * P + P], kv[:, b % 2, w, 2 * h:2 * h + 2, :],
                                     start=(i == 0), stop=(i == 2))
            last.then_inc(o_mm.sem, 1)

        def o_transposes(pe, t, c):
            g, b = t
            wait(pe, o_done, g, b + 1)
            if c:
                wait(pe, x1_lo, c[0], c[1] + 1)
                c3 = earlier(g, b, 2)
                if c3:
                    wait(pe, exp_done, c3[0], c3[1] + 1)
            for h in range(HP):
                last = pe.transpose(bank[5 + h // 4][:, (h % 4) * P:(h % 4) * P + P], o[:, b % 2, h * P:h * P + P], ident)
            last.then_inc(o_tr.sem, 1)

        def att_out(pe, t):
            g, b = t
            wait(pe, o_lo, g, 2 * b + 2)
            three_passes(pe, bank[3][:], [(lambda h, k=k: ot[:, b % 2, k, h, :], lambda h, k=k: wo[:, k, h, :])
                                          for k in range(HP)]).then_inc(att_mm.sem, 1)

        def x1_transposes(pe, t):
            g, b = t
            wait(pe, x1_done, g, b + 1)
            wait(pe, o_lo, g, 2 * b + 2)
            for c in range(CH):
                last = pe.transpose(bank[5][:, c * P:c * P + P], xr[:, b, c * P:c * P + P], ident)
            last.then_inc(x1_tr.sem, 1)

        def adapter_h(pe, t):
            g, b = t
            wait(pe, x1_lo, g, b + 1)
            wait(pe, aw_lo, g, b + 1)
            three_passes(pe, bank[7][:, 0:P], [(lambda h, c=c: aw1[:, c, h, :], lambda h, c=c: x1t[:, c, h, :])
                                               for c in range(CH)]).then_inc(h_mm.sem, 1)

        def adapter_out(pe, t):
            g, b = t
            wait(pe, h_lo, g, b + 1)
            n1 = earlier_of(t, -1)
            if n1:
                wait(pe, o_done, n1[0], n1[1] + 1)
            three_passes(pe, bank[2][:], [(lambda h: ht[:, h, :], lambda h: aw2[:, h, :])]).then_inc(ad_mm.sem, 1)

        def y_transposes(pe, t):
            g, b = t
            wait(pe, y_done, g, b + 1)
            n1 = earlier_of(t, -1)
            if n1:
                wait(pe, o_lo, n1[0], 2 * n1[1] + 2)
            for c in range(CH):
                last = pe.transpose(bank[6][:, c * P:c * P + P], y[:, b % 2, c * P:c * P + P], ident)
            last.then_inc(y_tr.sem, 1)

        def route(pe, t):
            g, b = t
            wait(pe, y_copied, g, b + 1)
            for c in range(CH):
                last = pe.matmul(bank[5][:, 0:8], yt[:, c * P:c * P + P], wr[:, c, :], start=(c == 0), stop=(c == CH - 1))
            last.then_inc(route_mm.sem, 1)

        def count(pe, t):
            g, b = t
            wait(pe, hith_done, g, b + 1)
            before_c = earlier(g, b, 1)
            if before_c:
                wait(pe, seen_done, before_c[0], before_c[1] + 1)
            pe.matmul(bank[4][:, 0:16], before[:], hit_h[:], start=True, stop=False)
            pe.matmul(bank[4][:, 0:16], ones[:], seen[:], start=False, stop=True).then_inc(count_mm.sem, 1)

        def earlier_of(t, k):
            g, b = t
            b -= k
            if b >= G:
                return (g + 1, b - G) if not (isinstance(g, int) and g + 1 >= TRIPS) else None
            return g, b

        def tensor_slot(pe, g, b, heavy):
            A, Bb, C = (earlier(g, b, k) for k in (1, 2, 3))
            A = A if alive(A) else None
            Bb = Bb if alive(Bb) else None
            if heavy:
                k_or_v(pe, g, b, 0)
            if A:
                kv_products(pe, A)
            if Bb:
                x1_transposes(pe, Bb)
            if C:
                y_transposes(pe, C)
            if heavy:
                k_or_v(pe, g, b, 1)
            if A:
                attend(pe, A)
            if Bb:
                adapter_h(pe, Bb)
            if C:
                route(pe, C)
            if heavy and b == 0:
                for i in range(HP):
                    q_block(pe, g, i)
            if heavy:
                k_or_v(pe, g, b, 2)
            if A:
                o_transposes(pe, A, Bb)
            if Bb:
                adapter_out(pe, Bb)
            if C:
                count(pe, C)
            if heavy:
                k_or_v(pe, g, b, 3)
            if A:
                att_out(pe, A)

        def alive(t):
            return t is not None and not (isinstance(t[0], int) and t[0] >= TRIPS)

        def scalar_slot(act, g, b, heavy):
            A, Bb, C = (t if alive(t) else None for t in (earlier(g, b, k) for k in (1, 2, 3)))

            def k_hi_half(i):
                wait(act, k_mm, g, 2 * b + i + 1)
                act.activation(phk[:, b % 2, 0, i * 512:i * 512 + 512], bank[i][:], ACT.Relu).then_inc(k_hi.sem, 1)

            def v_hi_half(i):
                wait(act, v_mm, g, 2 * b + i + 1)
                act.activation(v_h[:, b % 2, 0, 8 * i:8 * i + 8, 0:64], bank[i][:].rearrange("p (h d) -> p h d", d=64),
                               ACT.Copy).then_inc(v_hi.sem, 1)

            if heavy:
                k_hi_half(0)
            if Bb:
                wait(act, x1_tr, Bb[0], Bb[1] + 1)
                act.activation(x1t[:, :, 0, :], four(bank[5][:]), ACT.Copy).then_inc(x1_hi.sem, 1)
            if A:
                wait(act, kv_mm, A[0], A[1] + 1)
                for q in range(3):
                    n, src = pairs(q, 130)
                    src = src.rearrange("p (n a c) -> p n a c", n=n, a=2)
                    dst = kv[:, A[1] % 2, 0].rearrange("p (n a) c -> p n a c", a=2)[:, 3 * q:3 * q + n]
                    for a in range(2):
                        act.activation(dst[64 * a:64 * a + 64, :, a, 0:65], src[64 * a:64 * a + 64, :, a, :],
                                       ACT.Copy, scale=1.0 / 16).then_inc(kv_hi.sem, 1)
            if C:
                wait(act, y_tr, C[0], C[1] + 1)
                act.activation(yt[:], bank[6][:], ACT.Copy).then_inc(y_copied.sem, 1)
            if heavy:
                k_hi_half(1)
            if Bb:
                wait(act, h_mm, Bb[0], Bb[1] + 1)
                act.activation(hf[:], bank[7][:, 0:P], ACT.Relu, bias=b1[:, Bb[1] % 2:Bb[1] % 2 + 1],
                               scale=1.0 / WS).then_inc(h_done.sem, 1)
            if C:
                wait(act, max_done, C[0], C[1] + 1)
                act.activation(ex, bank[5][:, 0:8], ACT.Exp, bias=neg_max, accum_out=total).then_inc(exp_done.sem, 1)
            if heavy and b == 0:
                for i in range(HP):
                    wait(act, q_mm, g, i + 1)
                    act.activation(phq[:, i, 0, :], bank[i % 2][:], ACT.Relu).then_inc(q_hi.sem, 1)
            if heavy:
                v_hi_half(0)
            if A:
                wait(act, o_tr, A[0], A[1] + 1)
                for i in range(2):
                    act.activation(ot[:, A[1] % 2, 4 * i:4 * i + 4, 0, :], four(bank[5 + i][:]), ACT.Copy).then_inc(o_hi.sem, 1)
            if heavy:
                v_hi_half(1)
            if A:
                if Bb:
                    wait(act, ad_mm, Bb[0], Bb[1] + 1)
                wait(act, aw_in, A[0], 2 * A[1] + 2)
                act.activation(b1[:, A[1] % 2:A[1] % 2 + 1], aw_raw[:, 2 * E:2 * E + 1], ACT.Copy)
                act.activation(aw1[:, :, 0, :], aw_raw[:, 0:E].rearrange("p (c a) -> p c a", c=CH), ACT.Copy, scale=WS)
                act.activation(aw2[:, 0, :], aw_raw[:, E:2 * E], ACT.Copy, scale=WS).then_inc(aw_hi.sem, 1)
            if Bb:
                stores(act, Bb)

        def vector_slot(dve, g, b, heavy):
            A, Bb, C = (t if alive(t) else None for t in (earlier(g, b, k) for k in (1, 2, 3)))

            def k_lo_half(i):
                wait(dve, k_hi, g, 2 * b + i + 1)
                part = slice(i * 512, i * 512 + 512)
                dve.scalar_tensor_tensor(phk[:, b % 2, 1, part], bank[i][:], 0.0, phk[:, b % 2, 0, part],
                                         ALU.max, ALU.subtract).then_inc(k_lo.sem, 1)

            def v_lo_half(i):
                wait(dve, v_hi, g, 2 * b + i + 1)
                dve.tensor_tensor(v_h[:, b % 2, 1, 8 * i:8 * i + 8, 0:64], bank[i][:].rearrange("p (h d) -> p h d", d=64),
                                  v_h[:, b % 2, 0, 8 * i:8 * i + 8, 0:64], ALU.subtract).then_inc(v_lo.sem, 1)

            def link(sig, t):
                wait(dve, sig, t[0], t[1] + 1)

            def take_wait():
                dve.memset(scratch, 0.0)

            if heavy:
                k_lo_half(0)
            if Bb:
                link(x1_hi, Bb)
                dve.tensor_tensor(x1t[:, :, 1, :], four(bank[5][:]), x1t[:, :, 0, :], ALU.subtract).then_inc(x1_lo.sem, 1)
            if A:
                for q in range(3):
                    n, src = pairs(q, 130)
                    src = src.rearrange("p (n a c) -> p n a c", n=n, a=2)
                    halves = [kv[:, A[1] % 2, h].rearrange("p (n a) c -> p n a c", a=2)[:, 3 * q:3 * q + n] for h in range(2)]
                    for a in range(2):
                        rows = slice(64 * a, 64 * a + 64)
                        wait(dve, kv_hi, A[0], 6 * A[1] + 2 * q + a + 1)
                        dve.scalar_tensor_tensor(halves[1][rows, :, a, 0:65], src[rows, :, a, :], 1.0 / 16,
                                                 halves[0][rows, :, a, 0:65], ALU.mult, ALU.subtract).then_inc(kv_lo.sem, 1)
            if heavy:
                k_lo_half(1)
            if A:
                ab = A[1] % 2
                link(o_mm, A)
                for q in range(3):
                    n, src = pairs(q, 132)
                    last = dve.tensor_scalar(nrm[:, ab, 6 * q:6 * q + 2 * n], src.rearrange("p (h c) -> p h c", c=66)[:, :, 64],
                                             16e-6, None, ALU.add)
                last.then_inc(nrm_add.sem, 1)
                link(nrm_add, A)
                dve.reciprocal(nrm[:, ab, :], nrm[:, ab, :]).then_inc(nrm_inv.sem, 1)
                link(nrm_inv, A)
                for q in range(3):
                    n, src = pairs(q, 132)
                    last = dve.tensor_tensor(o[:, ab, 6 * q * 64:(6 * q + 2 * n) * 64].rearrange("p (h c) -> p h c", c=64),
                                             src.rearrange("p (h c) -> p h c", c=66)[:, :, 0:64],
                                             repeated(nrm[:, ab, 6 * q:6 * q + 2 * n], 2, 64), ALU.mult)
                last.then_inc(o_done.sem, 1)
            if C:
                link(route_mm, C)
                dve.tensor_reduce(neg_max, bank[5][:, 0:8], AX_X, ALU.max, negate=True).then_inc(max_done.sem, 1)
            if Bb:
                link(h_done, Bb)
                dve.tensor_copy(ht[:, 0, :], hf[:]).then_inc(h_hi.sem, 1)
                link(h_hi, Bb)
                dve.tensor_tensor(ht[:, 1, :], hf[:], ht[:, 0, :], ALU.subtract).then_inc(h_lo.sem, 1)
            if C:
                cb = C[1] % 2
                link(exp_done, C)
                dve.reciprocal(inv, total).then_inc(inv_done.sem, 1)
                link(inv_done, C)
                dve.tensor_scalar(ex, ex, inv, None, ALU.mult).then_inc(prob_done.sem, 1)
                link(prob_done, C)
                take_wait()
                dve.max(top, ex).then_inc(top_done.sem, 1)
                link(top_done, C)
                take_wait()
                dve.max_index(index_u[:], top, ex).then_inc(index_done.sem, 1)
                before_c, last_entry = earlier(*C, 1), earlier(*C, 2)
                if before_c:
                    link(cur_done, before_c)
                if last_entry:
                    wait(dve, slot_out[cb], last_entry[0], 2 * (last_entry[1] // 2) + 2)
                dve.tensor_copy(entry[:, cb, :, 0], cur_token.broadcast_to([P, 2]))
                dve.tensor_scalar(entry[:, cb, :, 1].bitcast(F32), top[:, 0:2], 1.0 / WS, None,
                                  ALU.mult).then_inc(entry_done.sem, 1)
                link(index_done, C)
                dve.tensor_copy(index_f, index_u[:, 0:2]).then_inc(indexf_done.sem, 1)
                link(indexf_done, C)
                dve.tensor_scalar(cur_token, cur_token, float(P), None, ALU.add).then_inc(cur_done.sem, 1)
                dve.tensor_tensor(hit.rearrange("p (k e) -> p k e", k=2), expert.rearrange("p (k e) -> p k e", k=2),
                                  repeated(index_f, 2, 8), ALU.is_equal).then_inc(hit_done.sem, 1)
                link(hit_done, C)
                dve.tensor_copy(hit_h[:], hit).then_inc(hith_done.sem, 1)
            if heavy and b == 0:
                for i in range(HP):
                    wait(dve, q_hi, g, i + 1)
                    dve.scalar_tensor_tensor(phq[:, i, 1, :], bank[i % 2][:], 0.0, phq[:, i, 0, :],
                                             ALU.max, ALU.subtract).then_inc(q_lo.sem, 1)
            if heavy:
                v_lo_half(0)
            if A:
                for i in range(2):
                    wait(dve, o_hi, A[0], 2 * A[1] + i + 1)
                    dve.tensor_tensor(ot[:, A[1] % 2, 4 * i:4 * i + 4, 1, :], four(bank[5 + i][:]),
                                      ot[:, A[1] % 2, 4 * i:4 * i + 4, 0, :], ALU.subtract).then_inc(o_lo.sem, 1)
            if Bb:
                bb = Bb[1] % 2
                link(r_done, Bb)
                link(ad_mm, Bb)
                dve.scalar_tensor_tensor(r[:, bb, :], bank[2][:], 1.0 / WS, r[:, bb, :], ALU.mult, ALU.add).then_inc(s_done.sem, 1)
                link(s_done, Bb)
                dve.bn_stats(stats[:], r[:, bb, :]).then_inc(st_done.sem, 1)
                link(st_done, Bb)
                take_wait()
                dve.bn_aggr(mv[:], stats[:]).then_inc(mv_done.sem, 1)
                link(mv_done, Bb)
                dve.tensor_scalar(var_e[:], mv[:, 1:2], 1e-5, None, ALU.add).then_inc(var_done.sem, 1)
                dve.wait_ge(arow_in[bb].sem, arow_in[bb].after(Bb[0], Bb[1] // 2 + 1))
                prev = earlier(*Bb, 2)
                if prev:
                    wait(dve, tok_out[bb], prev[0], prev[1] // 2 + 1)
                dve.scalar_tensor_tensor(y[:, bb, :], r[:, bb, :], mv[:, 0:1], arow[:, bb, E:2 * E],
                                         ALU.subtract, ALU.mult).then_inc(y_c.sem, 1)
                link(rstd_done, Bb)
                link(y_c, Bb)
                dve.scalar_tensor_tensor(y[:, bb, :], y[:, bb, :], rstd[:, 0:1], arow[:, bb, 2 * E:3 * E],
                                         ALU.mult, ALU.add).then_inc(y_done.sem, 1)
            if C:
                link(count_mm, C)
                dve.tensor_tensor(hit_n, bank[4][:, 0:16], hit, ALU.mult).then_inc(hitn_done.sem, 1)
                link(hitn_done, C)
                dve.tensor_reduce(pos, hit_n.rearrange("p (k e) -> p k e", k=2), AX_X, ALU.add).then_inc(pos_done.sem, 1)
                if before_c:
                    link(seen_done, before_c)
                dve.tensor_tensor(seen[:], seen[:], hit_h[:], ALU.add).then_inc(seen_done.sem, 1)
                link(pos_done, C)
                dve.scalar_tensor_tensor(place_f, pos, 16.0, index_f, ALU.mult, ALU.add).then_inc(placef_done.sem, 1)
                link(placef_done, C)
                dve.tensor_tensor(place_u[:, C[1] % 2, :], place_f, choice, ALU.add).then_inc(place_done.sem, 1)
            if heavy:
                v_lo_half(1)
            if A:
                link(aw_hi, A)
                dve.scalar_tensor_tensor(aw1[:, :, 1, :], aw_raw[:, 0:E].rearrange("p (c a) -> p c a", c=CH), WS,
                                         aw1[:, :, 0, :], ALU.mult, ALU.subtract)
                dve.scalar_tensor_tensor(aw2[:, 1, :], aw_raw[:, E:2 * E], WS, aw2[:, 0, :],
                                         ALU.mult, ALU.subtract).then_inc(aw_lo.sem, 1)
                link(xb_done, A)
                link(att_mm, A)
                dve.scalar_tensor_tensor(xr[:, A[1], :], bank[3][:], 1.0 / (QS * 16), xr[:, A[1], :],
                                         ALU.mult, ALU.add).then_inc(x1_done.sem, 1)

        def pool_slot(pool, g, b, heavy):
            A, Bb, C = (t if alive(t) else None for t in (earlier(g, b, k) for k in (1, 2, 3)))

            def take_wait(t):
                if isinstance(t[0], int):
                    return
                pool.tensor_tensor(pool_dummy[:, 0:1], pool_dummy[:, 1:2], pool_dummy[:, 1:2], ALU.add)

            if A:
                n = A[0] * G + A[1]
                before_a = earlier(A[0], A[1], 1)
                if before_a:
                    wait(pool, aw_lo, before_a[0], before_a[1] + 1)
                    wait(pool, aw_in, before_a[0], 2 * before_a[1] + 2)
                    wait(pool, arow_in[before_a[1] % 2], before_a[0], before_a[1] // 2 + 1)
                pool.tensor_tensor(row_now[:, 0:1], lang_rows[:, bass.ds(n, 1)], zero_i[:], ALU.add)
                pool.tensor_tensor(row_now[:, 1:2], lang_i[:, bass.ds(n, 1)], zero_i[:], ALU.add).then_inc(row_done.sem, 1)
                wait(pool, row_done, A[0], A[1] + 1)
                take_wait(A)
                rows = row_now[:, 0:1]
                pool.indirect_dma_start(out=aw_raw[:, 0:E], out_offset=None, in_=A1,
                                        in_offset=bass.IndirectOffsetOnAxis(rows, 0)).then_inc(aw_in.sem, 16)
                pool.indirect_dma_start(out=aw_raw[:, E:2 * E + 1], out_offset=None, in_=A2,
                                        in_offset=bass.IndirectOffsetOnAxis(rows, 0)).then_inc(aw_in.sem, 16)
                pool.indirect_dma_start(out=arow[:, A[1] % 2, :], out_offset=None, in_=rows3,
                                        in_offset=bass.IndirectOffsetOnAxis(row_now[:, 1:2], 0)).then_inc(arow_in[A[1] % 2].sem, 16)
            if Bb:
                bb = Bb[1] % 2
                wait(pool, arow_in[bb], Bb[0], Bb[1] // 2 + 1)
                wait(pool, x1_done, Bb[0], Bb[1] + 1)
                pool.tensor_tensor(r[:, bb, :], xr[:, Bb[1], :], arow[:, bb, 0:E], ALU.add).then_inc(r_done.sem, 1)
                prev = earlier(*Bb, 2)
                if prev:
                    wait(pool, acc_out[bb], prev[0], prev[1] // 2 + 1)
                wait(pool, x1_tr, Bb[0], Bb[1] + 1)
                pool.tensor_tensor(xo[:, bb, :], xr[:, Bb[1], :], bias_rows[:], ALU.add).then_inc(xo_done.sem, 1)
            if heavy:
                wait(pool, x_in[b], g, 1)
                pool.tensor_tensor(xr[:, b, :], xr[:, b, :], b_out_rows[:], ALU.add).then_inc(xb_done.sem, 1)
            if Bb:
                wait(pool, var_done, Bb[0], Bb[1] + 1)
                pool.tensor_tensor(rstd[:], var_e[:], half_pow[:], ALU.pow).then_inc(rstd_done.sem, 1)
            if C:
                wait(pool, place_done, C[0], C[1] + 1)
                take_wait(C)
                for k in range(2):
                    pool.indirect_dma_start(out=slots, out_offset=bass.IndirectOffsetOnAxis(place_u[:, C[1] % 2, k:k + 1], 0),
                                            in_=entry[:, C[1] % 2, k, :], in_offset=None, bounds_check=8 * 2 * 512 - 1,
                                            oob_is_err=False).then_inc(slot_out[C[1] % 2].sem, 16)

        def run(eng, slot):
            for b in range(G):
                slot(eng, 0, b, True)
            with eng.Fori(1, TRIPS) as g:
                for b in range(G):
                    slot(eng, g, b, True)
            for b in range(3):
                slot(eng, TRIPS, b, False)

        with nc.Block() as block:
            @block.sync
            def _(sp):
                run(sp, sync_slot)

            @block.tensor
            def _(pe):
                run(pe, tensor_slot)

            @block.scalar
            def _(act):
                run(act, scalar_slot)

            @block.vector
            def _(dve):
                run(dve, vector_slot)

            @block.gpsimd
            def _(pool):
                run(pool, pool_slot)
                for stored in (*acc_out, *tok_out, *slot_out):
                    wait(pool, stored, TRIPS)


def expert_phase(nc, table, acc, tokens, slots, weights, out):
    EXPERTS, FC, Q = 8, 16, 4
    _, AT = constant_tables()
    PASSES_ALL = 2 * EXPERTS
    with ExitStack() as ctx, Semaphores(nc) as semaphores:
        def sb(name, shape, dt=F32):
            return ctx.enter_context(nc.sbuf_tensor("e_" + name, shape, dt))

        def sem(name, per=1, step=1):
            return Signal(semaphores.new("e_" + name), per, step)

        bank = [ctx.enter_context(nc.psum_tensor(f"e_bank{i}", [P, 512], F32)) for i in range(8)]
        ident = sb("ident", [P, P])
        slot_sb = sb("slot_sb", [P, Q, 2, EXPERTS, 2], I32)
        stage = sb("stage", [P, 4, 2 * E])
        w1 = sb("w1", [P, FC, CH, 2, P], F16)
        w2 = sb("w2", [P, FC, 2, E], F16)
        take = sb("take", [P, 2, Q], I32)
        give = sb("give", [P, 2, Q], I32)
        share = sb("share", [P, 2, Q], I32)
        xg = sb("xg", [P, Q, E])
        xt = sb("xt", [P, 2, CH, 2, E], F16)
        hf = sb("hf", [P, 2, E])
        hh = sb("hh", [P, 4, 2, E], F16)
        ys = sb("ys", [P, Q, E])
        dummy = sb("dummy", [P, 16])

        ident_in, slots_in, d0 = sem("ident_in"), sem("slots_in"), sem("d0")
        stage_in = [sem(f"stage_in{i}", FC // 4, 16) for i in range(4)]
        w_hi, w_lo = sem("w_hi", FC), sem("w_lo", FC)
        take_done, give_done = sem("take_done"), sem("give_done")
        x_in, y_out = [sem(f"x_in{q}", 1, 16) for q in range(Q)], sem("y_out", Q, 16)
        x_tr, h_mm, y_mm = sem("x_tr", Q), sem("h_mm", FC), sem("y_mm", FC)
        x_hi, gelu_done = sem("x_hi", Q), sem("gelu_done", FC)
        x_lo, h_hi, h_lo = sem("x_lo", Q), sem("h_hi", FC), sem("h_lo", FC)
        y_done = sem("y_done", Q)
        out_done = sem("out_done")

        def back(p, f, n):
            if f >= n:
                return p, f - n
            return None if isinstance(p, int) and p == 0 else (p - 1, f - n + FC)

        def run(eng, one):
            one(eng, 0, 0, 0)
            with eng.Fori(1, EXPERTS) as t:
                one(eng, 2 * t - 1, t - 1, 1)
                one(eng, 2 * t, t, 0)
            one(eng, PASSES_ALL - 1, EXPERTS - 1, 1)

        def is_last(p):
            return isinstance(p, int) and p == PASSES_ALL - 1

        def following(p, e, k):
            return (p + 1, e, 1) if k == 0 else (p + 1, e + 1, 0)

        def load_expert(sp, e):
            for c in range(FC):
                if c >= 4:
                    wait(sp, w_lo, e, c - 3)
                elif not (isinstance(e, int) and e == 0):
                    wait(sp, w_lo, e - 1, FC + c - 3)
                sp.dma_start(stage[:, c % 4, :], weights[e][c]).then_inc(stage_in[c % 4].sem, 16)

        def chunk_at(p, e, k, f):
            if isinstance(p, int) and p == 0:
                return (e, f + 2) if f + 2 < FC else None
            if k == 1:
                return (e + 1, f - 4) if f >= 4 and not is_last(p) else None
            return (e, FC - 4 + f) if f < 4 else None

        def split_hi(act, e, c, readers):
            wait(act, stage_in[c % 4], e, c // 4 + 1)
            if readers:
                wait(act, y_mm, *readers)
            act.activation(w1[:, c, :, 0, :], stage[:, c % 4, 0:E].rearrange("p (c t) -> p c t", c=CH), ACT.Copy, scale=WS)
            act.activation(w2[:, c, 0, :], stage[:, c % 4, E:2 * E], ACT.Copy, scale=WS).then_inc(w_hi.sem, 1)

        def split_lo(dve, e, c):
            wait(dve, w_hi, e, c + 1)
            dve.scalar_tensor_tensor(w1[:, c, :, 1, :], stage[:, c % 4, 0:E].rearrange("p (c t) -> p c t", c=CH), WS,
                                     w1[:, c, :, 0, :], ALU.mult, ALU.subtract)
            dve.scalar_tensor_tensor(w2[:, c, 1, :], stage[:, c % 4, E:2 * E], WS, w2[:, c, 0, :],
                                     ALU.mult, ALU.subtract).then_inc(w_lo.sem, 1)

        def x_transposes(pe, p, k, q):
            wait(pe, x_in[q], p, 1)
            if q >= 2:
                wait(pe, x_lo, p, q - 1)
            elif not (isinstance(p, int) and p == 0):
                wait(pe, x_lo, p - 1, Q - 1 + q)
            for c in range(CH):
                last = pe.transpose(bank[2 + q % 2][:, c * P:c * P + P], xg[:, q, c * P:c * P + P], ident[:])
            last.then_inc(x_tr.sem, 1)

        def y_block(pe, p, f):
            if f == 0 and not (isinstance(p, int) and p == 0):
                wait(pe, y_done, p - 1, Q)
            wait(pe, h_lo, p, f + 1)
            for q in range(Q):
                for i, (a, w) in enumerate(PASSES):
                    last = pe.matmul(bank[4 + q][:], hh[:, f % 4, a, q * P:q * P + P], w2[:, f, w, :],
                                     start=(f == 0 and i == 0), stop=(f == FC - 1 and i == 2))
            last.then_inc(y_mm.sem, 1)

        def tensor_pass(pe, p, e, k):
            for f in range(FC):
                if f == 0:
                    wait(pe, x_lo, p, Q)
                if k == 0:
                    wait(pe, w_lo, e, f + 1)
                two = back(p, f, 2)
                if two:
                    wait(pe, gelu_done, two[0], two[1] + 1)
                three_passes(pe, bank[f % 2][:], [(lambda h, c=c: w1[:, f, c, h, :], lambda h, c=c: xt[:, k, c, h, :])
                                                  for c in range(CH)]).then_inc(h_mm.sem, 1)
                if two:
                    y_block(pe, *two)
                if 8 <= f < 8 + Q and not is_last(p):
                    x_transposes(pe, p + 1, 1 - k, f - 8)

        def x_hi_half(act, p, k, q):
            wait(act, x_tr, p, q + 1)
            act.activation(xt[:, k, :, 0, q * P:q * P + P], bank[2 + q % 2][:].rearrange("p (c t) -> p c t", c=CH),
                           ACT.Copy).then_inc(x_hi.sem, 1)

        def x_lo_half(dve, p, k, q):
            wait(dve, x_hi, p, q + 1)
            dve.tensor_tensor(xt[:, k, :, 1, q * P:q * P + P], bank[2 + q % 2][:].rearrange("p (c t) -> p c t", c=CH),
                              xt[:, k, :, 0, q * P:q * P + P], ALU.subtract).then_inc(x_lo.sem, 1)

        def scalar_pass(act, p, e, k):
            for f in range(FC):
                wait(act, h_mm, p, f + 1)
                two = back(p, f, 2)
                if two:
                    wait(act, h_lo, two[0], two[1] + 1)
                act.activation(hf[:, f % 2, :], bank[f % 2][:], ACT.Gelu_apprx_tanh, scale=1.0 / WS).then_inc(gelu_done.sem, 1)
                job = chunk_at(p, e, k, f)
                if job:
                    c = job[1]
                    split_hi(act, *job, None if isinstance(p, int) and p == 0 else
                             ((p, c + 1) if k == 1 else (p - 1, c + 1)))
                if 8 <= f < 8 + Q and not is_last(p):
                    x_hi_half(act, p + 1, 1 - k, f - 8)

        def y_evacuate(dve, p, k):
            wait(dve, y_mm, p, FC)
            wait(dve, give_done, p, 1)
            if not (isinstance(p, int) and p == 0):
                wait(dve, y_out, p - 1, Q)
            for q in range(Q):
                dve.tensor_scalar(ys[:, q, :], bank[4 + q][:], share[:, k, q:q + 1].bitcast(F32), None,
                                  ALU.mult).then_inc(y_done.sem, 1)

        def vector_pass(dve, p, e, k):
            for f in range(FC):
                wait(dve, gelu_done, p, f + 1)
                four = back(p, f, 4)
                if four:
                    wait(dve, y_mm, four[0], four[1] + 1)
                dve.tensor_copy(hh[:, f % 4, 0, :], hf[:, f % 2, :]).then_inc(h_hi.sem, 1)
                wait(dve, h_hi, p, f + 1)
                dve.tensor_tensor(hh[:, f % 4, 1, :], hf[:, f % 2, :], hh[:, f % 4, 0, :], ALU.subtract).then_inc(h_lo.sem, 1)
                if f == 1 and not (isinstance(p, int) and p == 0):
                    y_evacuate(dve, p - 1, 1 - k)
                job = chunk_at(p, e, k, f)
                if job:
                    split_lo(dve, *job)
                if 8 <= f < 8 + Q and not is_last(p):
                    x_lo_half(dve, p + 1, 1 - k, f - 8)

        def take_wait(pool, p, n):
            if not isinstance(p, int):
                pool.tensor_tensor(dummy[:, n:n + 1], dummy[:, 15:16], dummy[:, 15:16], ALU.add)

        def column(e, k, which):
            return slot_sb[:, :, k, bass.ds(e, 1), which]

        def gathers(pool, p, e, k):
            if not (isinstance(p, int) and p == 0):
                wait(pool, x_tr, p - 1, Q)
            pool.tensor_copy(take[:, k, :], column(e, k, 0)).then_inc(take_done.sem, 1)
            wait(pool, take_done, p, 1)
            take_wait(pool, p, k)
            for q in range(Q):
                pool.indirect_dma_start(out=xg[:, q, :], out_offset=None, in_=tokens,
                                        in_offset=bass.IndirectOffsetOnAxis(take[:, k, q:q + 1], 0)).then_inc(x_in[q].sem, 16)

        def additions(pool, p, e, k):
            for q in range(Q):
                wait(pool, y_done, p, q + 1)
                if q:
                    wait(pool, y_out, p, q)
                take_wait(pool, p, 2 + Q * k + q)
                pool.indirect_dma_start(out=acc, out_offset=bass.IndirectOffsetOnAxis(give[:, k, q:q + 1], 0),
                                        in_=ys[:, q, :], in_offset=None, compute_op=ALU.add).then_inc(y_out.sem, 16)

        def pool_pass(pool, p, e, k):
            if not is_last(p):
                gathers(pool, *following(p, e, k))
            if not (isinstance(p, int) and p == 0):
                additions(pool, p - 1, e if k == 1 else e - 1, 1 - k)
            pool.tensor_copy(give[:, k, :], column(e, k, 0))
            pool.tensor_copy(share[:, k, :], column(e, k, 1)).then_inc(give_done.sem, 1)

        with nc.Block() as block:
            @block.sync
            def _(sp):
                sp.dma_start(ident[:], table[:, AT["ident"][0]:AT["ident"][1]]).then_inc(ident_in.sem, 16)
                load_expert(sp, 0)
                with sp.Fori(1, EXPERTS) as e:
                    load_expert(sp, e)
                wait(sp, y_out, PASSES_ALL)
                half = B * P // 2
                sp.dma_start(out[0:half, :], acc[0:half, :]).then_inc(out_done.sem, 16)
                sp.wait_ge(out_done.sem, 32)

            @block.tensor
            def _(pe):
                pe.wait_ge(ident_in.sem, 16)
                for q in range(Q):
                    x_transposes(pe, 0, 0, q)
                run(pe, tensor_pass)
                y_block(pe, PASSES_ALL - 1, FC - 2)
                y_block(pe, PASSES_ALL - 1, FC - 1)

            @block.scalar
            def _(act):
                split_hi(act, 0, 0, None)
                split_hi(act, 0, 1, None)
                for q in range(Q):
                    x_hi_half(act, 0, 0, q)
                run(act, scalar_pass)
                half = B * P // 2
                wait(act, y_out, PASSES_ALL)
                act.dma_start(out[half:2 * half, :], acc[half:2 * half, :]).then_inc(out_done.sem, 16)

            @block.vector
            def _(dve):
                split_lo(dve, 0, 0)
                split_lo(dve, 0, 1)
                for q in range(Q):
                    x_lo_half(dve, 0, 0, q)
                run(dve, vector_pass)
                y_evacuate(dve, PASSES_ALL - 1, 1)

            @block.gpsimd
            def _(pool):
                pool.dma_start(slot_sb[:], slots.rearrange("(p q k e) w -> p q k e w", q=Q, k=2, e=EXPERTS)).then_inc(slots_in.sem, 16)
                pool.memset(dummy[:], 0.0).then_inc(d0.sem, 1)
                pool.wait_ge(d0.sem, 1)
                pool.wait_ge(slots_in.sem, 16)
                gathers(pool, 0, 0, 0)
                run(pool, pool_pass)
                additions(pool, PASSES_ALL - 1, EXPERTS - 1, 1)


def layer(nc, a, out):
    cond_t = nc.dram_tensor("cond_t", (TRIPS, P, G, CH, 2, P), F16, kind="Internal").ap()
    acc = nc.dram_tensor("acc", ((B + 1) * P, E), F32, kind="Internal").ap()
    tokens = nc.dram_tensor("tokens", ((B + 1) * P, E), F32, kind="Internal").ap()
    slots = nc.dram_tensor("slots", (8 * 2 * 512, 2), I32, kind="Internal").ap()
    cond_phase(nc, a["table"], a["x"], a["x_t"], a["tau_ctx"], a["tau"], a["Wg"], a["bg"], a["Wn1"], a["bn1"],
               a["Wn2"], a["bn2"], a["blend_t"], a["Wsoma"], a["bsoma"], a["Wtemp"], a["btemp"], a["Wout"],
               a["gamma"], a["beta"], cond_t)
    attention_phase(nc, a["table"], cond_t, a["x"], a["WqT"], a["WkT"], a["RF"], a["Wv"], a["Wo"], a["b_out"],
                    a["ffn_bias"], a["lang"], a["A1"], a["A2"], a["rows3"], a["router"], acc, tokens, slots)
    expert_phase(nc, a["table"], acc, tokens, slots, a["experts"], out)


def layouts(i):
    x = i["x"]

    def by_chunk(w):
        return np.ascontiguousarray(w.reshape(-1, P, w.shape[1]).transpose(1, 0, 2))

    def by_pair(w):
        return np.ascontiguousarray(w.T.reshape(8, P, E).transpose(1, 0, 2))

    W, rf = i["L0_attn_W_qkv"], i["L0_attn_RF"]
    HD = W.shape[1] // 3
    langs = i["L0_cond2_W1"].shape[0]
    w1, w2 = i["L0_ffn_w1"], i["L0_ffn_w2"]
    n_e, _, F = w1.shape
    w1 = w1.reshape(n_e, CH, P, F // P, P).transpose(0, 3, 2, 1, 4).reshape(n_e, F // P, P, E)
    w2 = w2.reshape(n_e, F // P, P, E)
    lay = {
        "table": constant_tables()[0],
        "x": x.reshape(TRIPS, G, P, E).transpose(0, 2, 1, 3),
        "x_t": x.reshape(TRIPS, G, P, CH, P).transpose(0, 4, 3, 1, 2).reshape(TRIPS, P, CH, GT),
        "tau_ctx": i["L0_cond_tau_ctx"].reshape(1), "tau": i["condB_tauraws"],
        "Wg": by_chunk(i["L0_cond_Wg"].T), "bg": i["L0_cond_bg"],
        "Wn1": by_chunk(i["L0_cond_Wn1"].T), "bn1": i["L0_cond_bn1"],
        "Wn2": i["cond_256"].T, "bn2": i["condB_bn2"],
        "blend_t": i["cond_1024"].reshape(D, CH, P).transpose(2, 1, 0).reshape(P, CH * D),
        "Wsoma": by_chunk(i["L0_cond_Wsoma"].T), "bsoma": i["L0_cond_bsoma"].reshape(CH, P).T,
        "Wtemp": by_chunk(i["L0_cond_Wtemp"].T), "btemp": i["L0_cond_btemp"].reshape(CH, P).T,
        "Wout": by_chunk(i["L0_cond_Wout"].T), "gamma": i["L0_cond_gamma"], "beta": i["L0_cond_beta"],
        "WqT": by_pair(W[:, 0:HD]), "WkT": by_pair(W[:, HD:2 * HD]),
        "RF": np.concatenate([rf[0::2], rf[1::2]]).transpose(1, 0, 2),
        "Wv": by_chunk(W[:, 2 * HD:]), "Wo": by_chunk(i["L0_attn_W_out"]), "b_out": i["L0_attn_b_out"],
        "ffn_bias": i["L0_ffn_bias"].reshape(E), "lang": i["itok_B_0_8"],
        "A1": i["L0_cond2_W1"].reshape(langs, CH, P, P).transpose(0, 2, 1, 3).reshape(langs * P, E),
        "A2": np.concatenate([i["L0_cond2_W2"], i["L0_cond2_b1"][:, :, None]], 2).reshape(langs * P, E + 1),
        "rows3": np.concatenate([i["L0_cond2_b2"], i["L0_cond2_gamma"], i["L0_cond2_beta"]], 1),
        "router": by_chunk(i["L0_ffn_router_w"]),
        "experts": np.concatenate([w1, w2], 3),
    }
    return {k: np.ascontiguousarray(v) for k, v in lay.items()}


def kernel(**inputs):
    import concourse.bacc as _bacc
    from concourse.bass_utils import run_bass_kernel_spmd as _run

    nc = _bacc.Bacc("TRN2", target_bir_lowering=False, num_devices=1)
    lay = layouts({k: np.asarray(v) for k, v in inputs.items()})
    args = {n: nc.dram_tensor(f"in_{n}_dram", a.shape, mybir.dt.from_np(a.dtype), kind="ExternalInput").ap()
            for n, a in lay.items()}
    out = nc.dram_tensor("out_0_dram", (B * P, E), F32, kind="ExternalOutput").ap()
    layer(nc, args, out)
    r = _run(nc, [{f"in_{n}_dram": a for n, a in lay.items()}], core_ids=[0])
    return r.results[0]["out_0_dram"].reshape(B, P, E)
```

```python
from contextlib import ExitStack

import numpy as np
import concourse.bass as bass
from concourse import mybir

F32 = mybir.dt.float32
F16 = mybir.dt.float16
I32 = mybir.dt.int32
U32 = mybir.dt.uint32
ALU = mybir.AluOpType
ACT = mybir.ActivationFunctionType
AX_X = mybir.AxisListType.X

P = 128
B = 32
E = 512
CH = E // P
G = 4
GT = G * P
TRIPS = B // G
D = 32
L = 8
NL = P // L

PASSES = ((0, 0), (0, 1), (1, 0))
WS = 64.0
QS = 16.0


class Signal:

    def __init__(self, sem, per=1, step=1):
        self.sem, self.per, self.step = sem, per, step

    def after(self, trip, n=0):
        return trip * (self.per * self.step) + n * self.step


class Semaphores:

    def __init__(self, nc):
        self.nc, self.taken = nc, []

    def new(self, name):
        self.taken.append(self.nc.alloc_semaphore(name))
        return self.taken[-1]

    def __enter__(self):
        return self

    def __exit__(self, *error):
        self.nc.clear_and_free_semaphores(self.taken)
        self.nc.all_engine_barrier()


def wait(eng, signal, trip, n=0):
    value = signal.after(trip, n)
    if isinstance(value, int) and value == 0:
        return
    eng.wait_ge(signal.sem, value)


def repeated(ap, axis, n):
    ap = ap.unsqueeze(axis)
    shape = list(ap.shape)
    shape[axis] = n
    return ap.broadcast_to(shape)


def three_passes(pe, out, pairs):
    n = len(pairs) * len(PASSES)
    i = 0
    for lhs, rhs in pairs:
        for a, b in PASSES:
            last = pe.matmul(out, lhs(a), rhs(b), start=(i == 0), stop=(i == n - 1))
            i += 1
    return last


def constant_tables():
    t = np.arange(P)
    s = t[:, None]
    n_ctx = t[None, :] - s
    n_blk = np.repeat(L * np.arange(NL) - 1, D)[None, :] - s
    p32 = (t // D)[:, None]
    n_out = np.arange(D)[None, :] - L * p32 + 1
    parts = {
        "ident": np.eye(P),
        "lag_mask": (s % L >= np.arange(L)[None, :]) / 16.0,
        "n_lag": np.tile(np.arange(L), (P, 1)),
        "n_ctx": np.maximum(n_ctx, 0), "m_ctx": n_ctx >= 0,
        "n_blk": np.maximum(n_blk, 0), "m_blk": n_blk >= 0,
        "n_out": np.clip(n_out, 0, L), "m_out": (n_out >= 1) & (n_out <= L),
        "expert": np.tile(np.arange(8), (P, 2)),
        "choice": np.tile([0, 8], (P, 1)),
        "token": s,
        "dump": B * P + s,
        "before": s < t[None, :],
    }
    at, cols = {}, 0
    for k, v in parts.items():
        at[k] = (cols, cols + v.shape[1])
        cols += v.shape[1]
    table = np.concatenate([np.asarray(v, np.float32) for v in parts.values()], 1)
    return table, at


def cond_phase(nc, table, x, x_t, tau_ctx, tau, Wg, bg, Wn1, bn1, Wn2, bn2, blend_t, Wsoma, bsoma,
               Wtemp, btemp, Wout, gamma, beta, cond_t):
    _, AT = constant_tables()
    with ExitStack() as ctx, Semaphores(nc) as semaphores:
        def sb(name, shape, dt=F32):
            return ctx.enter_context(nc.sbuf_tensor("c_" + name, shape, dt))

        def sem(name, per=1, step=1):
            return Signal(semaphores.new("c_" + name), per, step)

        bank = [ctx.enter_context(nc.psum_tensor(f"c_bank{i}", [P, 512], F32)) for i in range(8)]

        wg = sb("wg", [P, 2 * CH, 2, E], F16)
        wsoma = sb("wsoma", [P, CH, 2, E], F16)
        wtemp = sb("wtemp", [P, CH, 2, E], F16)
        wout = sb("wout", [P, CH, 2, E], F16)
        wn1 = sb("wn1", [P, CH, 2, P], F16)
        wn2 = sb("wn2", [P, 3, D])
        cst = sb("cst", [P, AT["n_lag"][1]])
        const = lambda k: cst[:, AT[k][0]:AT[k][1]]
        ident = const("ident")
        neg_sp = sb("neg_sp", [P, D + 2])
        sp_tmp = sb("sp_tmp", [P, D + 2])
        decay_ctx = sb("decay_ctx", [P, P])
        decay_blk = sb("decay_blk", [P, NL * D])
        decay_out = sb("decay_out", [P, D])
        decay_lag = sb("decay_lag", [P, L])
        blend_rows = sb("blend_rows", [P, E])
        lag_w = sb("lag_w", [3 * D, L, E], F16)
        bias_cols = sb("bias_cols", [P, 2 * CH + 2])
        bn2_rows = sb("bn2_rows", [P, D])
        bg_halves = sb("bg_halves", [D + 1, E], F16)
        ones_rows = sb("ones_rows", [D + 1, P], F16)
        gamma_rows = sb("gamma_rows", [P, E])
        beta_rows = sb("beta_rows", [P, E])

        xt_in = sb("xt_in", [P, CH, GT])
        x_in = sb("x_in", [P, G, E])
        x_h = sb("x_h", [P, CH, 2, GT], F16)
        ct_h = sb("ct_h", [P, CH, 2, GT], F16)
        h1 = sb("h1", [P, GT])
        modt = sb("modt", [3 * D, GT])
        mod_st = sb("mod_st", [3 * D, G, L + P], F16)
        mod = sb("mod", [P, G * D])
        gate_sig = sb("gate_sig", [P, 2, E])
        gated = sb("gated", [P, G, E])
        shifted = sb("shifted", [P, 2, L - 1, E])
        blk_mod = sb("blk_mod", [P, G, NL * D])
        state_w = sb("state_w", [P, 4, E])
        lagged = sb("lagged", [P, L, E])
        first_col = AT["n_ctx"][0]
        set_up_table = lambda k: lagged[:].rearrange("p l e -> p (l e)")[:, AT[k][0] - first_col:AT[k][1] - first_col]
        temporal = sb("temporal", [P, G, E])
        soma = sb("soma", [P, CH, GT])
        gate2 = sb("gate2", [P, 2, GT])
        prod_f = sb("prod_f", [P, 2, GT])
        prod_h = sb("prod_h", [P, CH, 2, GT], F16)
        stats = sb("stats", [P, G, 6])
        mv = sb("mv", [P, G, 2])
        var_e = sb("var_e", [P, G])
        half_pow = sb("half_pow", [P, 1])
        rstd = sb("rstd", [P, G])
        z = temporal
        z_h = prod_h[:].rearrange("p a h t -> p (a h t)").rearrange("p (b c h t) -> p b c h t", b=G, c=CH, h=2)
        bg_rows = blk_mod[0:D + 1, 1, :]

        cst_in = sem("cst_in")
        vec_in = sem("vec_in")
        w_in = [sem(f"w_in{i}") for i in range(6)]
        w_hi, w_lo = sem("w_hi"), sem("w_lo")
        sp_step = sem("sp_step")
        sp_exp = sem("sp_exp")
        dve_step = sem("dve_step")
        act_step = sem("act_step")
        pe_step = sem("pe_step")
        lag_rows, lag_hi = sem("lag_rows"), sem("lag_hi")
        z0 = sem("z0")
        pieces = [(Wn1, wn1, 0, P), (Wg, wg, 0, E), (Wg, wg, CH, E), (Wsoma, wsoma, 0, E),
                  (Wtemp, wtemp, 0, E), (Wout, wout, 0, E)]
        flat = prod_h[:].bitcast(F32).rearrange("p a h t -> p (a h t)").rearrange("p (c n) -> p c n", c=CH)
        stage = [gate2[:, 0, :].rearrange("p (c n) -> p c n", c=CH), flat, gated[:], temporal[:], soma[:], flat]
        const_loads = (
            (cst[:], table[:, 0:first_col]),
            (lagged[:].rearrange("p l e -> p (l e)")[:, 0:AT["m_out"][1] - first_col], table[:, first_col:AT["m_out"][1]]),
            (neg_sp[:, 0:D], tau.partition_broadcast(P)),
            (neg_sp[:, D:D + 1], tau_ctx.partition_broadcast(P)),
            *((neg_sp[D * q:D * q + D, D + 1:D + 2], tau.rearrange("(d a) -> d a", a=1)) for q in range(4)),
            (gate_sig[:, 0, 0:CH * D], blend_t),
            (bias_cols[:, 2 * CH:2 * CH + 1], bn1.rearrange("(d a) -> d a", a=1)),
            (bg_rows[0:1], bg.rearrange("(a d) -> a d", a=1)),
            (bg_rows[D:D + 1], bg.rearrange("(a d) -> a d", a=1)),
        )
        vector_loads = (
            (bias_cols[:, 0:CH], bsoma), (bias_cols[:, CH:2 * CH], btemp),
            *((bias_cols[D * q:D * q + D, 2 * CH + 1:2 * CH + 2], bn2.rearrange("(d a) -> d a", a=1)) for q in range(4)),
            (bn2_rows[:], bn2.partition_broadcast(P)),
            (gamma_rows[:], gamma.partition_broadcast(P)),
            (beta_rows[:], beta.partition_broadcast(P)),
            *((wn2[:, q, :], Wn2) for q in range(3)),
        )

        def load_piece(sp, i):
            src, _, c0, n = pieces[i]
            sp.dma_start(stage[i][:, :, 0:n], src[:, c0:c0 + CH, :]).then_inc(w_in[i].sem, 16)

        def piece_hi(act, i):
            _, dst, c0, n = pieces[i]
            act.wait_ge(w_in[i].sem, 16)
            act.activation(dst[:, c0:c0 + CH, 0, :], stage[i][:, :, 0:n], ACT.Copy, scale=WS).then_inc(w_hi.sem, 1)

        def piece_lo(dve, i):
            _, dst, c0, n = pieces[i]
            dve.wait_ge(w_hi.sem, i + 1)
            for c in range(CH):
                last = dve.scalar_tensor_tensor(dst[:, c0 + c, 1, :], stage[i][:, c, 0:n], WS, dst[:, c0 + c, 0, :],
                                                ALU.mult, ALU.subtract)
            last.then_inc(w_lo.sem, 1)

        def constants_pool(pool):
            pool.memset(bg_rows, 0.0).then_inc(z0.sem, 1)
            for dst, src in vector_loads:
                pool.dma_start(dst, src).then_inc(vec_in.sem, 16)
            pool.memset(mod_st[:], 0.0).then_inc(z0.sem, 1)
            pool.memset(shifted[:], 0.0).then_inc(z0.sem, 1)
            pool.memset(half_pow[:], -0.5).then_inc(z0.sem, 1)
            pool.memset(ones_rows[:], 1.0).then_inc(z0.sem, 1)
            pool.wait_ge(z0.sem, 5)

        def constants_scalar(act):
            act.wait_ge(cst_in.sem, 16 * len(const_loads))
            act.activation(sp_tmp[:], neg_sp[:], ACT.Abs).then_inc(sp_step.sem, 1)
            act.wait_ge(sp_step.sem, 1)
            act.activation(sp_tmp[:], sp_tmp[:], ACT.Exp, scale=-1.0).then_inc(act_step.sem, 1)
            act.wait_ge(act_step.sem, 1)
            act.activation(sp_tmp[:], sp_tmp[:], ACT.Ln, bias=1.0).then_inc(act_step.sem, 1)
            act.wait_ge(sp_step.sem, 4)
            act.activation(decay_ctx[:], set_up_table("n_ctx"), ACT.Exp, scale=neg_sp[:, D:D + 1]).then_inc(sp_exp.sem, 1)
            act.activation(decay_out[:], set_up_table("n_out"), ACT.Exp, scale=neg_sp[:, D + 1:D + 2]).then_inc(sp_exp.sem, 1)
            act.activation(decay_lag[:], const("n_lag"), ACT.Exp, scale=neg_sp[:, D + 1:D + 2]).then_inc(sp_exp.sem, 1)
            act.activation(decay_blk[:], decay_blk[:], ACT.Exp).then_inc(sp_exp.sem, 1)
            act.wait_ge(dve_step.sem, 2)
            act.activation(gate_sig[:, 0, 0:CH * D], gate_sig[:, 0, 0:CH * D], ACT.Exp).then_inc(act_step.sem, 1)

        def constants_vector(dve):
            dve.wait_ge(cst_in.sem, 16 * len(const_loads))
            dve.wait_ge(sp_step.sem, 1)
            dve.tensor_scalar(neg_sp[:], neg_sp[:], 0.0, -1.0, ALU.max, ALU.mult).then_inc(sp_step.sem, 1)
            dve.wait_ge(act_step.sem, 2)
            dve.wait_ge(sp_step.sem, 2)
            dve.tensor_tensor(neg_sp[:], neg_sp[:], sp_tmp[:], ALU.subtract).then_inc(sp_step.sem, 1)
            dve.wait_ge(sp_step.sem, 3)
            dve.tensor_tensor(decay_blk[:].rearrange("p (k d) -> p k d", d=D),
                              set_up_table("n_blk").rearrange("p (k d) -> p k d", d=D),
                              repeated(neg_sp[:, 0:D], 1, NL),
                              ALU.mult).then_inc(sp_step.sem, 1)
            bl = gate_sig[:, 0, 0:CH * D].rearrange("p (c d) -> p c d", d=D)
            red = stats[:, 0, 0:CH]
            red_b = repeated(red, 2, D)
            dve.tensor_reduce(red, bl, AX_X, ALU.max).then_inc(dve_step.sem, 1)
            dve.wait_ge(dve_step.sem, 1)
            dve.tensor_tensor(bl, bl, red_b, ALU.subtract).then_inc(dve_step.sem, 1)
            dve.wait_ge(act_step.sem, 3)
            dve.tensor_reduce(red, bl, AX_X, ALU.add).then_inc(dve_step.sem, 1)
            dve.wait_ge(dve_step.sem, 3)
            dve.reciprocal(red, red).then_inc(dve_step.sem, 1)
            dve.wait_ge(dve_step.sem, 4)
            bl4 = blk_mod[:, 0, :].rearrange("p (c r d) -> p c r d", c=CH, r=4)
            for r in range(4):
                dve.tensor_tensor(bl4[:, :, r, :], bl, red_b, ALU.mult).then_inc(dve_step.sem, 1)
            dve.wait_ge(sp_exp.sem, 4)
            dve.tensor_tensor(decay_ctx[:], decay_ctx[:], set_up_table("m_ctx"), ALU.mult).then_inc(dve_step.sem, 1)
            dve.tensor_tensor(decay_blk[:], decay_blk[:], set_up_table("m_blk"), ALU.mult).then_inc(dve_step.sem, 1)
            dve.tensor_tensor(decay_out[:], decay_out[:], set_up_table("m_out"), ALU.mult).then_inc(dve_step.sem, 1)
            dve.tensor_scalar(decay_lag[:], decay_lag[:], 16.0, None, ALU.mult).then_inc(dve_step.sem, 1)
            dve.wait_ge(pe_step.sem, 1)
            dve.tensor_copy(blend_rows[:], bank[0][:]).then_inc(dve_step.sem, 1)

        def bias_vector(dve):
            dve.tensor_scalar(bg_rows, bg_rows, WS, None, ALU.mult).then_inc(dve_step.sem, 1)
            dve.wait_ge(dve_step.sem, 14)
            dve.tensor_copy(bg_halves[:], bg_rows).then_inc(dve_step.sem, 1)
            dve.wait_ge(dve_step.sem, 15)
            dve.tensor_tensor(bg_halves[D:D + 1], bg_rows[D:D + 1], bg_halves[D:D + 1], ALU.subtract).then_inc(dve_step.sem, 1)

        lw = lagged[0:3 * D]

        def later_scalar(act):
            piece_hi(act, 3)
            act.wait_ge(vec_in.sem, 16 * len(vector_loads))
            act.wait_ge(dve_step.sem, 13)
            for j in range(L):
                act.activation(lw[:, j, :], blend_rows[0:3 * D, :], ACT.Copy,
                               scale=decay_lag[0:3 * D, j:j + 1]).then_inc(lag_rows.sem, 1)
                act.wait_ge(lag_rows.sem, j + 1)
                act.activation(lag_w[:, j, :], lw[:, j, :], ACT.Copy).then_inc(lag_hi.sem, 1)

        def later_vector(dve):
            piece_lo(dve, 3)
            for j in range(L):
                dve.wait_ge(lag_hi.sem, j + 1)
                dve.tensor_tensor(lag_w[D:2 * D, j, :], lw[D:2 * D, j, :], lag_w[D:2 * D, j, :],
                                  ALU.subtract).then_inc(dve_step.sem, 1)

        def constants_tensor(pe):
            pe.wait_ge(dve_step.sem, 8)
            for c in range(CH):
                last = pe.transpose(bank[0][:, c * P:c * P + P], blk_mod[:, 0, c * P:c * P + P], ident)
            last.then_inc(pe_step.sem, 1)

        xt_load, x_load = sem("xt_load", 1, 16), sem("x_load", 1, 16)
        shift_in = [sem(f"shift_in{i}", 2 * (L - 1), 16) for i in range(2)]
        z_out = sem("z_out", 1, 16)
        ctx_mm, h1_mm, modt_mm, mod_mm = sem("ctx_mm", G), sem("h1_mm"), sem("modt_mm"), sem("mod_mm")
        gate_mm, state_mm, lag_mm, y_mm = sem("gate_mm", G), sem("state_mm", 4 * G), sem("lag_mm", L * G), sem("y_mm", G)
        soma_mm, temp_tr, gate2_mm = sem("soma_mm", CH), sem("temp_tr", G), sem("gate2_mm", CH)
        out_mm, z_tr = sem("out_mm"), sem("z_tr", G)
        x_hi, ctx_hi, h1_done, modt_sig, mod_sig = sem("x_hi"), sem("ctx_hi", G), sem("h1_done"), sem("modt_sig"), sem("mod_sig")
        gate_done, soma_done, temp_hi, gate2_done, z_hi = sem("gate_done", G), sem("soma_done", CH), sem("temp_hi", G), sem("gate2_done", CH), sem("z_hi", G)
        x_lo, ctx_lo, modt_half, modt_hi, modt_lo = sem("x_lo"), sem("ctx_lo", G), sem("modt_half"), sem("modt_hi"), sem("modt_lo")
        mod_pre, gated_done, blk_done = sem("mod_pre"), sem("gated_done", G), sem("blk_done", G)
        state_done, lag_done, temp_done, temp_lo = sem("state_done", 4 * G), sem("lag_done", L * G), sem("temp_done", G), sem("temp_lo", G)
        prod_done, prod_hi, prod_lo = sem("prod_done", CH), sem("prod_hi", CH), sem("prod_lo", CH)
        st_done, mv_done, var_done = sem("st_done", G), sem("mv_done", G), sem("var_done")
        centred, z_done, z_lo = sem("centred", G), sem("z_done", G), sem("z_lo", G)
        tail_done = sem("tail_done", 2)
        sum_done, rstd_done = sem("sum_done", (L - 1) * G - 2), sem("rstd_done")

        CTX_BANK = (5, 2, 3, 4)
        GATE_BANK = (7, 0, 1, 0)
        Z_BANK = (3, 4, 5, 6)
        SOMA_BANK = (0, 0, 0, 5)
        OUT_BANK = (6, 7, 0, 1)

        def cols(b):
            return slice(b * P, b * P + P)

        FIRST, LAST = 0, TRIPS - 1

        def first(g):
            return isinstance(g, int) and g == FIRST

        def final(g):
            return isinstance(g, int) and g == LAST

        def sync_trip(sp, g):
            if first(g):
                for i, (dst, src) in enumerate(const_loads):
                    if i == len(const_loads) - 2:
                        sp.wait_ge(z0.sem, 1)
                    sp.dma_start(dst, src).then_inc(cst_in.sem, 16)
                load_piece(sp, 0)
                sp.dma_start(xt_in[:], x_t[0]).then_inc(xt_load.sem, 16)
                sp.dma_start(x_in[:], x[0]).then_inc(x_load.sem, 16)
                for i in range(1, 5):
                    load_piece(sp, i)
                sp.wait_ge(w_lo.sem, 2)
                load_piece(sp, 5)
            if not final(g):
                wait(sp, x_lo, g, 1)
                sp.dma_start(xt_in[:], x_t[g + 1]).then_inc(xt_load.sem, 16)
            for b in range(G):
                wait(sp, gated_done, g, b + 1)
                for j in range(1, L):
                    sp.dma_start(shifted[j:P, b % 2, j - 1, :], gated[0:P - j, b, :]).then_inc(shift_in[b % 2].sem, 16)
            if not final(g):
                sp.dma_start(x_in[:], x[g + 1]).then_inc(x_load.sem, 16)

        def store_z(sp, g):
            if final(g):
                for b in range(G):
                    wait(sp, z_lo, g, b + 1)
                    sp.dma_start(cond_t[g][:, b], z_h[:, b]).then_inc(z_out.sem, 16)
            else:
                wait(sp, z_lo, g, G)
                sp.dma_start(cond_t[g], z_h).then_inc(z_out.sem, 16)

        def z_transposes(pe, g):
            for b in range(G):
                wait(pe, z_done, g, b + 1)
                for c in range(CH):
                    last = pe.transpose(bank[Z_BANK[b]][:, cols(c)], z[:, b, cols(c)], ident)
                last.then_inc(z_tr.sem, 1)

        def tensor_trip(pe, g, prev):
            def lag_pair(b, i):
                for j in (2 * i, 2 * i + 1):
                    n = L * b + j
                    if n < 2 and prev is not None:
                        wait(pe, z_lo, prev, n + 2)
                    if n >= 2:
                        wait(pe, lag_done, g, n - 1)
                    pe.matmul(bank[4 + j % 2][:], mod_st[:, b, L - j:L - j + P], lag_w[:, j, :],
                              start=True, stop=True).then_inc(lag_mm.sem, 1)

            def outputs(b, i):
                n = 4 * b + i
                wait(pe, state_done, g, n + 1)
                mm = pe.matmul(bank[6 + b % 2][D * i:D * i + D, :], decay_out[:], state_w[:, i, :],
                               start=True, stop=True)
                if i == 3:
                    mm.then_inc(y_mm.sem, 1)

            if first(g):
                constants_tensor(pe)
                pe.wait_ge(w_lo.sem, 1)
            wait(pe, x_lo, g, 1)
            wait(pe, x_hi, g, 1)
            wait(pe, lag_done, g)
            three_passes(pe, bank[4][:], [(lambda h, c=c: wn1[:, c, h, :], lambda h, c=c: x_h[:, c, h, :])
                                          for c in range(CH)]).then_inc(h1_mm.sem, 1)
            wait(pe, x_load, g, 1)
            for b in range(G):
                if b == 0:
                    wait(pe, soma_done, g)
                elif b < 3:
                    if prev is not None:
                        wait(pe, gate2_done, prev, b + 2)
                else:
                    wait(pe, h1_done, g, 1)
                for c in range(CH):
                    last = pe.matmul(bank[CTX_BANK[b]][:, cols(c)], x_in[:, b, cols(c)], decay_ctx[:], start=True, stop=True)
                last.then_inc(ctx_mm.sem, 1)

            def gate(b, quarters=range(4)):
                k = GATE_BANK[b]
                for quarter in quarters:
                    if quarter == 0:
                        if b == 0:
                            wait(pe, centred, g)
                        elif b == 3:
                            wait(pe, gate_done, g, 2)
                        if first(g) and b == 0:
                            pe.wait_ge(w_lo.sem, 3)
                            pe.wait_ge(dve_step.sem, 16)
                            pe.wait_ge(z0.sem, 5)
                        pe.matmul(bank[k][:], ones_rows[:], bg_halves[:], start=True, stop=False)
                    if quarter == 2:
                        wait(pe, ctx_lo, g, b + 1)
                    for c in (2 * quarter, 2 * quarter + 1):
                        act_in = x_h if c < CH else ct_h
                        for a, w in PASSES:
                            last = pe.matmul(bank[k][:], act_in[:, c % CH, a, cols(b)], wg[:, c, w, :],
                                             start=False, stop=(c == 2 * CH - 1 and (a, w) == PASSES[-1]))
                    if quarter == 3:
                        last.then_inc(gate_mm.sem, 1)

            gate(0)
            wait(pe, h1_done, g, 1)
            if first(g):
                pe.wait_ge(vec_in.sem, 16 * len(vector_loads))
            wait(pe, ctx_lo, g, 1)
            pe.matmul(bank[5][0:3 * D, :], wn2[:].rearrange("p a d -> p (a d)"), h1[:],
                      start=True, stop=True).then_inc(modt_mm.sem, 1)
            for b in range(G):
                last = pe.matmul(bank[6][:, D * b:D * b + D], h1[:, cols(b)], wn2[:, 0, :], start=True, stop=True)
            last.then_inc(mod_mm.sem, 1)
            gate(1)
            gate(2)
            if prev is not None:
                wait(pe, ctx_lo, g, 4)
                wait(pe, modt_sig, g, 1)
                wait(pe, mod_pre, g, 1)
                z_transposes(pe, prev)

            def soma_chunk(e, chunks=range(CH)):
                for c in chunks:
                    if c == 0:
                        if e == 0 and first(g):
                            pe.wait_ge(w_lo.sem, 4)
                        if e == 0:
                            wait(pe, gate_done, g, G)
                        elif e < 3:
                            wait(pe, soma_done, g, e)
                        else:
                            wait(pe, lag_done, g, L * G)
                    for a, w in PASSES:
                        last = pe.matmul(bank[SOMA_BANK[e]][:], wsoma[:, c, a, cols(e)], x_h[:, c, w, :],
                                         start=(c == 0 and (a, w) == PASSES[0]), stop=(c == CH - 1 and (a, w) == PASSES[-1]))
                    if c == CH - 1:
                        last.then_inc(soma_mm.sem, 1)

            def between(b, i):
                part = ((0, 1), (2,), (3,), ())[i]
                if b == 0:
                    gate(3, part)
                elif b < 3:
                    soma_chunk(b - 1, part)

            wait(pe, modt_lo, g, 1)
            if first(g):
                pe.wait_ge(dve_step.sem, 16 + L)
            for b in range(G):
                for i in range(4):
                    n = 4 * b + i
                    if i == 0:
                        wait(pe, blk_done, g, b + 1)
                        wait(pe, gated_done, g, b + 1)
                    if n == 0:
                        wait(pe, ctx_lo, g, 2)
                        wait(pe, modt_sig, g, 1)
                    if n == 1:
                        if prev is not None:
                            wait(pe, z_lo, prev, 1)
                        else:
                            wait(pe, ctx_lo, g, G)
                    if n >= 2:
                        wait(pe, state_done, g, n - 1)
                    pe.matmul(bank[2 + i % 2][:], blk_mod[:, b, P * i:P * i + P], gated[:, b, :],
                              start=True, stop=True).then_inc(state_mm.sem, 1)
                    if i == 0 and b >= 1:
                        outputs(b - 1, 3)
                    between(b, i)
                    lag_pair(b, i)
                    if i == 1:
                        if b == 0:
                            if prev is not None:
                                wait(pe, z_lo, prev, G)
                            else:
                                wait(pe, mod_pre, g, 1)
                        elif b == 1:
                            wait(pe, gate_done, g, 1)
                        else:
                            wait(pe, temp_done, g, b - 1)
                    if i >= 1:
                        outputs(b, i - 1)
                if b >= 1:
                    temporal_transpose(pe, g, b - 1)
            outputs(G - 1, 3)
            soma_chunk(2)
            temporal_transpose(pe, g, G - 1)
            soma_chunk(3)

            if first(g):
                pe.wait_ge(w_lo.sem, 5)

            def gate2_chunk(e):
                if e >= 2:
                    wait(pe, gate2_done, g, e - 1)
                else:
                    wait(pe, state_done, g, 4 * G)
                three_passes(pe, bank[2 + e % 2][:], [(lambda h, c=c: wtemp[:, c, h, cols(e)], lambda h, c=c: ct_h[:, c, h, :])
                                                      for c in range(CH)]).then_inc(gate2_mm.sem, 1)

            def out_chunk(e):
                wait(pe, prod_lo, g, e + 1)
                if e == 0 and first(g):
                    pe.wait_ge(w_lo.sem, 6)
                for b in range(G):
                    k = OUT_BANK[b]
                    if e == 0:
                        if b < 2:
                            wait(pe, temp_done, g, G)
                        elif b == 2:
                            wait(pe, soma_done, g, CH)
                        else:
                            wait(pe, temp_lo, g, G)
                    for i, (a, w) in enumerate(PASSES):
                        last = pe.matmul(bank[k][:], prod_h[:, e, a, cols(b)], wout[:, e, w, :],
                                         start=(e == 0 and i == 0), stop=(e == CH - 1 and i == 2))
                if e == CH - 1:
                    last.then_inc(out_mm.sem, 1)

            wait(pe, temp_hi, g, G)
            wait(pe, temp_lo, g, G)
            gate2_chunk(0)
            gate2_chunk(1)
            out_chunk(0)
            gate2_chunk(2)
            out_chunk(1)
            gate2_chunk(3)
            out_chunk(2)
            out_chunk(3)

        def temporal_transpose(pe, g, b):
            wait(pe, temp_done, g, b + 1)
            if b == 0:
                wait(pe, gate_done, g, 3)
            else:
                wait(pe, temp_lo, g, b)
            for c in range(CH):
                last = pe.transpose(bank[1][:, cols(c)], temporal[:, b, cols(c)], ident)
            last.then_inc(temp_tr.sem, 1)

        def scalar_z(act, g):
            for b in range(G):
                wait(act, z_tr, g, b + 1)
                act.activation(z_h[:, b, :, 0, :], bank[Z_BANK[b]][:].rearrange("p (c t) -> p c t", c=CH),
                               ACT.Copy).then_inc(z_hi.sem, 1)

        def scalar_x(act, g):
            wait(act, xt_load, g, 1)
            wait(act, soma_mm, g)
            act.activation(x_h[:, :, 0, :], xt_in[:], ACT.Copy).then_inc(x_hi.sem, 1)

        def scalar_trip(act, g, prev):
            if first(g):
                constants_scalar(act)
                piece_hi(act, 0)
                scalar_x(act, 0)
                piece_hi(act, 1)
                piece_hi(act, 2)
            wait(act, h1_mm, g, 1)
            wait(act, mod_mm, g)
            act.activation(h1[:], bank[4][:], ACT.Gelu, bias=bias_cols[:, 2 * CH:2 * CH + 1],
                           scale=1.0 / WS).then_inc(h1_done.sem, 1)
            wait(act, gate2_mm, g)
            for b in range(G):
                wait(act, ctx_mm, g, b + 1)
                act.activation(ct_h[:, :, 0, cols(b)], bank[CTX_BANK[b]][:].rearrange("p (c t) -> p c t", c=CH),
                               ACT.Copy).then_inc(ctx_hi.sem, 1)
            if first(g):
                later_scalar(act)
            wait(act, gated_done, g)
            for b in range(G):
                wait(act, gate_mm, g, b + 1)
                if b >= 2:
                    wait(act, gated_done, g, b - 1)
                act.activation(gate_sig[:, b % 2, :], bank[GATE_BANK[b]][:], ACT.Sigmoid,
                               scale=1.0 / WS).then_inc(gate_done.sem, 1)
                if b == 2 and prev is not None:
                    scalar_z(act, prev)
                elif b == 2:
                    piece_hi(act, 4)
                    piece_hi(act, 5)
                if b == 0:
                    wait(act, modt_mm, g, 1)
                    wait(act, modt_lo, g)
                    act.activation(modt[:], bank[5][0:3 * D, :], ACT.Sigmoid,
                                   bias=bias_cols[0:3 * D, 2 * CH + 1:2 * CH + 2]).then_inc(modt_sig.sem, 1)
                    wait(act, mod_pre, g, 1)
                    act.activation(mod[:], mod[:], ACT.Sigmoid).then_inc(mod_sig.sem, 1)
            def scalar_soma(e):
                wait(act, soma_mm, g, e + 1)
                if e == 0:
                    wait(act, prod_done, g)
                act.activation(soma[:, e, :], bank[SOMA_BANK[e]][:], ACT.Gelu, bias=bias_cols[:, e:e + 1],
                               scale=1.0 / WS).then_inc(soma_done.sem, 1)

            scalar_soma(0)
            scalar_temporal(act, g, 0)
            scalar_soma(1)
            scalar_temporal(act, g, 1)
            scalar_temporal(act, g, 2)
            scalar_soma(2)
            scalar_temporal(act, g, 3)
            scalar_soma(3)
            for e in range(CH):
                wait(act, gate2_mm, g, e + 1)
                if e >= 2:
                    wait(act, prod_done, g, e - 1)
                act.activation(gate2[:, e % 2, :], bank[2 + e % 2][:], ACT.Sigmoid,
                               bias=bias_cols[:, CH + e:CH + e + 1], scale=1.0 / WS).then_inc(gate2_done.sem, 1)
                if e == 1 and not final(g):
                    scalar_x(act, g + 1)

        def scalar_temporal(act, g, b):
            wait(act, temp_tr, g, b + 1)
            act.activation(ct_h[:, :, 0, cols(b)], bank[1][:].rearrange("p (c t) -> p c t", c=CH),
                           ACT.Copy).then_inc(temp_hi.sem, 1)

        def vector_z(dve, g):
            for b in range(G):
                wait(dve, z_hi, g, b + 1)
                dve.tensor_tensor(z_h[:, b, :, 1, :], bank[Z_BANK[b]][:].rearrange("p (c t) -> p c t", c=CH),
                                  z_h[:, b, :, 0, :], ALU.subtract).then_inc(z_lo.sem, 1)

        def vector_x(dve, g):
            wait(dve, x_hi, g, 1)
            dve.tensor_tensor(x_h[:, :, 1, :], xt_in[:], x_h[:, :, 0, :], ALU.subtract).then_inc(x_lo.sem, 1)

        def vector_norm(dve, g):
            wait(dve, rstd_done, g, 1)
            for b in range(G):
                wait(dve, centred, g, b + 1)
                dve.scalar_tensor_tensor(z[:, b, :], z[:, b, :], rstd[:, b:b + 1], beta_rows[:],
                                         ALU.mult, ALU.add).then_inc(z_done.sem, 1)

        def vector_trip(dve, g, prev):
            if first(g):
                constants_vector(dve)
                piece_lo(dve, 0)
                vector_x(dve, 0)
                piece_lo(dve, 1)
                piece_lo(dve, 2)
                bias_vector(dve)
            for b in range(G):
                wait(dve, ctx_hi, g, b + 1)
                dve.tensor_tensor(ct_h[:, :, 1, cols(b)], bank[CTX_BANK[b]][:].rearrange("p (c t) -> p c t", c=CH),
                                  ct_h[:, :, 0, cols(b)], ALU.subtract).then_inc(ctx_lo.sem, 1)
            if prev is not None:
                vector_norm(dve, prev)
            else:
                dve.wait_ge(vec_in.sem, 16 * len(vector_loads))
                dve.wait_ge(z0.sem, 5)
                later_vector(dve)
            wait(dve, mod_mm, g, 1)
            wait(dve, blk_done, g)
            dve.tensor_tensor(mod[:].rearrange("p (b d) -> p b d", d=D),
                              bank[6][:, 0:G * D].rearrange("p (b d) -> p b d", d=D),
                              repeated(bn2_rows[:], 1, G), ALU.add).then_inc(mod_pre.sem, 1)
            wait(dve, modt_sig, g, 1)
            dve.tensor_scalar(modt[:], modt[:], 0.5, None, ALU.add).then_inc(modt_half.sem, 1)
            wait(dve, modt_half, g, 1)
            wait(dve, lag_mm, g)
            m4 = modt[:].rearrange("p (b t) -> p b t", b=G)
            dve.tensor_copy(mod_st[:, :, L:L + P], m4).then_inc(modt_hi.sem, 1)
            wait(dve, modt_hi, g, 1)
            dve.tensor_tensor(mod_st[2 * D:3 * D, :, L:L + P], m4[2 * D:3 * D], mod_st[2 * D:3 * D, :, L:L + P],
                              ALU.subtract).then_inc(modt_lo.sem, 1)
            wait(dve, x_load, g, 1)

            def apply_gate(b):
                if b == 0:
                    wait(dve, state_mm, g)
                    wait(dve, shift_in[0], g)
                    wait(dve, shift_in[1], g)
                    wait(dve, lag_done, g)
                wait(dve, gate_done, g, b + 1)
                dve.tensor_tensor(gated[:, b, :], x_in[:, b, :], gate_sig[:, b % 2, :], ALU.mult).then_inc(gated_done.sem, 1)

            def decay_block(b):
                dve.scalar_tensor_tensor(blk_mod[:, b, :].rearrange("p (k d) -> p k d", d=D),
                                         repeated(mod[:, D * b:D * b + D], 1, NL), 0.5,
                                         decay_blk[:].rearrange("p (k d) -> p k d", d=D),
                                         ALU.add, ALU.mult).then_inc(blk_done.sem, 1)

            apply_gate(0)
            wait(dve, mod_sig, g, 1)
            decay_block(0)
            apply_gate(1)
            for b in range(1, G):
                decay_block(b)
            if prev is not None:
                vector_z(dve, prev)
            def temporal_sum(b):
                wait(dve, sum_done, g, (L - 1) * (b + 1))
                wait(dve, y_mm, g, b + 1)
                dve.tensor_tensor(temporal[:, b, :], bank[6 + b % 2][:], temporal[:, b, :], ALU.add).then_inc(temp_done.sem, 1)

            for b in range(G):
                if b >= 1 and b + 1 < G:
                    apply_gate(b + 1)
                if b >= 2:
                    vector_temporal(dve, g, b - 2)
                for i in range(4):
                    n = 4 * b + i
                    wait(dve, state_mm, g, n + 1)
                    if n >= 4:
                        wait(dve, y_mm, g, b)
                    elif n == 0:
                        wait(dve, y_mm, g)
                    dve.tensor_tensor(state_w[:, i, :], bank[2 + i % 2][:], blend_rows[:], ALU.mult).then_inc(state_done.sem, 1)
                    for j in (2 * i, 2 * i + 1):
                        n = L * b + j
                        wait(dve, lag_mm, g, n + 1)
                        if j == 0:
                            wait(dve, gated_done, g, b + 1)
                        if j == 1:
                            wait(dve, shift_in[b % 2], g, (L - 1) * (b // 2 + 1))
                        if b == 0:
                            if j == 0:
                                wait(dve, sum_done, g)
                                wait(dve, temp_done, g)
                        else:
                            wait(dve, sum_done, g, (L - 1) * (b - 1) + max(j, 1))
                        src = gated[:, b, :] if j == 0 else shifted[:, b % 2, j - 1, :]
                        dve.scalar_tensor_tensor(lagged[:, j, :], bank[4 + j % 2][:], const("lag_mask")[:, j:j + 1],
                                                 src, ALU.mult, ALU.mult).then_inc(lag_done.sem, 1)
                    if i == 1 and b >= 1:
                        temporal_sum(b - 1)
                if b == 0 and first(g):
                    piece_lo(dve, 4)
            vector_temporal(dve, g, G - 2)
            wait(dve, lag_done, g, L * G)
            dve.tensor_tensor(lagged[:, 6, :], lagged[:, 6, :], lagged[:, 7, :], ALU.add).then_inc(tail_done.sem, 1)
            wait(dve, tail_done, g, 1)
            wait(dve, y_mm, g, G)
            dve.tensor_tensor(lagged[:, 6, :], bank[7][:], lagged[:, 6, :], ALU.add).then_inc(tail_done.sem, 1)
            wait(dve, tail_done, g, 2)
            wait(dve, sum_done, g + 1)
            dve.tensor_tensor(temporal[:, G - 1, :], temporal[:, G - 1, :], lagged[:, 6, :], ALU.add).then_inc(temp_done.sem, 1)
            vector_temporal(dve, g, G - 1)
            if first(g):
                piece_lo(dve, 5)
            for e in range(CH):
                wait(dve, gate2_done, g, e + 1)
                wait(dve, soma_done, g, e + 1)
                dve.tensor_tensor(prod_f[:, e % 2, :], soma[:, e, :], gate2[:, e % 2, :], ALU.mult).then_inc(prod_done.sem, 1)
                wait(dve, prod_done, g, e + 1)
                if e == 0:
                    wait(dve, z_out, g)
                dve.tensor_copy(prod_h[:, e, 0, :], prod_f[:, e % 2, :]).then_inc(prod_hi.sem, 1)
                wait(dve, prod_hi, g, e + 1)
                dve.tensor_tensor(prod_h[:, e, 1, :], prod_f[:, e % 2, :], prod_h[:, e, 0, :],
                                  ALU.subtract).then_inc(prod_lo.sem, 1)
                if e == 1 and not final(g):
                    vector_x(dve, g + 1)
            wait(dve, out_mm, g, 1)
            for b in range(G):
                k = OUT_BANK[b]
                dve.bn_stats(stats[:, b, :], bank[k][:]).then_inc(st_done.sem, 1)
            wait(dve, st_done, g, G)
            dve.memset(var_e[:], 0.0)
            for b in range(G):
                dve.bn_aggr(mv[:, b, :], stats[:, b, :]).then_inc(mv_done.sem, 1)
            wait(dve, mv_done, g, G)
            dve.tensor_scalar(var_e[:], mv[:, :, 1], 1e-5 * WS * WS, None, ALU.add).then_inc(var_done.sem, 1)
            for b in range(G):
                k = OUT_BANK[b]
                dve.scalar_tensor_tensor(z[:, b, :], bank[k][:], mv[:, b, 0:1], gamma_rows[:],
                                         ALU.subtract, ALU.mult).then_inc(centred.sem, 1)

        def vector_temporal(dve, g, b):
            wait(dve, temp_hi, g, b + 1)
            dve.tensor_tensor(ct_h[:, :, 1, cols(b)], bank[1][:].rearrange("p (c t) -> p c t", c=CH),
                              ct_h[:, :, 0, cols(b)], ALU.subtract).then_inc(temp_lo.sem, 1)

        def pool_trip(pool, g):
            wait(pool, z_tr, g)
            for b in range(G):
                for j in range(1, L if b < G - 1 else L - 2):
                    wait(pool, lag_done, g, L * b + j + 1)
                    if j > 1:
                        wait(pool, sum_done, g, (L - 1) * b + j - 1)
                    pool.tensor_tensor(temporal[:, b, :], lagged[:, 0, :] if j == 1 else temporal[:, b, :],
                                       lagged[:, j, :], ALU.add).then_inc(sum_done.sem, 1)
            wait(pool, var_done, g, 1)
            pool.tensor_tensor(rstd[:], var_e[:], half_pow[:].broadcast_to([P, G]), ALU.pow).then_inc(rstd_done.sem, 1)

        with nc.Block() as block:
            @block.sync
            def _(sp):
                sync_trip(sp, FIRST)
                with sp.Fori(1, LAST) as g:
                    sync_trip(sp, g)
                    store_z(sp, g - 1)
                sync_trip(sp, LAST)
                store_z(sp, LAST - 1)
                store_z(sp, LAST)
                wait(sp, z_out, LAST, G)

            @block.tensor
            def _(pe):
                tensor_trip(pe, FIRST, None)
                with pe.Fori(1, LAST) as g:
                    tensor_trip(pe, g, g - 1)
                tensor_trip(pe, LAST, LAST - 1)
                z_transposes(pe, TRIPS - 1)

            @block.scalar
            def _(act):
                scalar_trip(act, FIRST, None)
                with act.Fori(1, LAST) as g:
                    scalar_trip(act, g, g - 1)
                scalar_trip(act, LAST, LAST - 1)
                scalar_z(act, TRIPS - 1)

            @block.vector
            def _(dve):
                vector_trip(dve, FIRST, None)
                with dve.Fori(1, LAST) as g:
                    vector_trip(dve, g, g - 1)
                vector_trip(dve, LAST, LAST - 1)
                vector_norm(dve, LAST)
                vector_z(dve, LAST)

            @block.gpsimd
            def _(pool):
                constants_pool(pool)
                pool_trip(pool, 0)
                with pool.Fori(1, TRIPS) as g:
                    pool_trip(pool, g)


def attention_phase(nc, table, cond_t, x, WqT, WkT, RF, Wv, Wo, b_out, ffn_bias, lang, A1, A2, rows3,
                    router, out, tokens, slots):
    _, AT = constant_tables()
    HP = 8
    HD = P * HP
    with ExitStack() as ctx, Semaphores(nc) as semaphores:
        def sb(name, shape, dt=F32):
            return ctx.enter_context(nc.sbuf_tensor("a_" + name, shape, dt))

        def sem(name, per=1, step=1):
            return Signal(semaphores.new("a_" + name), per, step)

        bank = [ctx.enter_context(nc.psum_tensor(f"a_bank{i}", [P, 512], F32)) for i in range(8)]

        wq = sb("wq", [P, CH, 2, HD], F16)
        wk = sb("wk", [P, CH, 2, HD], F16)
        wv = sb("wv", [P, CH, 2, HD], F16)
        wo = sb("wo", [P, HP, 2, E], F16)
        wr = sb("wr", [P, CH, 8])
        cst = sb("cst", [P, P + 20])
        ident = cst[:, 0:P]
        expert, choice = cst[:, P:P + 16], cst[:, P + 16:P + 18]
        cur_token, dump = cst[:, P + 18:P + 19], cst[:, P + 19:P + 20]
        before = sb("before", [P, P], F16)
        ones = sb("ones", [P, P], F16)
        b_out_rows = sb("b_out_rows", [P, E])
        bias_rows = sb("bias_rows", [P, E])
        half_pow = sb("half_pow", [P, 1])
        lang_i = sb("lang_i", [P, B], I32)
        lang_rows = sb("lang_rows", [P, B], I32)
        ct = sb("ct", [P, G, CH, 2, P], F16)
        phq = sb("phq", [P, HP, 2, GT], F16)
        phk = sb("phk", [P, 2, 2, HD], F16)
        v_h = sb("v_h", [P, 2, 2, 16, 65], F16)
        kv = sb("kv", [P, 2, 2, 16, 66], F16)
        nrm = sb("nrm", [P, 2, 16])
        o = sb("o", [P, 2, HD])
        ot = sb("ot", [P, 2, HP, 2, P], F16)
        xr = sb("xr", [P, G, E])
        r = sb("r", [P, 2, E])
        xo = sb("xo", [P, 2, E])
        x1t = sb("x1t", [P, CH, 2, P], F16)
        aw_raw = sb("aw_raw", [P, E + E + 1])
        aw1 = sb("aw1", [P, CH, 2, P], F16)
        aw2 = sb("aw2", [P, 2, E], F16)
        b1 = sb("b1", [P, 2])
        arow = sb("arow", [P, 2, 3 * E])
        hf = sb("hf", [P, P])
        ht = sb("ht", [P, 2, P], F16)
        y = sb("y", [P, 2, E])
        yt = sb("yt", [P, E])
        stats, mv, var_e, rstd = sb("stats", [P, 6]), sb("mv", [P, 2]), sb("var_e", [P, 1]), sb("rstd", [P, 1])
        small = sb("small", [P, 96])
        scratch = small[:, 88:89]
        neg_max, total, inv = small[:, 0:1], small[:, 1:2], small[:, 2:3]
        ex, top = small[:, 8:16], small[:, 16:24]
        index_f, hit, pos, place_f = small[:, 24:26], small[:, 32:48], small[:, 48:50], small[:, 50:52]
        hit_n = small[:, 56:72]
        index_u = sb("index_u", [P, 8], U32)
        hit_h = sb("hit_h", [P, 16], F16)
        seen = sb("seen", [P, 16], F16)
        place_u = sb("place_u", [P, 2, 2], U32)
        entry = sb("entry", [P, 2, 2, 2], I32)
        pool_dummy = sb("pool_dummy", [P, 2])
        row_now, zero_i = sb("row_now", [P, 2], I32), sb("zero_i", [P, 1], I32)

        in_a, in_b, z0 = sem("in_a"), sem("in_b"), sem("z0")
        fold_mm, fold_hi, fold_lo, pre, tab_out = sem("fold_mm"), sem("fold_hi"), sem("fold_lo"), sem("pre"), sem("tab_out")
        rf_bd = y[:].rearrange("p a e -> p (a e)").rearrange("p (h c) -> p h c", h=HP)
        dump_rows = r[:, 0, 0:P].bitcast(I32)
        before_f = r[:, 1, 0:P]
        zero_rows = xo[:, 0, :]

        def stage_of(flat):
            return flat[:, 0:4 * E].rearrange("p (c n) -> p c n", c=4)

        phq_flat = phq[:].bitcast(F32).rearrange("p a h t -> p (a h t)")
        o_flat = o[:].rearrange("p a n -> p (a n)")
        ot_flat = ot[:].bitcast(F32).rearrange("p a h b t -> p (a h b t)")
        arow_flat = arow[:].rearrange("p a e -> p (a e)")
        kv_flat = kv[:].bitcast(F32).rearrange("p a h n c -> p (a h n c)")
        pieces = [(WkT, wk, 0, phq_flat), (WkT, wk, 4, phq_flat[:, 4 * E:8 * E]), (WqT, wq, 0, o_flat),
                  (Wv, wv, 0, arow_flat), (WqT, wq, 4, ot_flat), (Wv, wv, 1, kv_flat),
                  (Wo, wo, 0, o_flat), (Wo, wo, 1, ot_flat)]
        folds = [0, 1, 2, 4]
        wt_in = [sem(f"wt_in{i}") for i in range(8)]
        loads_a = (
            (cst[:, P:P + 20], table[:, AT["expert"][0]:AT["dump"][1]]),
            (ident, table[:, AT["ident"][0]:AT["ident"][1]]),
            (before_f, table[:, AT["before"][0]:AT["before"][1]]),
            (lang_i[:], lang.partition_broadcast(P)),
        )
        loads_b = (
            (wr[:], router), (b_out_rows[:], b_out.partition_broadcast(P)),
            (bias_rows[:], ffn_bias.partition_broadcast(P)),
        )
        rf_loads = ((rf_bd[0:64, :, 0:64], RF[:, 0:HP, :]), (rf_bd[64:P, :, 64:P], RF[:, HP:2 * HP, :]))
        rf_in = sem("rf_in")

        def load_piece(sp, i):
            src, _, p0, flat = pieces[i]
            if src is Wv:
                piece = src[:, 2 * p0:2 * p0 + 2, :].rearrange("p c (a n) -> p (c a) n", a=2)
            elif src is Wo:
                piece = src[:, 4 * p0:4 * p0 + 4, :]
            else:
                piece = src[:, p0:p0 + 4, :]
            sp.dma_start(stage_of(flat), piece).then_inc(wt_in[i].sem, 16)

        def fold(pe):
            pe.wait_ge(rf_in.sem, 32)
            n = 0
            for i in folds:
                pe.wait_ge(wt_in[i].sem, 16)
                for c in range(CH):
                    if n >= 8:
                        pe.wait_ge(fold_lo.sem, CH * folds[n // 4 - 2] + c + 1)
                    for q in range(4):
                        last = pe.matmul(bank[n % 8][:, q * P:q * P + P], stage_of(pieces[i][3])[:, q, c * P:c * P + P],
                                         rf_bd[:, pieces[i][2] + q, :], start=True, stop=True)
                    last.then_inc(fold_mm.sem, 1)
                    n += 1

        def dst_of(i, c, h):
            _, dst, p0, _ = pieces[i]
            if i in folds:
                return dst[:, c, h, p0 * P:p0 * P + 512]
            if dst is wv:
                return dst[:, 2 * p0 + c // 2, h, (c % 2) * 512:(c % 2) * 512 + 512]
            return dst[:, 4 * p0 + c, h, :]

        def src_of(i, c):
            return bank[(CH * folds.index(i) + c) % 8][:] if i in folds else stage_of(pieces[i][3])[:, c, :]

        def piece_hi(act, i, chunks=range(CH)):
            for c in chunks:
                if i in folds:
                    act.wait_ge(fold_mm.sem, CH * folds.index(i) + c + 1)
                elif c == 0:
                    act.wait_ge(wt_in[i].sem, 16)
                act.activation(dst_of(i, c, 0), src_of(i, c), ACT.Copy, scale=QS).then_inc(fold_hi.sem, 1)

        def piece_lo(dve, i, chunks=range(CH)):
            for c in chunks:
                dve.wait_ge(fold_hi.sem, CH * i + c + 1)
                dve.scalar_tensor_tensor(dst_of(i, c, 1), src_of(i, c), QS, dst_of(i, c, 0),
                                         ALU.mult, ALU.subtract).then_inc(fold_lo.sem, 1)

        def setup_sync(sp):
            sp.wait_ge(z0.sem, 1)
            for dst, src in rf_loads:
                sp.dma_start(dst, src).then_inc(rf_in.sem, 16)
            load_piece(sp, 0)
            for dst, src in loads_a:
                sp.dma_start(dst, src).then_inc(in_a.sem, 16)
            for i in range(1, 6):
                load_piece(sp, i)

        def setup_sync_later(sp):
            for i in (6, 7):
                sp.wait_ge(fold_mm.sem, CH * (i - 3))
                load_piece(sp, i)
            sp.wait_ge(pre.sem, 1)
            sp.dma_start(slots.rearrange("(p j) e -> p j e", p=P),
                         dump_rows.rearrange("p (j e) -> p j e", e=2)).then_inc(tab_out.sem, 16)
            sp.wait_ge(z0.sem, 10)
            sp.dma_start(tokens[B * P:(B + 1) * P, :], zero_rows).then_inc(tab_out.sem, 16)

        def setup_pool(pool):
            pool.memset(rf_bd, 0.0).then_inc(z0.sem, 1)
            for dst, src in loads_b:
                pool.dma_start(dst, src).then_inc(in_b.sem, 16)
            pool.memset(dump_rows, 0).then_inc(z0.sem, 1)
            pool.memset(v_h[:, :, 0], 1.0).then_inc(z0.sem, 1)
            pool.memset(v_h[:, :, 1], 0.0).then_inc(z0.sem, 1)
            pool.memset(zero_rows, 0.0).then_inc(z0.sem, 1)
            pool.memset(ones[:], 1.0).then_inc(z0.sem, 1)
            pool.memset(seen[:], 0.0).then_inc(z0.sem, 1)
            pool.memset(half_pow[:], -0.5).then_inc(z0.sem, 1)
            pool.memset(pool_dummy[:], 0.0).then_inc(z0.sem, 1)
            pool.memset(zero_i[:], 0).then_inc(z0.sem, 1)
            pool.wait_ge(fold_lo.sem, 24)
            pool.memset(kv[:], 0.0).then_inc(z0.sem, 1)

        def setup_scalar(act):
            for i in range(6):
                piece_hi(act, i)
            act.wait_ge(z0.sem, 4)

        def setup_vector(dve):
            dve.wait_ge(in_a.sem, 16 * len(loads_a))
            dve.wait_ge(z0.sem, 2)
            dve.tensor_copy(dump_rows.rearrange("p (j e) -> p j e", e=2)[:, :, 0], dump.broadcast_to([P, 64])).then_inc(pre.sem, 1)
            dve.tensor_copy(before[:], before_f).then_inc(pre.sem, 1)
            dve.tensor_copy(aw_raw[:, 0:B], lang_i[:]).then_inc(pre.sem, 1)
            dve.wait_ge(pre.sem, 3)
            dve.scalar_tensor_tensor(aw_raw[:, 0:B], aw_raw[:, 0:B], float(P), cur_token.broadcast_to([P, B]),
                                     ALU.mult, ALU.add).then_inc(pre.sem, 1)
            dve.wait_ge(pre.sem, 4)
            dve.tensor_copy(lang_rows[:], aw_raw[:, 0:B]).then_inc(pre.sem, 1)
            for i in range(6):
                piece_lo(dve, i)

        def all_set(eng):
            eng.wait_ge(fold_lo.sem, 32)
            eng.wait_ge(z0.sem, 11)
            eng.wait_ge(pre.sem, 5)
            eng.wait_ge(in_b.sem, 16 * len(loads_b))
            eng.wait_ge(tab_out.sem, 32)

        ct_in, x_in = ([sem(f"{k}{i}", 1, 16) for i in range(G)] for k in ("ct_in", "x_in"))
        sum_out, tok_out = ([sem(f"{k}{i}", G // 2, 16) for i in range(2)] for k in ("sum_out", "tok_out"))
        slot_out = [sem(f"slot_out{i}", G, 16) for i in range(2)]
        aw_in, arow_in = sem("aw_in", 2 * G, 16), [sem(f"arow_in{i}", G // 2, 16) for i in range(2)]
        q_mm, k_mm, v_mm = sem("q_mm", HP), sem("k_mm", 2 * G), sem("v_mm", 2 * G)
        kv_mm, o_mm, o_tr, att_mm = sem("kv_mm", G), sem("o_mm", G), sem("o_tr", G), sem("att_mm", G)
        x1_tr, h_mm, ad_mm, y_tr, route_mm, count_mm = (sem(k, G) for k in ("x1_tr", "h_mm", "ad_mm", "y_tr", "route_mm", "count_mm"))
        q_hi, k_hi, v_hi, kv_hi, o_hi = sem("q_hi", HP), sem("k_hi", 2 * G), sem("v_hi", 2 * G), sem("kv_hi", 6 * G), sem("o_hi", 2 * G)
        x1_hi, h_done, y_copied, exp_done, aw_hi = (sem(k, G) for k in ("x1_hi", "h_done", "y_copied", "exp_done", "aw_hi"))
        q_lo, k_lo, v_lo, kv_lo, o_lo = sem("q_lo", HP), sem("k_lo", 2 * G), sem("v_lo", 2 * G), sem("kv_lo", 6 * G), sem("o_lo", 2 * G)
        nrm_add, nrm_inv, o_done, x1_done, x1_lo, h_hi, h_lo = (sem(k, G) for k in ("nrm_add", "nrm_inv", "o_done", "x1_done", "x1_lo", "h_hi", "h_lo"))
        s_done, st_done, mv_done, var_done, y_c, y_done, aw_lo = (sem(k, G) for k in ("s_done", "st_done", "mv_done", "var_done", "y_c", "y_done", "aw_lo"))
        max_done, inv_done, prob_done, top_done, index_done, indexf_done, hit_done, hith_done = (
            sem(k, G) for k in ("max_done", "inv_done", "prob_done", "top_done", "index_done", "indexf_done", "hit_done", "hith_done"))
        hitn_done, pos_done, placef_done, place_done = (sem(k, G) for k in ("hitn_done", "pos_done", "placef_done", "place_done"))
        xb_done, r_done, xo_done, rstd_done, cur_done = (sem(k, G) for k in ("xb_done", "r_done", "xo_done", "rstd_done", "cur_done"))
        seen_done, row_done = sem("seen_done", G), sem("row_done", G)
        entry_done = sem("entry_done", G)

        def earlier(g, b, k):
            if b >= k:
                return g, b - k
            return None if isinstance(g, int) and g == 0 else (g - 1, b - k + G)

        def four(ap):
            return ap.rearrange("p (c t) -> p c t", c=CH)

        def pairs(q, width):
            n = min(3, HP - 3 * q)
            return n, bank[2 + q][:, 0:n * width]

        def sync_slot(sp, g, b, heavy):
            if heavy:
                prev = earlier(g, b, G)
                if prev:
                    wait(sp, v_mm, prev[0], 2 * b + 2)
                sp.dma_start(ct[:, b], cond_t[g][:, b]).then_inc(ct_in[b].sem, 16)
                if prev:
                    wait(sp, xo_done, prev[0], b + 1)
                sp.dma_start(xr[:, b, :], x[g][:, b, :]).then_inc(x_in[b].sem, 16)

        def stores(act, t):
            wait(act, xo_done, t[0], t[1] + 1)
            act.dma_start(out_rows(t), xo[:, t[1] % 2, :]).then_inc(sum_out[t[1] % 2].sem, 16)
            wait(act, y_done, t[0], t[1] + 1)
            act.dma_start(token_rows(t), y[:, t[1] % 2, :]).then_inc(tok_out[t[1] % 2].sem, 16)

        out_v = out.rearrange("(g b p) e -> g b p e", b=G, p=P)
        tok_v = tokens[0:B * P, :].rearrange("(g b p) e -> g b p e", b=G, p=P)

        def out_rows(t):
            return out_v[t[0]][t[1]]

        def token_rows(t):
            return tok_v[t[0]][t[1]]

        def k_or_v(pe, g, b, i):
            w, mm, lo = (wk, k_mm, k_lo) if i < 2 else (wv, v_mm, v_lo)
            if isinstance(g, int) and g == 0 and b == 0:
                pe.wait_ge(fold_lo.sem, 3 * CH if i < 2 else 6 * CH)
            if i == 0:
                wait(pe, ct_in[b], g, 1)
                before_b = earlier(g, b, 1)
                if before_b:
                    wait(pe, v_lo, before_b[0], 2 * before_b[1] + 1)
            elif i == 1:
                before_b = earlier(g, b, 1)
                if before_b:
                    wait(pe, v_lo, before_b[0], 2 * before_b[1] + 2)
            elif b == 0:
                wait(pe, q_lo, g, HP - 3 + i)
            else:
                wait(pe, k_lo, g, 2 * b + i - 1)
            half = slice((i % 2) * 512, (i % 2) * 512 + 512)
            three_passes(pe, bank[i % 2][:], [(lambda h, c=c: ct[:, b, c, h, :], lambda h, c=c: w[:, c, h, half])
                                              for c in range(CH)]).then_inc(mm.sem, 1)

        def q_block(pe, g, i):
            if isinstance(g, int) and g == 0 and i == 0:
                pe.wait_ge(fold_lo.sem, 5 * CH)
            for b in range(G if i == 0 else 0):
                wait(pe, ct_in[b], g, 1)
            if i < 2:
                wait(pe, k_lo, g, i + 1)
            else:
                wait(pe, q_lo, g, i - 1)
            three_passes(pe, bank[i % 2][:], [(lambda h, c=c: wq[:, c, h, i * P:i * P + P], lambda h, c=c: ct[:, :, c, h, :])
                                              for c in range(CH)]).then_inc(q_mm.sem, 1)

        def kv_products(pe, t):
            g, b = t
            wait(pe, k_lo, g, 2 * b + 2)
            wait(pe, v_lo, g, 2 * b + 2)
            before_b = earlier(g, b, 1)
            if before_b:
                wait(pe, x1_done, before_b[0], before_b[1] + 1)
                before_c = earlier(g, b, 2)
                if before_c:
                    wait(pe, s_done, before_c[0], before_c[1] + 1)
            for h in range(HP):
                out = bank[2 + h // 3][:, (h % 3) * 130:(h % 3) * 130 + 130]
                for i, (a, w) in enumerate(PASSES):
                    last = pe.matmul(out, phk[:, b % 2, a, h * P:h * P + P], v_h[:, b % 2, w, 2 * h:2 * h + 2, :],
                                     start=(i == 0), stop=(i == 2))
            last.then_inc(kv_mm.sem, 1)

        def attend(pe, t):
            g, b = t
            wait(pe, kv_lo, g, 6 * b + 6)
            wait(pe, q_lo, g, HP)
            for h in range(HP):
                out = bank[2 + h // 3][:, (h % 3) * 132:(h % 3) * 132 + 132]
                for i, (a, w) in enumerate(PASSES):
                    last = pe.matmul(out, phq[:, h, a, b * P:b * P + P], kv[:, b % 2, w, 2 * h:2 * h + 2, :],
                                     start=(i == 0), stop=(i == 2))
            last.then_inc(o_mm.sem, 1)

        def o_transposes(pe, t, c):
            g, b = t
            wait(pe, o_done, g, b + 1)
            if c:
                wait(pe, x1_lo, c[0], c[1] + 1)
                c3 = earlier(g, b, 2)
                if c3:
                    wait(pe, exp_done, c3[0], c3[1] + 1)
            for h in range(HP):
                last = pe.transpose(bank[5 + h // 4][:, (h % 4) * P:(h % 4) * P + P], o[:, b % 2, h * P:h * P + P], ident)
            last.then_inc(o_tr.sem, 1)

        def att_out(pe, t):
            g, b = t
            wait(pe, o_lo, g, 2 * b + 2)
            three_passes(pe, bank[3][:], [(lambda h, k=k: ot[:, b % 2, k, h, :], lambda h, k=k: wo[:, k, h, :])
                                          for k in range(HP)]).then_inc(att_mm.sem, 1)

        def x1_transposes(pe, t):
            g, b = t
            wait(pe, x1_done, g, b + 1)
            wait(pe, o_lo, g, 2 * b + 2)
            for c in range(CH):
                last = pe.transpose(bank[5][:, c * P:c * P + P], xr[:, b, c * P:c * P + P], ident)
            last.then_inc(x1_tr.sem, 1)

        def adapter_h(pe, t):
            g, b = t
            wait(pe, x1_lo, g, b + 1)
            wait(pe, aw_lo, g, b + 1)
            three_passes(pe, bank[7][:, 0:P], [(lambda h, c=c: aw1[:, c, h, :], lambda h, c=c: x1t[:, c, h, :])
                                               for c in range(CH)]).then_inc(h_mm.sem, 1)

        def adapter_out(pe, t):
            g, b = t
            wait(pe, h_lo, g, b + 1)
            n1 = earlier_of(t, -1)
            if n1:
                wait(pe, o_done, n1[0], n1[1] + 1)
            three_passes(pe, bank[2][:], [(lambda h: ht[:, h, :], lambda h: aw2[:, h, :])]).then_inc(ad_mm.sem, 1)

        def y_transposes(pe, t):
            g, b = t
            wait(pe, y_done, g, b + 1)
            n1 = earlier_of(t, -1)
            if n1:
                wait(pe, o_lo, n1[0], 2 * n1[1] + 2)
            for c in range(CH):
                last = pe.transpose(bank[6][:, c * P:c * P + P], y[:, b % 2, c * P:c * P + P], ident)
            last.then_inc(y_tr.sem, 1)

        def route(pe, t):
            g, b = t
            wait(pe, y_copied, g, b + 1)
            for c in range(CH):
                last = pe.matmul(bank[5][:, 0:8], yt[:, c * P:c * P + P], wr[:, c, :], start=(c == 0), stop=(c == CH - 1))
            last.then_inc(route_mm.sem, 1)

        def count(pe, t):
            g, b = t
            wait(pe, hith_done, g, b + 1)
            before_c = earlier(g, b, 1)
            if before_c:
                wait(pe, seen_done, before_c[0], before_c[1] + 1)
            pe.matmul(bank[4][:, 0:16], before[:], hit_h[:], start=True, stop=False)
            pe.matmul(bank[4][:, 0:16], ones[:], seen[:], start=False, stop=True).then_inc(count_mm.sem, 1)

        def earlier_of(t, k):
            g, b = t
            b -= k
            if b >= G:
                return (g + 1, b - G) if not (isinstance(g, int) and g + 1 >= TRIPS) else None
            return g, b

        def tensor_slot(pe, g, b, heavy):
            A, Bb, C = (earlier(g, b, k) for k in (1, 2, 3))
            A = A if alive(A) else None
            Bb = Bb if alive(Bb) else None
            if heavy:
                k_or_v(pe, g, b, 0)
            if A:
                kv_products(pe, A)
            if Bb:
                x1_transposes(pe, Bb)
            if C:
                y_transposes(pe, C)
            if heavy:
                k_or_v(pe, g, b, 1)
            if A:
                attend(pe, A)
            if Bb:
                adapter_h(pe, Bb)
            if C:
                route(pe, C)
            if heavy and b == 0:
                for i in range(HP):
                    q_block(pe, g, i)
            if heavy:
                k_or_v(pe, g, b, 2)
            if A:
                o_transposes(pe, A, Bb)
            if Bb:
                adapter_out(pe, Bb)
            if C:
                count(pe, C)
            if heavy:
                k_or_v(pe, g, b, 3)
            if A:
                att_out(pe, A)

        def alive(t):
            return t is not None and not (isinstance(t[0], int) and t[0] >= TRIPS)

        def scalar_slot(act, g, b, heavy):
            A, Bb, C = (t if alive(t) else None for t in (earlier(g, b, k) for k in (1, 2, 3)))

            def k_hi_half(i):
                wait(act, k_mm, g, 2 * b + i + 1)
                act.activation(phk[:, b % 2, 0, i * 512:i * 512 + 512], bank[i][:], ACT.Relu).then_inc(k_hi.sem, 1)

            def v_hi_half(i):
                wait(act, v_mm, g, 2 * b + i + 1)
                act.activation(v_h[:, b % 2, 0, 8 * i:8 * i + 8, 0:64], bank[i][:].rearrange("p (h d) -> p h d", d=64),
                               ACT.Copy).then_inc(v_hi.sem, 1)

            if heavy:
                k_hi_half(0)
            if Bb:
                wait(act, x1_tr, Bb[0], Bb[1] + 1)
                act.activation(x1t[:, :, 0, :], four(bank[5][:]), ACT.Copy).then_inc(x1_hi.sem, 1)
            if A:
                wait(act, kv_mm, A[0], A[1] + 1)
                for q in range(3):
                    n, src = pairs(q, 130)
                    src = src.rearrange("p (n a c) -> p n a c", n=n, a=2)
                    dst = kv[:, A[1] % 2, 0].rearrange("p (n a) c -> p n a c", a=2)[:, 3 * q:3 * q + n]
                    for a in range(2):
                        act.activation(dst[64 * a:64 * a + 64, :, a, 0:65], src[64 * a:64 * a + 64, :, a, :],
                                       ACT.Copy, scale=1.0 / 16).then_inc(kv_hi.sem, 1)
            if C:
                wait(act, y_tr, C[0], C[1] + 1)
                act.activation(yt[:], bank[6][:], ACT.Copy).then_inc(y_copied.sem, 1)
            if heavy:
                k_hi_half(1)
            if Bb:
                wait(act, h_mm, Bb[0], Bb[1] + 1)
                act.activation(hf[:], bank[7][:, 0:P], ACT.Relu, bias=b1[:, Bb[1] % 2:Bb[1] % 2 + 1],
                               scale=1.0 / WS).then_inc(h_done.sem, 1)
            if C:
                wait(act, max_done, C[0], C[1] + 1)
                act.activation(ex, bank[5][:, 0:8], ACT.Exp, bias=neg_max, accum_out=total).then_inc(exp_done.sem, 1)
            if heavy and b == 0:
                for i in range(HP):
                    wait(act, q_mm, g, i + 1)
                    act.activation(phq[:, i, 0, :], bank[i % 2][:], ACT.Relu).then_inc(q_hi.sem, 1)
                    if isinstance(g, int) and g == 0:
                        piece_hi(act, 6 + i // CH, (i % CH,))
            if heavy:
                v_hi_half(0)
            if A:
                wait(act, o_tr, A[0], A[1] + 1)
                for i in range(2):
                    act.activation(ot[:, A[1] % 2, 4 * i:4 * i + 4, 0, :], four(bank[5 + i][:]), ACT.Copy).then_inc(o_hi.sem, 1)
            if heavy:
                v_hi_half(1)
            if A:
                if Bb:
                    wait(act, ad_mm, Bb[0], Bb[1] + 1)
                wait(act, aw_in, A[0], 2 * A[1] + 2)
                act.activation(b1[:, A[1] % 2:A[1] % 2 + 1], aw_raw[:, 2 * E:2 * E + 1], ACT.Copy)
                act.activation(aw1[:, :, 0, :], aw_raw[:, 0:E].rearrange("p (c a) -> p c a", c=CH), ACT.Copy, scale=WS)
                act.activation(aw2[:, 0, :], aw_raw[:, E:2 * E], ACT.Copy, scale=WS).then_inc(aw_hi.sem, 1)
            if Bb:
                stores(act, Bb)

        def vector_slot(dve, g, b, heavy):
            A, Bb, C = (t if alive(t) else None for t in (earlier(g, b, k) for k in (1, 2, 3)))

            def k_lo_half(i):
                wait(dve, k_hi, g, 2 * b + i + 1)
                part = slice(i * 512, i * 512 + 512)
                dve.scalar_tensor_tensor(phk[:, b % 2, 1, part], bank[i][:], 0.0, phk[:, b % 2, 0, part],
                                         ALU.max, ALU.subtract).then_inc(k_lo.sem, 1)

            def v_lo_half(i):
                wait(dve, v_hi, g, 2 * b + i + 1)
                dve.tensor_tensor(v_h[:, b % 2, 1, 8 * i:8 * i + 8, 0:64], bank[i][:].rearrange("p (h d) -> p h d", d=64),
                                  v_h[:, b % 2, 0, 8 * i:8 * i + 8, 0:64], ALU.subtract).then_inc(v_lo.sem, 1)

            def link(sig, t):
                wait(dve, sig, t[0], t[1] + 1)

            def take_wait():
                dve.memset(scratch, 0.0)

            if heavy:
                k_lo_half(0)
            if Bb:
                link(x1_hi, Bb)
                dve.tensor_tensor(x1t[:, :, 1, :], four(bank[5][:]), x1t[:, :, 0, :], ALU.subtract).then_inc(x1_lo.sem, 1)
            if A:
                for q in range(3):
                    n, src = pairs(q, 130)
                    src = src.rearrange("p (n a c) -> p n a c", n=n, a=2)
                    halves = [kv[:, A[1] % 2, h].rearrange("p (n a) c -> p n a c", a=2)[:, 3 * q:3 * q + n] for h in range(2)]
                    for a in range(2):
                        rows = slice(64 * a, 64 * a + 64)
                        wait(dve, kv_hi, A[0], 6 * A[1] + 2 * q + a + 1)
                        dve.scalar_tensor_tensor(halves[1][rows, :, a, 0:65], src[rows, :, a, :], 1.0 / 16,
                                                 halves[0][rows, :, a, 0:65], ALU.mult, ALU.subtract).then_inc(kv_lo.sem, 1)
            if heavy:
                k_lo_half(1)
            if A:
                ab = A[1] % 2
                link(o_mm, A)
                for q in range(3):
                    n, src = pairs(q, 132)
                    last = dve.tensor_scalar(nrm[:, ab, 6 * q:6 * q + 2 * n], src.rearrange("p (h c) -> p h c", c=66)[:, :, 64],
                                             16e-6, None, ALU.add)
                last.then_inc(nrm_add.sem, 1)
                link(nrm_add, A)
                dve.reciprocal(nrm[:, ab, :], nrm[:, ab, :]).then_inc(nrm_inv.sem, 1)
                link(nrm_inv, A)
                for q in range(3):
                    n, src = pairs(q, 132)
                    last = dve.tensor_tensor(o[:, ab, 6 * q * 64:(6 * q + 2 * n) * 64].rearrange("p (h c) -> p h c", c=64),
                                             src.rearrange("p (h c) -> p h c", c=66)[:, :, 0:64],
                                             repeated(nrm[:, ab, 6 * q:6 * q + 2 * n], 2, 64), ALU.mult)
                last.then_inc(o_done.sem, 1)
            if C:
                link(route_mm, C)
                dve.tensor_reduce(neg_max, bank[5][:, 0:8], AX_X, ALU.max, negate=True).then_inc(max_done.sem, 1)
            if Bb:
                link(h_done, Bb)
                dve.tensor_copy(ht[:, 0, :], hf[:]).then_inc(h_hi.sem, 1)
                link(h_hi, Bb)
                dve.tensor_tensor(ht[:, 1, :], hf[:], ht[:, 0, :], ALU.subtract).then_inc(h_lo.sem, 1)
            if C:
                cb = C[1] % 2
                link(exp_done, C)
                dve.reciprocal(inv, total).then_inc(inv_done.sem, 1)
                link(inv_done, C)
                dve.tensor_scalar(ex, ex, inv, None, ALU.mult).then_inc(prob_done.sem, 1)
                link(prob_done, C)
                take_wait()
                dve.max(top, ex).then_inc(top_done.sem, 1)
                link(top_done, C)
                take_wait()
                dve.max_index(index_u[:], top, ex).then_inc(index_done.sem, 1)
                before_c, last_entry = earlier(*C, 1), earlier(*C, 2)
                if before_c:
                    link(cur_done, before_c)
                if last_entry:
                    wait(dve, slot_out[cb], last_entry[0], 2 * (last_entry[1] // 2) + 2)
                dve.tensor_copy(entry[:, cb, :, 0], cur_token.broadcast_to([P, 2]))
                dve.tensor_scalar(entry[:, cb, :, 1].bitcast(F32), top[:, 0:2], 1.0 / WS, None,
                                  ALU.mult).then_inc(entry_done.sem, 1)
                link(index_done, C)
                dve.tensor_copy(index_f, index_u[:, 0:2]).then_inc(indexf_done.sem, 1)
                link(indexf_done, C)
                dve.tensor_scalar(cur_token, cur_token, float(P), None, ALU.add).then_inc(cur_done.sem, 1)
                dve.tensor_tensor(hit.rearrange("p (k e) -> p k e", k=2), expert.rearrange("p (k e) -> p k e", k=2),
                                  repeated(index_f, 2, 8), ALU.is_equal).then_inc(hit_done.sem, 1)
                link(hit_done, C)
                dve.tensor_copy(hit_h[:], hit).then_inc(hith_done.sem, 1)
            if heavy and b == 0:
                for i in range(HP):
                    wait(dve, q_hi, g, i + 1)
                    dve.scalar_tensor_tensor(phq[:, i, 1, :], bank[i % 2][:], 0.0, phq[:, i, 0, :],
                                             ALU.max, ALU.subtract).then_inc(q_lo.sem, 1)
                    if isinstance(g, int) and g == 0:
                        piece_lo(dve, 6 + i // CH, (i % CH,))
            if heavy:
                v_lo_half(0)
            if A:
                for i in range(2):
                    wait(dve, o_hi, A[0], 2 * A[1] + i + 1)
                    dve.tensor_tensor(ot[:, A[1] % 2, 4 * i:4 * i + 4, 1, :], four(bank[5 + i][:]),
                                      ot[:, A[1] % 2, 4 * i:4 * i + 4, 0, :], ALU.subtract).then_inc(o_lo.sem, 1)
            if Bb:
                bb = Bb[1] % 2
                link(r_done, Bb)
                link(ad_mm, Bb)
                dve.scalar_tensor_tensor(r[:, bb, :], bank[2][:], 1.0 / WS, r[:, bb, :], ALU.mult, ALU.add).then_inc(s_done.sem, 1)
                link(s_done, Bb)
                dve.bn_stats(stats[:], r[:, bb, :]).then_inc(st_done.sem, 1)
                link(st_done, Bb)
                take_wait()
                dve.bn_aggr(mv[:], stats[:]).then_inc(mv_done.sem, 1)
                link(mv_done, Bb)
                dve.tensor_scalar(var_e[:], mv[:, 1:2], 1e-5, None, ALU.add).then_inc(var_done.sem, 1)
                dve.wait_ge(arow_in[bb].sem, arow_in[bb].after(Bb[0], Bb[1] // 2 + 1))
                prev = earlier(*Bb, 2)
                if prev:
                    wait(dve, tok_out[bb], prev[0], prev[1] // 2 + 1)
                dve.scalar_tensor_tensor(y[:, bb, :], r[:, bb, :], mv[:, 0:1], arow[:, bb, E:2 * E],
                                         ALU.subtract, ALU.mult).then_inc(y_c.sem, 1)
                link(rstd_done, Bb)
                link(y_c, Bb)
                dve.scalar_tensor_tensor(y[:, bb, :], y[:, bb, :], rstd[:, 0:1], arow[:, bb, 2 * E:3 * E],
                                         ALU.mult, ALU.add).then_inc(y_done.sem, 1)
            if C:
                link(count_mm, C)
                dve.tensor_tensor(hit_n, bank[4][:, 0:16], hit, ALU.mult).then_inc(hitn_done.sem, 1)
                link(hitn_done, C)
                dve.tensor_reduce(pos, hit_n.rearrange("p (k e) -> p k e", k=2), AX_X, ALU.add).then_inc(pos_done.sem, 1)
                if before_c:
                    link(seen_done, before_c)
                dve.tensor_tensor(seen[:], seen[:], hit_h[:], ALU.add).then_inc(seen_done.sem, 1)
                link(pos_done, C)
                dve.scalar_tensor_tensor(place_f, pos, 16.0, index_f, ALU.mult, ALU.add).then_inc(placef_done.sem, 1)
                link(placef_done, C)
                dve.tensor_tensor(place_u[:, C[1] % 2, :], place_f, choice, ALU.add).then_inc(place_done.sem, 1)
            if heavy:
                v_lo_half(1)
            if A:
                link(aw_hi, A)
                dve.scalar_tensor_tensor(aw1[:, :, 1, :], aw_raw[:, 0:E].rearrange("p (c a) -> p c a", c=CH), WS,
                                         aw1[:, :, 0, :], ALU.mult, ALU.subtract)
                dve.scalar_tensor_tensor(aw2[:, 1, :], aw_raw[:, E:2 * E], WS, aw2[:, 0, :],
                                         ALU.mult, ALU.subtract).then_inc(aw_lo.sem, 1)
                link(xb_done, A)
                link(att_mm, A)
                dve.scalar_tensor_tensor(xr[:, A[1], :], bank[3][:], 1.0 / (QS * 16), xr[:, A[1], :],
                                         ALU.mult, ALU.add).then_inc(x1_done.sem, 1)

        def pool_slot(pool, g, b, heavy):
            A, Bb, C = (t if alive(t) else None for t in (earlier(g, b, k) for k in (1, 2, 3)))

            def take_wait(t):
                if isinstance(t[0], int):
                    return
                pool.tensor_tensor(pool_dummy[:, 0:1], pool_dummy[:, 1:2], pool_dummy[:, 1:2], ALU.add)

            if A:
                n = A[0] * G + A[1]
                before_a = earlier(A[0], A[1], 1)
                if before_a:
                    wait(pool, aw_lo, before_a[0], before_a[1] + 1)
                    wait(pool, aw_in, before_a[0], 2 * before_a[1] + 2)
                    wait(pool, arow_in[before_a[1] % 2], before_a[0], before_a[1] // 2 + 1)
                pool.tensor_tensor(row_now[:, 0:1], lang_rows[:, bass.ds(n, 1)], zero_i[:], ALU.add)
                pool.tensor_tensor(row_now[:, 1:2], lang_i[:, bass.ds(n, 1)], zero_i[:], ALU.add).then_inc(row_done.sem, 1)
                wait(pool, row_done, A[0], A[1] + 1)
                take_wait(A)
                rows = row_now[:, 0:1]
                pool.indirect_dma_start(out=aw_raw[:, 0:E], out_offset=None, in_=A1,
                                        in_offset=bass.IndirectOffsetOnAxis(rows, 0)).then_inc(aw_in.sem, 16)
                pool.indirect_dma_start(out=aw_raw[:, E:2 * E + 1], out_offset=None, in_=A2,
                                        in_offset=bass.IndirectOffsetOnAxis(rows, 0)).then_inc(aw_in.sem, 16)
                pool.indirect_dma_start(out=arow[:, A[1] % 2, :], out_offset=None, in_=rows3,
                                        in_offset=bass.IndirectOffsetOnAxis(row_now[:, 1:2], 0)).then_inc(arow_in[A[1] % 2].sem, 16)
            if Bb:
                bb = Bb[1] % 2
                wait(pool, arow_in[bb], Bb[0], Bb[1] // 2 + 1)
                wait(pool, x1_done, Bb[0], Bb[1] + 1)
                pool.tensor_tensor(r[:, bb, :], xr[:, Bb[1], :], arow[:, bb, 0:E], ALU.add).then_inc(r_done.sem, 1)
                prev = earlier(*Bb, 2)
                if prev:
                    wait(pool, sum_out[bb], prev[0], prev[1] // 2 + 1)
                wait(pool, x1_tr, Bb[0], Bb[1] + 1)
                pool.tensor_tensor(xo[:, bb, :], xr[:, Bb[1], :], bias_rows[:], ALU.add).then_inc(xo_done.sem, 1)
            if heavy:
                if isinstance(g, int) and g == 0 and b == 0:
                    pool.wait_ge(in_b.sem, 16 * len(loads_b))
                wait(pool, x_in[b], g, 1)
                pool.tensor_tensor(xr[:, b, :], xr[:, b, :], b_out_rows[:], ALU.add).then_inc(xb_done.sem, 1)
            if Bb:
                wait(pool, var_done, Bb[0], Bb[1] + 1)
                pool.tensor_tensor(rstd[:], var_e[:], half_pow[:], ALU.pow).then_inc(rstd_done.sem, 1)
            if C:
                wait(pool, place_done, C[0], C[1] + 1)
                take_wait(C)
                for k in range(2):
                    pool.indirect_dma_start(out=slots, out_offset=bass.IndirectOffsetOnAxis(place_u[:, C[1] % 2, k:k + 1], 0),
                                            in_=entry[:, C[1] % 2, k, :], in_offset=None, bounds_check=8 * 2 * 512 - 1,
                                            oob_is_err=False).then_inc(slot_out[C[1] % 2].sem, 16)

        def run(eng, slot):
            slot(eng, 0, 0, True)
            if slot is sync_slot:
                for b in range(1, G):
                    slot(eng, 0, b, True)
                setup_sync_later(eng)
            else:
                all_set(eng)
                for b in range(1, G):
                    slot(eng, 0, b, True)
            with eng.Fori(1, TRIPS) as g:
                for b in range(G):
                    slot(eng, g, b, True)
            for b in range(3):
                slot(eng, TRIPS, b, False)

        with nc.Block() as block:
            @block.sync
            def _(sp):
                setup_sync(sp)
                run(sp, sync_slot)

            @block.tensor
            def _(pe):
                fold(pe)
                run(pe, tensor_slot)

            @block.scalar
            def _(act):
                setup_scalar(act)
                run(act, scalar_slot)

            @block.vector
            def _(dve):
                setup_vector(dve)
                run(dve, vector_slot)

            @block.gpsimd
            def _(pool):
                setup_pool(pool)
                run(pool, pool_slot)
                for stored in (*sum_out, *tok_out, *slot_out):
                    wait(pool, stored, TRIPS)


def expert_phase(nc, table, tokens, slots, weights, out):
    EXPERTS, FC, Q = 8, 16, 4
    _, AT = constant_tables()
    PASSES_ALL = 2 * EXPERTS
    with ExitStack() as ctx, Semaphores(nc) as semaphores:
        def sb(name, shape, dt=F32):
            return ctx.enter_context(nc.sbuf_tensor("e_" + name, shape, dt))

        def sem(name, per=1, step=1):
            return Signal(semaphores.new("e_" + name), per, step)

        bank = [ctx.enter_context(nc.psum_tensor(f"e_bank{i}", [P, 512], F32)) for i in range(8)]
        ident = sb("ident", [P, P])
        slot_sb = sb("slot_sb", [P, Q, 2, EXPERTS, 2], I32)
        stage = sb("stage", [P, 4, 2 * E])
        w1 = sb("w1", [P, FC, CH, 2, P], F16)
        w2 = sb("w2", [P, FC, 2, E], F16)
        take = sb("take", [P, 2, Q], I32)
        give = sb("give", [P, 2, Q], I32)
        share = sb("share", [P, 2, Q], I32)
        xg = sb("xg", [P, Q, E])
        xt = sb("xt", [P, 2, CH, 2, E], F16)
        hf = sb("hf", [P, 2, E])
        hh = sb("hh", [P, 4, 2, E], F16)
        ys = sb("ys", [P, Q, E])
        dummy = sb("dummy", [P, 16])

        ident_in, slots_in, d0 = sem("ident_in"), sem("slots_in"), sem("d0")
        stage_in = [sem(f"stage_in{i}", FC // 4, 16) for i in range(4)]
        w_hi, w_lo = sem("w_hi", FC), sem("w_lo", FC)
        take_done, give_done = sem("take_done"), sem("give_done")
        x_in, y_out = [sem(f"x_in{q}", 1, 16) for q in range(Q)], sem("y_out", Q, 16)
        x_tr, h_mm, y_mm = sem("x_tr", Q), sem("h_mm", FC), sem("y_mm", FC)
        x_hi, gelu_done = sem("x_hi", Q), sem("gelu_done", FC)
        x_lo, h_hi, h_lo = sem("x_lo", Q), sem("h_hi", FC), sem("h_lo", FC)
        y_done = sem("y_done", Q)

        def back(p, f, n):
            if f >= n:
                return p, f - n
            return None if isinstance(p, int) and p == 0 else (p - 1, f - n + FC)

        def run(eng, one):
            one(eng, 0, 0, 0)
            with eng.Fori(1, EXPERTS) as t:
                one(eng, 2 * t - 1, t - 1, 1)
                one(eng, 2 * t, t, 0)
            one(eng, PASSES_ALL - 1, EXPERTS - 1, 1)

        def is_last(p):
            return isinstance(p, int) and p == PASSES_ALL - 1

        def following(p, e, k):
            return (p + 1, e, 1) if k == 0 else (p + 1, e + 1, 0)

        def load_expert(sp, e):
            for c in range(FC):
                if c >= 4:
                    wait(sp, w_lo, e, c - 3)
                elif not (isinstance(e, int) and e == 0):
                    wait(sp, w_lo, e - 1, FC + c - 3)
                sp.dma_start(stage[:, c % 4, :], weights[e][c]).then_inc(stage_in[c % 4].sem, 16)

        def chunk_at(p, e, k, f):
            if isinstance(p, int) and p == 0:
                return (e, f + 2) if f + 2 < FC else None
            if k == 1:
                return (e + 1, f - 4) if f >= 4 and not is_last(p) else None
            return (e, FC - 4 + f) if f < 4 else None

        def split_hi(act, e, c, readers):
            wait(act, stage_in[c % 4], e, c // 4 + 1)
            if readers:
                wait(act, y_mm, *readers)
            act.activation(w1[:, c, :, 0, :], stage[:, c % 4, 0:E].rearrange("p (c t) -> p c t", c=CH), ACT.Copy, scale=WS)
            act.activation(w2[:, c, 0, :], stage[:, c % 4, E:2 * E], ACT.Copy, scale=WS).then_inc(w_hi.sem, 1)

        def split_lo(dve, e, c):
            wait(dve, w_hi, e, c + 1)
            dve.scalar_tensor_tensor(w1[:, c, :, 1, :], stage[:, c % 4, 0:E].rearrange("p (c t) -> p c t", c=CH), WS,
                                     w1[:, c, :, 0, :], ALU.mult, ALU.subtract)
            dve.scalar_tensor_tensor(w2[:, c, 1, :], stage[:, c % 4, E:2 * E], WS, w2[:, c, 0, :],
                                     ALU.mult, ALU.subtract).then_inc(w_lo.sem, 1)

        def x_transposes(pe, p, k, q):
            wait(pe, x_in[q], p, 1)
            if q >= 2:
                wait(pe, x_lo, p, q - 1)
            elif not (isinstance(p, int) and p == 0):
                wait(pe, x_lo, p - 1, Q - 1 + q)
            for c in range(CH):
                last = pe.transpose(bank[2 + q % 2][:, c * P:c * P + P], xg[:, q, c * P:c * P + P], ident[:])
            last.then_inc(x_tr.sem, 1)

        def y_block(pe, p, f):
            if f == 0 and not (isinstance(p, int) and p == 0):
                wait(pe, y_done, p - 1, Q)
            wait(pe, h_lo, p, f + 1)
            for q in range(Q):
                for i, (a, w) in enumerate(PASSES):
                    last = pe.matmul(bank[4 + q][:], hh[:, f % 4, a, q * P:q * P + P], w2[:, f, w, :],
                                     start=(f == 0 and i == 0), stop=(f == FC - 1 and i == 2))
            last.then_inc(y_mm.sem, 1)

        def tensor_pass(pe, p, e, k):
            for f in range(FC):
                if f == 0:
                    wait(pe, x_lo, p, Q)
                if k == 0:
                    wait(pe, w_lo, e, f + 1)
                two = back(p, f, 2)
                if two:
                    wait(pe, gelu_done, two[0], two[1] + 1)
                three_passes(pe, bank[f % 2][:], [(lambda h, c=c: w1[:, f, c, h, :], lambda h, c=c: xt[:, k, c, h, :])
                                                  for c in range(CH)]).then_inc(h_mm.sem, 1)
                if two:
                    y_block(pe, *two)
                if 8 <= f < 8 + Q and not is_last(p):
                    x_transposes(pe, p + 1, 1 - k, f - 8)

        def x_hi_half(act, p, k, q):
            wait(act, x_tr, p, q + 1)
            act.activation(xt[:, k, :, 0, q * P:q * P + P], bank[2 + q % 2][:].rearrange("p (c t) -> p c t", c=CH),
                           ACT.Copy).then_inc(x_hi.sem, 1)

        def x_lo_half(dve, p, k, q):
            wait(dve, x_hi, p, q + 1)
            dve.tensor_tensor(xt[:, k, :, 1, q * P:q * P + P], bank[2 + q % 2][:].rearrange("p (c t) -> p c t", c=CH),
                              xt[:, k, :, 0, q * P:q * P + P], ALU.subtract).then_inc(x_lo.sem, 1)

        def scalar_pass(act, p, e, k):
            for f in range(FC):
                wait(act, h_mm, p, f + 1)
                two = back(p, f, 2)
                if two:
                    wait(act, h_lo, two[0], two[1] + 1)
                act.activation(hf[:, f % 2, :], bank[f % 2][:], ACT.Gelu_apprx_tanh, scale=1.0 / WS).then_inc(gelu_done.sem, 1)
                job = chunk_at(p, e, k, f)
                if job:
                    c = job[1]
                    split_hi(act, *job, None if isinstance(p, int) and p == 0 else
                             ((p, c + 1) if k == 1 else (p - 1, c + 1)))
                if 8 <= f < 8 + Q and not is_last(p):
                    x_hi_half(act, p + 1, 1 - k, f - 8)

        def y_evacuate(dve, p, k):
            wait(dve, y_mm, p, FC)
            wait(dve, give_done, p, 1)
            if not (isinstance(p, int) and p == 0):
                wait(dve, y_out, p - 1, Q)
            for q in range(Q):
                dve.tensor_scalar(ys[:, q, :], bank[4 + q][:], share[:, k, q:q + 1].bitcast(F32), None,
                                  ALU.mult).then_inc(y_done.sem, 1)

        def vector_pass(dve, p, e, k):
            for f in range(FC):
                wait(dve, gelu_done, p, f + 1)
                four = back(p, f, 4)
                if four:
                    wait(dve, y_mm, four[0], four[1] + 1)
                dve.tensor_copy(hh[:, f % 4, 0, :], hf[:, f % 2, :]).then_inc(h_hi.sem, 1)
                wait(dve, h_hi, p, f + 1)
                dve.tensor_tensor(hh[:, f % 4, 1, :], hf[:, f % 2, :], hh[:, f % 4, 0, :], ALU.subtract).then_inc(h_lo.sem, 1)
                if f == 1 and not (isinstance(p, int) and p == 0):
                    y_evacuate(dve, p - 1, 1 - k)
                job = chunk_at(p, e, k, f)
                if job:
                    split_lo(dve, *job)
                if 8 <= f < 8 + Q and not is_last(p):
                    x_lo_half(dve, p + 1, 1 - k, f - 8)

        def take_wait(pool, p, n):
            if not isinstance(p, int):
                pool.tensor_tensor(dummy[:, n:n + 1], dummy[:, 15:16], dummy[:, 15:16], ALU.add)

        def column(e, k, which):
            return slot_sb[:, :, k, bass.ds(e, 1), which]

        def gathers(pool, p, e, k):
            if not (isinstance(p, int) and p == 0):
                wait(pool, x_tr, p - 1, Q)
            pool.tensor_copy(take[:, k, :], column(e, k, 0)).then_inc(take_done.sem, 1)
            wait(pool, take_done, p, 1)
            take_wait(pool, p, k)
            for q in range(Q):
                pool.indirect_dma_start(out=xg[:, q, :], out_offset=None, in_=tokens,
                                        in_offset=bass.IndirectOffsetOnAxis(take[:, k, q:q + 1], 0)).then_inc(x_in[q].sem, 16)

        def additions(pool, p, e, k):
            if not (isinstance(p, int) and p == 0):
                wait(pool, y_out, p - 1, Q)
                take_wait(pool, p, 12 + k)
            for q in range(Q):
                wait(pool, y_done, p, q + 1)
                take_wait(pool, p, 2 + Q * k + q)
                pool.indirect_dma_start(out=out, out_offset=bass.IndirectOffsetOnAxis(give[:, k, q:q + 1], 0),
                                        in_=ys[:, q, :], in_offset=None, bounds_check=B * P - 1, oob_is_err=False,
                                        compute_op=ALU.add).then_inc(y_out.sem, 16)

        def pool_pass(pool, p, e, k):
            if not is_last(p):
                gathers(pool, *following(p, e, k))
            if not (isinstance(p, int) and p == 0):
                additions(pool, p - 1, e if k == 1 else e - 1, 1 - k)
            pool.tensor_copy(give[:, k, :], column(e, k, 0))
            pool.tensor_copy(share[:, k, :], column(e, k, 1)).then_inc(give_done.sem, 1)

        with nc.Block() as block:
            @block.sync
            def _(sp):
                sp.dma_start(ident[:], table[:, AT["ident"][0]:AT["ident"][1]]).then_inc(ident_in.sem, 16)
                load_expert(sp, 0)
                with sp.Fori(1, EXPERTS) as e:
                    load_expert(sp, e)

            @block.tensor
            def _(pe):
                pe.wait_ge(ident_in.sem, 16)
                for q in range(Q):
                    x_transposes(pe, 0, 0, q)
                run(pe, tensor_pass)
                y_block(pe, PASSES_ALL - 1, FC - 2)
                y_block(pe, PASSES_ALL - 1, FC - 1)

            @block.scalar
            def _(act):
                split_hi(act, 0, 0, None)
                split_hi(act, 0, 1, None)
                for q in range(Q):
                    x_hi_half(act, 0, 0, q)
                run(act, scalar_pass)

            @block.vector
            def _(dve):
                split_lo(dve, 0, 0)
                split_lo(dve, 0, 1)
                for q in range(Q):
                    x_lo_half(dve, 0, 0, q)
                run(dve, vector_pass)
                y_evacuate(dve, PASSES_ALL - 1, 1)

            @block.gpsimd
            def _(pool):
                pool.dma_start(slot_sb[:], slots.rearrange("(p q k e) w -> p q k e w", q=Q, k=2, e=EXPERTS)).then_inc(slots_in.sem, 16)
                pool.memset(dummy[:], 0.0).then_inc(d0.sem, 1)
                pool.wait_ge(d0.sem, 1)
                pool.wait_ge(slots_in.sem, 16)
                gathers(pool, 0, 0, 0)
                run(pool, pool_pass)
                additions(pool, PASSES_ALL - 1, EXPERTS - 1, 1)
                wait(pool, y_out, PASSES_ALL)


def layer(nc, a, out):
    cond_t = nc.dram_tensor("cond_t", (TRIPS, P, G, CH, 2, P), F16, kind="Internal").ap()
    tokens = nc.dram_tensor("tokens", ((B + 1) * P, E), F32, kind="Internal").ap()
    slots = nc.dram_tensor("slots", (8 * 2 * 512, 2), I32, kind="Internal").ap()
    cond_phase(nc, a["table"], a["x"], a["x_t"], a["tau_ctx"], a["tau"], a["Wg"], a["bg"], a["Wn1"], a["bn1"],
               a["Wn2"], a["bn2"], a["blend_t"], a["Wsoma"], a["bsoma"], a["Wtemp"], a["btemp"], a["Wout"],
               a["gamma"], a["beta"], cond_t)
    attention_phase(nc, a["table"], cond_t, a["x"], a["WqT"], a["WkT"], a["RF"], a["Wv"], a["Wo"], a["b_out"],
                    a["ffn_bias"], a["lang"], a["A1"], a["A2"], a["rows3"], a["router"], out, tokens, slots)
    expert_phase(nc, a["table"], tokens, slots, a["experts"], out)


def layouts(i):
    x = i["x"]

    def by_chunk(w):
        return np.ascontiguousarray(w.reshape(-1, P, w.shape[1]).transpose(1, 0, 2))

    def by_pair(w):
        return np.ascontiguousarray(w.T.reshape(8, P, E).transpose(1, 0, 2))

    W, rf = i["L0_attn_W_qkv"], i["L0_attn_RF"]
    HD = W.shape[1] // 3
    langs = i["L0_cond2_W1"].shape[0]
    w1, w2 = i["L0_ffn_w1"], i["L0_ffn_w2"]
    n_e, _, F = w1.shape
    w1 = w1.reshape(n_e, CH, P, F // P, P).transpose(0, 3, 2, 1, 4).reshape(n_e, F // P, P, E)
    w2 = w2.reshape(n_e, F // P, P, E)
    lay = {
        "table": constant_tables()[0],
        "x": x.reshape(TRIPS, G, P, E).transpose(0, 2, 1, 3),
        "x_t": x.reshape(TRIPS, G, P, CH, P).transpose(0, 4, 3, 1, 2).reshape(TRIPS, P, CH, GT),
        "tau_ctx": i["L0_cond_tau_ctx"].reshape(1), "tau": i["condB_tauraws"],
        "Wg": by_chunk(i["L0_cond_Wg"].T), "bg": i["L0_cond_bg"],
        "Wn1": by_chunk(i["L0_cond_Wn1"].T), "bn1": i["L0_cond_bn1"],
        "Wn2": i["cond_256"].T, "bn2": i["condB_bn2"],
        "blend_t": i["cond_1024"].reshape(D, CH, P).transpose(2, 1, 0).reshape(P, CH * D),
        "Wsoma": by_chunk(i["L0_cond_Wsoma"].T), "bsoma": i["L0_cond_bsoma"].reshape(CH, P).T,
        "Wtemp": by_chunk(i["L0_cond_Wtemp"].T), "btemp": i["L0_cond_btemp"].reshape(CH, P).T,
        "Wout": by_chunk(i["L0_cond_Wout"].T), "gamma": i["L0_cond_gamma"], "beta": i["L0_cond_beta"],
        "WqT": by_pair(W[:, 0:HD]), "WkT": by_pair(W[:, HD:2 * HD]),
        "RF": np.concatenate([rf[0::2], rf[1::2]]).transpose(1, 0, 2),
        "Wv": by_chunk(W[:, 2 * HD:]), "Wo": by_chunk(i["L0_attn_W_out"]), "b_out": i["L0_attn_b_out"],
        "ffn_bias": i["L0_ffn_bias"].reshape(E), "lang": i["itok_B_0_8"],
        "A1": i["L0_cond2_W1"].reshape(langs, CH, P, P).transpose(0, 2, 1, 3).reshape(langs * P, E),
        "A2": np.concatenate([i["L0_cond2_W2"], i["L0_cond2_b1"][:, :, None]], 2).reshape(langs * P, E + 1),
        "rows3": np.concatenate([i["L0_cond2_b2"], i["L0_cond2_gamma"], i["L0_cond2_beta"]], 1),
        "router": by_chunk(i["L0_ffn_router_w"]),
        "experts": np.concatenate([w1, w2], 3),
    }
    return {k: np.ascontiguousarray(v) for k, v in lay.items()}


def kernel(**inputs):
    import concourse.bacc as _bacc
    from concourse.bass_utils import run_bass_kernel_spmd as _run

    nc = _bacc.Bacc("TRN2", target_bir_lowering=False, num_devices=1)
    lay = layouts({k: np.asarray(v) for k, v in inputs.items()})
    args = {n: nc.dram_tensor(f"in_{n}_dram", a.shape, mybir.dt.from_np(a.dtype), kind="ExternalInput").ap()
            for n, a in lay.items()}
    out = nc.dram_tensor("out_0_dram", (B * P, E), F32, kind="ExternalOutput").ap()
    layer(nc, args, out)
    r = _run(nc, [{f"in_{n}_dram": a for n, a in lay.items()}], core_ids=[0])
    return r.results[0]["out_0_dram"].reshape(B, P, E)
```
